# Optimizing a Trainium2 kernel written in Bass

```python
import numpy as np
import jax
import jax.numpy as jnp

def _softmax(x, axis=-1):
    return jax.nn.softmax(x, axis=axis)

def _gelu(x):
    return jax.nn.gelu(x, approximate=True)

def _silu(x):
    return jax.nn.silu(x)

def _sigmoid(x):
    return jax.nn.sigmoid(x)

def _layernorm(x, axis=-1, eps=1e-05):
    m = jnp.mean(x, axis=axis, keepdims=True)
    v = jnp.var(x, axis=axis, keepdims=True)
    return (x - m) / jnp.sqrt(v + eps)

def _scatter_add(tgt, idx, src, axis=0):
    return tgt.at[idx].add(src)

def _segment_sum(src, seg, n):
    return jax.ops.segment_sum(src, seg, n)
kernel_name = 'mk_adj_ffn_d1_adj_r2_dfedf1'

def setup_inputs(seed: int=0):
    np.random.seed(seed)
    _w = jnp.asarray

    def _rec_inputs():
        import jax
        import jax.numpy as jnp
        _gk = jax.random.key(seed)
        x = -0.0005207 + 1.001 * jax.random.normal(jax.random.fold_in(_gk, 1), (16, 512, 128), jnp.float32)
        _w = (1.0 + jnp.arange(512, dtype=jnp.float32)) ** (-0.5)
        _w = _w / _w.mean()
        _pij = jnp.clip(0.0078125 * _w[:, None] * _w[None, :], 0.0, 1.0)
        _a = jax.random.uniform(jax.random.fold_in(_gk, 2), (16, 512, 512)) < _pij
        _a = jnp.logical_or(_a, jnp.eye(512, dtype=bool))
        adj = _a.astype(jnp.int32)
        return (x, adj)
    x, adj = _rec_inputs()

    def _L0_gnn_setup():
        import jax, jax.numpy as jnp
        import numpy as np
        BS, N, D, R = (16, 256, 128, 2)
        key = jax.random.key(seed)
        ks = jax.random.split(key, 9)
        s = 1.0 / np.sqrt(D)
        return {'encoded_spans': jax.random.normal(ks[0], (BS, N, D), dtype=jnp.float32), 'w_rel1': jax.random.normal(ks[1], (R, D, D), dtype=jnp.float32) * s, 'w_root1': jax.random.normal(ks[2], (D, D), dtype=jnp.float32) * s, 'b1': jnp.zeros((D,), dtype=jnp.float32), 'w_rel2': jax.random.normal(ks[3], (R, D, D), dtype=jnp.float32) * s, 'w_root2': jax.random.normal(ks[4], (D, D), dtype=jnp.float32) * s, 'b2': jnp.zeros((D,), dtype=jnp.float32), 'aug_adj': jax.random.randint(ks[5], (BS, N, N), 0, 16, dtype=jnp.int64), 'punct_graph': jax.random.randint(ks[6], (BS, N, N), 0, 16, dtype=jnp.int64)}
    _L0_gnn_all = _L0_gnn_setup()
    _L0_gnn_in = {k: v for k, v in _L0_gnn_all.items() if k in ('w_rel1', 'w_root1', 'b1', 'w_rel2', 'w_root2', 'b2')}
    del _L0_gnn_all

    def _L0_ffn_setup():
        import jax, jax.numpy as jnp
        import numpy as np
        B, S, D_MODEL, FFN, P = (8, 2048, 128, 512, 8)
        BLK = 128
        key = jax.random.key(seed)
        ks = jax.random.split(key, 12)
        x = jax.random.normal(ks[0], (B, S, D_MODEL), jnp.float32)
        Wt = 0.05 * jax.random.normal(ks[1], (FFN, D_MODEL), jnp.float32)
        bt = 0.05 * jax.random.normal(ks[2], (FFN,), jnp.float32)
        sl_cvx = 1.0 + 0.1 * jax.random.normal(ks[3], (FFN, P), jnp.float32)
        of_cvx = 0.1 * jax.random.normal(ks[4], (FFN, P), jnp.float32)
        sl_ccv = 1.0 + 0.1 * jax.random.normal(ks[5], (FFN, P), jnp.float32)
        of_ccv = 0.1 * jax.random.normal(ks[6], (FFN, P), jnp.float32)
        alpha = jnp.zeros((FFN,), jnp.float32)
        Wc = jax.random.normal(ks[7], (D_MODEL, FFN), jnp.float32) / np.sqrt(D_MODEL)
        bc = jnp.zeros((FFN,), jnp.float32)
        Wg = 0.01 * jax.random.normal(ks[8], (D_MODEL, FFN), jnp.float32)
        bg = 2.0 * jnp.ones((FFN,), jnp.float32)
        Wd = jax.random.normal(ks[9], (FFN, D_MODEL), jnp.float32) / np.sqrt(FFN)
        bd = jnp.zeros((D_MODEL,), jnp.float32)
        return {'x': x, 'Wt': Wt, 'bt': bt, 'sl_cvx': sl_cvx, 'of_cvx': of_cvx, 'sl_ccv': sl_ccv, 'of_ccv': of_ccv, 'alpha': alpha, 'Wc': Wc, 'bc': bc, 'Wg': Wg, 'bg': bg, 'Wd': Wd, 'bd': bd}
    _L0_ffn_all = _L0_ffn_setup()
    _L0_ffn_in = {k: v for k, v in _L0_ffn_all.items() if k in ('Wt', 'bt', 'sl_cvx', 'of_cvx', 'sl_ccv', 'of_ccv', 'alpha', 'Wc', 'bc', 'Wg', 'bg', 'Wd', 'bd')}
    del _L0_ffn_all
    return {'x': x, 'adj': adj, 'L0_gnn_w_rel1': _L0_gnn_in['w_rel1'], 'L0_gnn_w_root1': _L0_gnn_in['w_root1'], 'L0_gnn_b1': _L0_gnn_in['b1'], 'L0_gnn_w_rel2': _L0_gnn_in['w_rel2'], 'L0_gnn_w_root2': _L0_gnn_in['w_root2'], 'L0_gnn_b2': _L0_gnn_in['b2'], 'L0_ffn_Wt': _L0_ffn_in['Wt'], 'L0_ffn_bt': _L0_ffn_in['bt'], 'L0_ffn_sl_cvx': _L0_ffn_in['sl_cvx'], 'L0_ffn_of_cvx': _L0_ffn_in['of_cvx'], 'L0_ffn_sl_ccv': _L0_ffn_in['sl_ccv'], 'L0_ffn_of_ccv': _L0_ffn_in['of_ccv'], 'L0_ffn_alpha': _L0_ffn_in['alpha'], 'L0_ffn_Wc': _L0_ffn_in['Wc'], 'L0_ffn_bc': _L0_ffn_in['bc'], 'L0_ffn_Wg': _L0_ffn_in['Wg'], 'L0_ffn_bg': _L0_ffn_in['bg'], 'L0_ffn_Wd': _L0_ffn_in['Wd'], 'L0_ffn_bd': _L0_ffn_in['bd']}

def reference(x, adj, L0_gnn_w_rel1, L0_gnn_w_root1, L0_gnn_b1, L0_gnn_w_rel2, L0_gnn_w_root2, L0_gnn_b2, L0_ffn_Wt, L0_ffn_bt, L0_ffn_sl_cvx, L0_ffn_of_cvx, L0_ffn_sl_ccv, L0_ffn_of_ccv, L0_ffn_alpha, L0_ffn_Wc, L0_ffn_bc, L0_ffn_Wg, L0_ffn_bg, L0_ffn_Wd, L0_ffn_bd):
    import jax
    import jax.numpy as jnp

    def _L0_gnn_ref(encoded_spans, w_rel1, w_root1, b1, w_rel2, w_root2, b2, aug_adj, punct_graph):
        import jax, jax.numpy as jnp
        import numpy as np
        BS, N, D, R = (16, 256, 128, 2)
        mask_punct = (punct_graph == 1) & (aug_adj != 1)
        mask_aug = aug_adj == 1
        masks = jnp.stack([mask_punct, mask_aug]).astype(encoded_spans.dtype)
        deg = jnp.maximum(masks.sum(axis=2), 1.0)[..., None]

        def conv(x, w_rel, w_root, b):
            out = jnp.einsum('bnd,de->bne', x, w_root) + b
            for r in range(R):
                agg = jnp.einsum('bij,bid->bjd', masks[r], x) / deg[r]
                out = out + jnp.einsum('bjd,de->bje', agg, w_rel[r])
            return out
        h = jax.nn.elu(conv(encoded_spans, w_rel1, w_root1, b1))
        h = jax.nn.elu(conv(h, w_rel2, w_root2, b2))
        return h

    def _L0_ffn_ref(x, Wt, bt, sl_cvx, of_cvx, sl_ccv, of_ccv, alpha, Wc, bc, Wg, bg, Wd, bd):
        import jax, jax.numpy as jnp
        import numpy as np
        B, S, D_MODEL, FFN, P = (8, 2048, 128, 512, 8)
        BLK = 128
        Bx, Sx, D = x.shape
        T = Bx * Sx
        xf = x.reshape(T, D)
        xb = xf.reshape(T // BLK, BLK, D)
        s = jax.nn.sigmoid(alpha)

        def blk_fn(xx):
            t = jnp.max(xx[:, None, :] + Wt[None, :, :], axis=-1) + bt
            z = t[:, :, None]
            cvx = jnp.max(z * sl_cvx[None] + of_cvx[None], axis=-1)
            ccv = jnp.min(z * sl_ccv[None] + of_ccv[None], axis=-1)
            return s * cvx + (1.0 - s) * ccv
        trop = jax.lax.map(blk_fn, xb).reshape(T, FFN)
        classical = jax.nn.gelu(xf @ Wc + bc, approximate=False)
        g = jax.nn.sigmoid(xf @ Wg + bg)
        fused = g * trop + (1.0 - g) * classical
        out = fused @ Wd + bd
        return out.reshape(Bx, Sx, D)
    x = x + _L0_gnn_ref(_layernorm(x, axis=-1), L0_gnn_w_rel1, L0_gnn_w_root1, L0_gnn_b1, L0_gnn_w_rel2, L0_gnn_w_root2, L0_gnn_b2, adj, adj)
    x = x + _L0_ffn_ref(_layernorm(x, axis=-1), L0_ffn_Wt, L0_ffn_bt, L0_ffn_sl_cvx, L0_ffn_of_cvx, L0_ffn_sl_ccv, L0_ffn_of_ccv, L0_ffn_alpha, L0_ffn_Wc, L0_ffn_bc, L0_ffn_Wg, L0_ffn_bg, L0_ffn_Wd, L0_ffn_bd)
    return x

_drawn_inputs = setup_inputs


def setup_inputs(seed=0):
    import zlib

    import numpy as np

    out = dict(_drawn_inputs(seed))
    spreads = {'L0_gnn_b1': (0.0, 0.1),
     'L0_gnn_b2': (0.0, 0.1),
     'L0_ffn_alpha': (0.0, 0.8),
     'L0_ffn_bc': (0.0, 2.0),
     'L0_ffn_bg': (2.0, 0.2),
     'L0_ffn_bd': (0.0, 0.1)}
    factors = {'L0_ffn_Wt': 3.619,
     'L0_ffn_bt': 3.565,
     'L0_ffn_of_cvx': 3.921,
     'L0_ffn_of_ccv': 4.067,
     'L0_ffn_Wg': 4.809}
    for name, (base, spread) in spreads.items():
        noise = np.random.default_rng([zlib.crc32(name.encode()), seed]).standard_normal(out[name].shape)
        drawn = base * np.exp(spread * noise) if base else spread * noise
        out[name] = jnp.asarray(drawn.astype(out[name].dtype))
    for name, factor in factors.items():
        out[name] = (out[name] * factor).astype(out[name].dtype)
    return out
```

```python
from contextlib import ExitStack

import concourse.bass as bass
from concourse import mybir

F32 = mybir.dt.float32
BF16 = mybir.dt.bfloat16
I32 = mybir.dt.int32
U32 = mybir.dt.uint32
ALU = mybir.AluOpType
ACT = mybir.ActivationFunctionType
AX_X = mybir.AxisListType.X

P = 128
BATCHES = 16
TILES = 4
NODES = TILES * P
D = 128
FFN = 512
CHUNKS = FFN // P
LINES = 8
TOP = 16
PLAN = (2, 2, 2, 4)
SLOTS = max(PLAN)
DRAWN = [2 * n for n in PLAN]
STEPS = [2 * (n - 1) for n in PLAN]
V_SL, V_OF = 0, 2 * LINES
V_SS = 4 * LINES
V_SO = V_SS + 2 * SLOTS
V_BC, V_BG = V_SO + 2 * SLOTS, V_SO + 2 * SLOTS + 1
V_N = V_BG + 1
V_COLS = V_N + 2
PARTS = 3
ROUNDS = TILES * TOP
SLOT_ROUNDS = 8
EPS = 1e-5
MARGIN = 1e-4
Z_LO, Z_HI = 1.4, 4.8
LOWEST = -3.0e38
T_EVENTS = 5
NCOLS = BATCHES * TILES


class At:

    def __init__(self, b, parity, half):
        self.b, self.parity, self.half = b, parity, half

    def plus(self, n):
        h = self.half + (self.parity + n) // 2
        return At(self.b + n, (self.parity + n) % 2, h)


def fixed(b):
    return At(b, b % 2, b // 2)


def wait(engine, semaphore, value):
    if isinstance(value, int) and value <= 0:
        return
    engine.wait_ge(semaphore, value)


def wait_apart(engine, semaphore, value, held):
    if isinstance(value, int):
        wait(engine, semaphore, value)
        return
    register = engine.to_reg(value)
    engine.wait_ge(held, 1)
    engine.wait_ge(semaphore, register)


def build(nc, x, adj, w_rel1, w_root1, b1, w_rel2, w_root2, b2, Wt, bt, sl_cvx, of_cvx,
          sl_ccv, of_ccv, alpha, Wc, bc, Wg, bg, Wd, bd, out):
    ctx = ExitStack()
    with ctx:
        def sb(name, shape, dt=F32):
            return ctx.enter_context(nc.sbuf_tensor(name, shape, dt))

        def bank(name, shape=(P, 512), dt=F32):
            return ctx.enter_context(nc.psum_tensor(name, list(shape), dt))

        def sem(name):
            return ctx.enter_context(nc.semaphore(name))

        ident = sb("ident", [P, P])
        identb = sb("identb", [P, P], BF16)
        onesb = sb("onesb", [P, P], BF16)
        below = sb("below", [P, P], BF16)
        zerof = sb("zerof", [P, P])
        row0 = sb("row0", [P, P])
        iota_i = sb("iota_i", [P, P], I32)
        iota = sb("iota", [P, P])
        minus_half = sb("minus_half", [P, TILES])
        w_root = [sb("w_root1_s", [P, D]), sb("w_root2_s", [P, D])]
        w_rel = [sb("w_rel1_s", [P, D]), sb("w_rel2_s", [P, D])]
        bias = [sb("b1_s", [P, 1]), sb("b2_s", [P, 1])]
        wc = sb("wc", [P, FFN])
        wg = sb("wg", [P, FFN])
        wd = sb("wd", [P, CHUNKS, D])
        bc_s = sb("bc_s", [P, CHUNKS])
        bg_s = sb("bg_s", [P, CHUNKS])
        bd_s = sb("bd_s", [P, D])
        bt_s = sb("bt_s", [P, CHUNKS])
        al = sb("al", [P, CHUNKS])
        wt_f = sb("wt_f", [P, CHUNKS, D])
        wt_r = sb("wt_r", [P, FFN])
        wcT = sb("wcT", [P, CHUNKS, D])
        wgT = sb("wgT", [P, CHUNKS, D])
        wt = [sb(f"wt{p}", [P, FFN], BF16) for p in range(PARTS)]
        wmax = sb("wmax", [P, CHUNKS])
        wmin = sb("wmin", [P, CHUNKS])
        wmax_all = sb("wmax_all", [P, FFN])
        FC = 2 * CHUNKS
        table = sb("table", [P, CHUNKS, V_COLS])
        feat = sb("feat", [P, CHUNKS, V_COLS])
        slope = sb("slope", [P, FC, LINES])
        offs = sb("offs", [P, FC, LINES])
        share = sb("share", [P, FC])
        end_a = sb("end_a", [P, FC, LINES])
        end_b = sb("end_b", [P, FC, LINES])
        need = sb("need", [P, FC, LINES])
        rank = sb("rank", [P, FC, LINES])
        count = sb("count", [P, FC])
        pick = sb("pick", [P, FC, LINES])
        picked = sb("picked", [P, FC, LINES])
        empty = sb("empty", [P, FC])
        lo_hi = sb("lo_hi", [P, 2, CHUNKS])
        slot_sl = sb("slot_sl", [P, SLOTS, FC])
        slot_of = sb("slot_of", [P, SLOTS, FC])
        key = sb("key", [P, CHUNKS])
        key_half = sb("key_half", [P, CHUNKS])
        key_sum = sb("key_sum", [P, CHUNKS])
        place = sb("place", [P, CHUNKS])
        place_i = sb("place_i", [P, FFN], I32)
        wt_fp = [sb(f"wt_f{p}", [P, CHUNKS, D], BF16) for p in range(PARTS)]
        permb = sb("permb", [P, CHUNKS, FFN], BF16)
        planned = sb("planned", [P, CHUNKS, 2])
        over = sb("over", [P, CHUNKS, 2])
        over1 = sb("over1", [P, 1])
        over1b = sb("over1b", [P, 1], BF16)
        over_all = sb("over_all", [P, 1])

        xs = [sb(f"x{q}", [P, TILES, D]) for q in range(2)]
        adjs = [sb(f"adj{q}", [P, TILES, NODES], I32) for q in range(2)]
        mask = sb("mask", [P, TILES, NODES], BF16)
        st = sb("st", [P, TILES, 6])
        mv1 = sb("mv1", [P, TILES, 2])
        ve1 = sb("ve1", [P, TILES])
        rs1 = sb("rs1", [P, TILES])
        mv2 = sb("mv2", [P, TILES, 2])
        ve2 = sb("ve2", [P, TILES])
        rs2 = sb("rs2", [P, TILES])
        xn = sb("xn", [P, TILES, D])
        xT = sb("xT", [P, NODES])
        hT = [sb(f"h{q}T", [P, NODES]) for q in range(2)]
        yp = [sb(f"y{p}", [P, TILES, D], BF16) for p in range(PARTS)]
        y_rest = sb("y_rest", [P, NODES])
        rdeg = sb("rdeg", [P, NODES])
        deg = sb("deg", [P, NODES])
        u = sb("u", [P, NODES])
        v = sb("v", [P, NODES])
        ev = sb("ev", [P, NODES])
        rv = sb("rv", [P, NODES])
        em = sb("em", [P, NODES])
        x2 = [sb(f"x2{q}", [P, TILES, D]) for q in range(2)]
        x2_before = sb("x2_before", [P, TILES, D])
        z = sb("z", [P, TILES, D])
        z_left = sb("z_left", [P, D])
        top = [sb(f"top{q}", [P, TOP]) for q in range(2)]
        top_at = [sb(f"top_at{q}", [P, TOP], U32) for q in range(2)]
        zmax = [sb(f"zmax{q}", [P, TILES]) for q in range(2)]
        hot = sb("hot", [P, TOP, P], BF16)
        hotT = [sb(f"hotT{q}", [P, TOP, P], BF16) for q in range(2)]
        acc = [sb(f"acc{q}", [P, FFN]) for q in range(2)]
        beyond = sb("beyond", [P, FFN], BF16)
        open_n = sb("open_n", [P, TILES])
        fl_a = sb("fl_a", [P, TILES])
        fl_b = sb("fl_b", [P, TILES])
        fl_c = sb("fl_c", [P, TILES])
        flags = sb("flags", [P, NCOLS])
        tT = [sb(f"tT{q}", [P, CHUNKS, NODES]) for q in range(2)]
        zT = sb("zT", [P, NODES])
        cl = [sb(f"cl{c}", [P, NODES]) for c in range(CHUNKS)]
        gt = [sb(f"gt{c}", [P, NODES]) for c in range(CHUNKS)]
        line = [sb(f"line{n}", [P, NODES]) for n in range(2 * SLOTS)]
        cvx = [sb(f"cvx{q}", [P, NODES]) for q in range(2)]
        ccv = [sb(f"ccv{q}", [P, NODES]) for q in range(2)]
        trop = sb("trop", [P, NODES])
        diff = sb("diff", [P, NODES])
        fused = [sb(f"fused{c}", [P, NODES]) for c in range(CHUNKS)]
        o_s = sb("o_s", [P, TILES, D])

        fb = sb("fb", [P, NCOLS], BF16)
        ff = sb("ff", [P, NCOLS])
        tot = [sb(f"tot{q}", [P, NCOLS]) for q in range(2)]
        total = sb("total", [P, NCOLS])
        rk = sb("rk", [P, NCOLS])
        rk_i = sb("rk_i", [P, NCOLS], I32)
        rk_c_i = sb("rk_c_i", [P, NCOLS], I32)
        rk_s_i = sb("rk_s_i", [P, NCOLS], I32)
        rk_c = sb("rk_c", [P, NCOLS])
        rk_s = sb("rk_s", [P, NCOLS])
        tok_i = sb("tok_i", [P, NCOLS], I32)
        tok = sb("tok", [P, NCOLS])
        n_tiles_f = sb("n_tiles_f", [P, 1])
        n_tiles_i = sb("n_tiles_i", [P, 1], I32)
        n_tiles_s = sb("n_tiles_s", [P, 1], I32)
        n_tiles_m = sb("n_tiles_m", [P, 1], I32)
        at_slot = [sb(f"at_slot{q}", [P, P]) for q in range(2)]
        at_tile = [sb(f"at_tile{q}", [P, NCOLS]) for q in range(2)]
        got = sb("got", [P, NCOLS])
        hole = sb("hole", [P, NCOLS])
        src = sb("src", [P, NCOLS])
        dst = sb("dst", [P, NCOLS])
        src_i = sb("src_i", [P, 1], U32)
        dst_i = sb("dst_i", [P, 1], U32)
        g_x = sb("g_x", [P, D])
        g_st = sb("g_st", [P, 6])
        g_mv = sb("g_mv", [P, 2])
        g_ve = sb("g_ve", [P, 1])
        g_rs = sb("g_rs", [P, 1])
        g_z = sb("g_z", [P, D])
        g_zT = sb("g_zT", [P, P])
        g_acc = acc[0]
        g_tT, g_cl, g_gt, g_fu = [w[:].rearrange("p (c n) -> p c n", c=CHUNKS) for w in (line[0], cl[0], gt[0], fused[0])]
        g_line = [sb(f"g_line{q}", [P, P]) for q in range(2)]
        g_pw = [line[1 + q][:].rearrange("p (c n) -> p c n", c=CHUNKS) for q in range(2)]
        g_o = sb("g_o", [P, D])

        x2_dram = nc.dram_tensor("x2_rows", [BATCHES * NODES, D], F32, kind="Internal").ap()

        G = [bank(f"gathered{q}") for q in range(3)]
        H = bank("hot_bank", (P, 1024), BF16)
        P1 = bank("gnn_bank1")
        P2 = bank("gnn_bank2")
        T = bank("transpose_bank")
        FB = bank("ffn_bank")

        s_const = sem("constants_made")
        s_wload = sem("weights_loaded")
        s_wtf = sem("wt_parts_made")
        s_wT = sem("wc_wg_transposed")
        s_wTc = sem("wc_wg_transposed_copied")
        s_key = sem("keys_made")
        s_keyr = sem("keys_spread")
        s_perm = sem("order_made")
        s_put = sem("put_in_order")
        s_putc = sem("put_in_order_copied")
        s_share = sem("tanh_alpha")
        s_setup_dve = sem("setup_dve")
        s_setup_done = sem("setup_done")
        s_over = sem("over_counted")
        s_xin = [sem(f"x_in{q}") for q in range(2)]
        s_adjin = [sem(f"adj_in{q}") for q in range(2)]
        s_mask = sem("mask_made")
        s_ln1_st = sem("ln1_stats")
        s_ln1_mv = sem("ln1_meanvar")
        s_ln1_rs = sem("ln1_rstd")
        s_xn = sem("xn_ready")
        s_p1 = sem("gnn_bank1_full")
        s_p2 = sem("gnn_bank2_full")
        s_xT = sem("xT_ready")
        s_yhi = sem("y_hi")
        s_yrest = sem("y_rest")
        s_ymid = sem("y_mid")
        s_ylo = sem("y_lo")
        s_deg = sem("degree")
        s_u = sem("u_ready")
        s_v = sem("v_ready")
        s_eluact = sem("elu_exp_relu")
        s_em = sem("exp_minus_one")
        s_h = sem("h_ready")
        s_x2 = sem("x2_ready")
        s_ln2_st = sem("ln2_stats")
        s_ln2_mv = sem("ln2_meanvar")
        s_ln2_rs = sem("ln2_rstd")
        s_z = sem("z_ready")
        s_top = sem("top_found")
        s_zmax = sem("zmax_kept")
        s_hot = sem("hot_made")
        s_H = sem("hot_bank_full")
        s_hotT = sem("hotT_copied")
        s_gath = sem("round_gathered")
        s_round = sem("round_done")
        s_open = sem("open_counted")
        s_flags = sem("flags_ready")
        s_T = sem("transpose_bank_full")
        s_Tc = sem("transpose_bank_copied")
        s_F = sem("ffn_bank_full")
        s_Fa = sem("gelu_tanh_done")
        s_gate = sem("gate_ready")
        s_line = sem("line_ready")
        s_pwl = sem("pwl_step")
        s_trop = sem("trop_step")
        s_fused = sem("fused_ready")
        s_keep = sem("x2_kept")
        s_out = sem("out_summed")
        s_outd = sem("out_stored")
        s_x2d = sem("x2_stored")
        q_dve = sem("g_dve")
        q_rank = sem("g_flags_counted")
        q_fb = sem("g_flags_bf16")
        q_hot = sem("g_one_hots")
        q_hotu = sem("g_one_hots_used")
        q_list = sem("g_list")
        q_n = sem("g_tiles_known")
        q_idx = sem("g_indices")
        q_gath = sem("g_rows_in")
        q_mv = sem("g_meanvar")
        q_rs = sem("g_rstd")
        q_z = sem("g_z")
        q_zTp = sem("g_zT_psum")
        q_zT = sem("g_zT")
        q_wg = sem("g_gathered")
        q_rd = sem("g_round")
        q_tTp = sem("g_tT_psum")
        q_tT = sem("g_tT")
        q_F = sem("g_ffn_psum")
        q_Fa = sem("g_gelu_tanh")
        q_fu = sem("g_fused")
        q_o = sem("g_out_psum")
        q_os = sem("g_out_summed")
        q_st = sem("g_stored")

        x_t = x.rearrange("b (j p) d -> b p j d", p=P)
        adj_t = adj.rearrange("b (j p) m -> b p j m", p=P)
        out_t = out.rearrange("b (j p) d -> b p j d", p=P)
        out_rows = out.rearrange("b n d -> (b n) d")
        x2_t = x2_dram.rearrange("(b j p) d -> b p j d", j=TILES, p=P)
        weight_loads = [
            (w_root[0][:], w_root1), (w_root[1][:], w_root2), (w_rel[0][:], w_rel1[1]), (w_rel[1][:], w_rel2[1]),
            (bias[0][:], b1.rearrange("(p o) -> p o", o=1)), (bias[1][:], b2.rearrange("(p o) -> p o", o=1)),
            (wt_f[:], Wt.rearrange("(c p) d -> p c d", p=P)),
            (wc[:], Wc), (wg[:], Wg), (wd[:], Wd.rearrange("(c p) d -> p c d", p=P)),
            (bc_s[:], bc.rearrange("(c p) -> p c", p=P)), (bg_s[:], bg.rearrange("(c p) -> p c", p=P)),
            (bt_s[:], bt.rearrange("(c p) -> p c", p=P)), (al[:], alpha.rearrange("(c p) -> p c", p=P)),
            (bd_s[0:1, :], bd.rearrange("(o d) -> o d", o=1)),
            (slope[:, 0:CHUNKS, :], sl_cvx.rearrange("(c p) q -> p c q", p=P)),
            (slope[:, CHUNKS:FC, :], sl_ccv.rearrange("(c p) q -> p c q", p=P)),
            (offs[:, 0:CHUNKS, :], of_cvx.rearrange("(c p) q -> p c q", p=P)),
            (offs[:, CHUNKS:FC, :], of_ccv.rearrange("(c p) q -> p c q", p=P)),
        ]
        LOADED = 16 * len(weight_loads)
        N_CONST = 12
        ALL_STEPS, ALL_DRAWN = sum(STEPS), sum(DRAWN)
        perm = fused
        work = [u, v, ev, rv, em]

        def bank_rounds_before(i, at):
            if i >= 3:
                return at.b * ROUNDS + i - 2
            return (at.b - 1) * ROUNDS + {0: 64, 1: 62, 2: 63}[i]

        block = ctx.enter_context(nc.Block())

        @block.sync
        def _(sp):
            def load_x(at):
                wait(sp, s_x2, at.b - 1)
                sp.dma_start(xs[at.parity][:], x_t[at.b]).then_inc(s_xin[at.parity], 16)

            def load_adj(at):
                wait(sp, s_mask, at.b - 1)
                sp.dma_start(adjs[at.parity][:], adj_t[at.b]).then_inc(s_adjin[at.parity], 16)

            def store_x2(at):
                sp.wait_ge(s_x2, at.b + 1)
                sp.dma_start(x2_t[at.b], x2[at.parity][:]).then_inc(s_x2d, 16)

            def store_out(at):
                sp.wait_ge(s_out, at.b + 1)
                sp.dma_start(out_t[at.b], o_s[:]).then_inc(s_outd, 16)

            def tick(at, finish, gnn, load):
                if load:
                    load_adj(at.plus(3))
                if gnn:
                    store_x2(at.plus(1))
                if load:
                    load_x(at.plus(3))
                if finish:
                    store_out(at.plus(-1))

            load_x(fixed(0))
            load_adj(fixed(0))
            sp.wait_ge(s_const, N_CONST)
            for to, of in weight_loads:
                sp.dma_start(to, of, allow_slow_non_contiguous=True).then_inc(s_wload, 16)
            load_x(fixed(1))
            load_adj(fixed(1))
            load_adj(fixed(2))
            store_x2(fixed(0))
            load_x(fixed(2))
            tick(fixed(0), False, True, True)
            tick(fixed(1), True, True, True)
            with sp.Fori(0, 5) as i:
                tick(At(i * 2 + 2, 0, i + 1), True, True, True)
                tick(At(i * 2 + 3, 1, i + 1), True, True, True)
            tick(fixed(12), True, True, True)
            tick(fixed(13), True, True, False)
            tick(fixed(14), True, True, False)
            tick(fixed(15), True, False, False)
            store_out(fixed(15))
            sp.wait_ge(s_outd, 16 * BATCHES)
            sp.wait_ge(s_x2d, 16 * BATCHES)

        @block.gpsimd
        def _(pool):
            pool.memset(ident[:], 0.0).then_inc(s_const, 1)
            pool.memset(identb[:], 0.0).then_inc(s_const, 1)
            pool.memset(onesb[:], 1.0).then_inc(s_const, 1)
            pool.memset(below[:], 1.0).then_inc(s_const, 1)
            pool.memset(row0[:], 1.0).then_inc(s_const, 1)
            pool.memset(zerof[:], 0.0).then_inc(s_const, 1)
            pool.memset(bd_s[:], 0.0).then_inc(s_const, 1)
            pool.memset(minus_half[:], -0.5).then_inc(s_const, 1)
            pool.wait_ge(s_const, 8)
            pool.affine_select(out=ident[:], in_=ident[:], compare_op=ALU.not_equal, fill=1.0, base=0,
                               pattern=[[-1, P]], channel_multiplier=1).then_inc(s_const, 1)
            pool.affine_select(out=identb[:], in_=identb[:], compare_op=ALU.not_equal, fill=1.0, base=0,
                               pattern=[[-1, P]], channel_multiplier=1).then_inc(s_const, 1)
            pool.affine_select(out=below[:], in_=below[:], compare_op=ALU.is_gt, fill=0.0, base=0,
                               pattern=[[1, P]], channel_multiplier=-1).then_inc(s_const, 1)
            pool.affine_select(out=row0[:], in_=row0[:], compare_op=ALU.is_ge, fill=0.0, base=0,
                               pattern=[[0, P]], channel_multiplier=-1).then_inc(s_const, 1)
            pool.iota(iota_i[:], pattern=[[1, P]], base=0, channel_multiplier=0).then_inc(s_const, 1)
            pool.iota(place_i[:], pattern=[[1, FFN]], base=0, channel_multiplier=0).then_inc(s_const, 1)
            pool.iota(tok_i[:], pattern=[[P, NCOLS]], base=1, channel_multiplier=1).then_inc(s_const, 1)
            pool.wait_ge(s_const, N_CONST + 3)
            pool.tensor_copy(iota[:], iota_i[:]).then_inc(s_const, 1)
            pool.tensor_copy(tok[:], tok_i[:]).then_inc(s_const, 1)
            pool.wait_ge(s_const, N_CONST + 5)

            def make_mask(at):
                pool.wait_ge(s_adjin[at.parity], 16 * (at.half + 1))
                wait_apart(pool, s_p1, 6 * (at.b - 1) + 5, s_const)
                pool.tensor_scalar(mask[:], adjs[at.parity][:], 1, None, ALU.is_equal).then_inc(s_mask, 1)

            def rstd(at, meanvar, s_mv, ve, rs, s_rs):
                wait_apart(pool, s_mv, at.b + 1, s_const)
                pool.tensor_scalar(ve[:], meanvar[:, :, 1], EPS, None, ALU.add).then_inc(s_rs, 1)
                pool.wait_ge(s_rs, 2 * at.b + 1)
                pool.tensor_tensor(rs[:], ve[:], minus_half[:], ALU.pow).then_inc(s_rs, 1)

            def one_hots(at, j):
                tile = at.b * TILES + j
                q = j % 2
                for group in range(2):
                    wait_apart(pool, s_top, 5 * tile + (3 if group == 0 else 5), s_const)
                    if group == 0:
                        pool.tensor_copy(zmax[at.parity][:, j:j + 1], top[q][:, 0:1]).then_inc(s_zmax, 1)
                    wait_apart(pool, s_H, 2 * (tile - 1) + group + 1, s_const)
                    for k in range(8 * group, 8 * group + 8):
                        last = pool.tensor_scalar(hot[:, k, :], iota[:], top_at[q][:, k:k + 1], None, ALU.is_equal)
                    last.then_inc(s_hot, 1)

            def elu(at, layer):
                wait_apart(pool, s_eluact, 4 * at.b + 2 * layer + 2, s_const)
                pool.tensor_scalar(em[:], ev[:], 1.0, -1.0, ALU.min, ALU.add).then_inc(s_em, 1)
                pool.wait_ge(s_em, 2 * at.b + layer + 1)
                pool.tensor_tensor(hT[layer][:], em[:], rv[:], ALU.add).then_inc(s_h, 1)

            def fuse(at, c):
                wait_apart(pool, s_Fa, 8 * at.b + 2 * c + 2, s_const)
                pool.tensor_scalar(gt[c][:], gt[c][:], 0.5, 0.5, ALU.mult, ALU.add).then_inc(s_gate, 1)
                pool.wait_ge(s_pwl, ALL_STEPS * at.b + sum(STEPS[:c + 1]))
                wait(pool, s_fused, 4 * at.b + c)
                pool.tensor_tensor(trop[:], cvx[c % 2][:], ccv[c % 2][:], ALU.subtract).then_inc(s_trop, 1)
                pool.wait_ge(s_trop, 12 * at.b + 3 * c + 1)
                pool.tensor_tensor(diff[:], trop[:], cl[c][:], ALU.subtract).then_inc(s_trop, 1)
                pool.wait_ge(s_trop, 12 * at.b + 3 * c + 2)
                pool.wait_ge(s_gate, 4 * at.b + c + 1)
                pool.tensor_tensor(trop[:], diff[:], gt[c][:], ALU.mult).then_inc(s_trop, 1)
                pool.wait_ge(s_trop, 12 * at.b + 3 * c + 3)
                wait(pool, s_F, 9 * at.b)
                pool.tensor_tensor(fused[c][:], trop[:], cl[c][:], ALU.add).then_inc(s_fused, 1)

            def note(at):
                wait_apart(pool, s_zmax, 4 * at.b + 4, s_const)
                pool.tensor_scalar(fl_a[:], zmax[at.parity][:], Z_LO, over_all[:], ALU.is_lt, ALU.add).then_inc(s_flags, 1)
                pool.tensor_scalar(fl_b[:], zmax[at.parity][:], Z_HI, None, ALU.is_gt).then_inc(s_flags, 1)
                pool.wait_ge(s_flags, 4 * at.b + 2)
                pool.tensor_tensor(fl_c[:], fl_a[:], fl_b[:], ALU.add).then_inc(s_flags, 1)
                pool.wait_ge(s_flags, 4 * at.b + 3)
                pool.wait_ge(s_open, 4 * at.b + 4)
                pool.tensor_tensor(flags[:, bass.ds(at.b * TILES, TILES)], fl_c[:], open_n[:], ALU.add)\
                    .then_inc(s_flags, 1)

            def tick(at, finish, gnn, ahead):
                before, after = at.plus(-1), at.plus(1)
                if finish:
                    wait_apart(pool, s_out, at.b - 1, s_const)
                    pool.tensor_copy(x2_before[:], x2[before.parity][:]).then_inc(s_keep, 1)
                one_hots(at, 1)
                one_hots(at, 2)
                if finish:
                    fuse(before, 0)
                if gnn:
                    elu(after, 0)
                if finish:
                    fuse(before, 1)
                one_hots(at, 3)
                if finish:
                    fuse(before, 2)
                    fuse(before, 3)
                if gnn:
                    elu(after, 1)
                if ahead:
                    make_mask(at.plus(2))
                if gnn:
                    rstd(after, mv2, s_ln2_mv, ve2, rs2, s_ln2_rs)
                    one_hots(after, 0)
                if ahead:
                    rstd(at.plus(2), mv1, s_ln1_mv, ve1, rs1, s_ln1_rs)
                note(at)

            make_mask(fixed(0))
            rstd(fixed(0), mv1, s_ln1_mv, ve1, rs1, s_ln1_rs)
            elu(fixed(0), 0)
            elu(fixed(0), 1)
            make_mask(fixed(1))
            rstd(fixed(0), mv2, s_ln2_mv, ve2, rs2, s_ln2_rs)
            rstd(fixed(1), mv1, s_ln1_mv, ve1, rs1, s_ln1_rs)
            one_hots(fixed(0), 0)
            pool.wait_ge(s_over, 2)
            tick(fixed(0), False, True, True)
            tick(fixed(1), True, True, True)
            with pool.Fori(0, 5) as i:
                tick(At(i * 2 + 2, 0, i + 1), True, True, True)
                tick(At(i * 2 + 3, 1, i + 1), True, True, True)
            tick(fixed(12), True, True, True)
            tick(fixed(13), True, True, True)
            tick(fixed(14), True, True, False)
            tick(fixed(15), True, False, False)
            pool.wait_ge(s_out, 15)
            pool.tensor_copy(x2_before[:], x2[1][:]).then_inc(s_keep, 1)
            for c in range(CHUNKS):
                fuse(fixed(15), c)

            pool.wait_ge(q_n, 1)
            tiles = pool.value_load(n_tiles_m[0:1, 0:1], min_val=1, max_val=NCOLS)
            pool.wait_ge(s_x2d, 16 * BATCHES)
            pool.wait_ge(s_outd, 16 * BATCHES)
            with pool.Fori(0, tiles) as g:
                wait_apart(pool, q_idx, g + 1, s_const)
                pool.indirect_dma_start(out=g_x[:], out_offset=None, in_=x2_dram,
                                        in_offset=bass.IndirectOffsetOnAxis(ap=src_i[:], axis=0))\
                    .then_inc(q_gath, 16)
                wait_apart(pool, q_mv, g + 1, s_const)
                pool.tensor_scalar(g_ve[:], g_mv[:, 1:2], EPS, None, ALU.add).then_inc(q_rs, 1)
                pool.wait_ge(q_rs, g * 2 + 1)
                pool.tensor_tensor(g_rs[:], g_ve[:], minus_half[:, 0:1], ALU.pow).then_inc(q_rs, 1)
                wait_apart(pool, q_os, g + 1, s_const)
                pool.indirect_dma_start(out=out_rows, in_=g_o[:], in_offset=None,
                                        out_offset=bass.IndirectOffsetOnAxis(ap=dst_i[:], axis=0),
                                        bounds_check=BATCHES * NODES - 1, oob_is_err=False)\
                    .then_inc(q_st, 16)
                wait_apart(pool, q_st, g * 16 + 16, s_const)

        @block.tensor
        def _(pe):
            pe.wait_ge(s_wload, LOADED)
            pe.wait_ge(s_const, N_CONST + 5)
            for to, w in ((FB, wc), (T, wg)):
                for c in range(CHUNKS):
                    last = pe.transpose(to[:, c * P:(c + 1) * P], w[:, c * P:(c + 1) * P], ident[:])
                last.then_inc(s_wT, 1)
            pe.wait_ge(s_key, 1)
            for c in range(CHUNKS):
                last = pe.matmul(G[0][:, c * P:(c + 1) * P], key[:, c:c + 1].to_broadcast([P, P]), ident[:],
                                 start=True, stop=True)
            last.then_inc(s_keyr, 1)
            pe.wait_ge(s_wtf, 1)
            pe.wait_ge(s_perm, 1)
            pe.wait_ge(s_wTc, 2)
            for part in range(PARTS):
                for c in range(CHUNKS):
                    last = pe.matmul(G[part][:], wt_fp[part][:, c, :], permb[:, c, :],
                                     start=(c == 0), stop=(c == CHUNKS - 1))
                last.then_inc(s_put, 1)
            for to, w in ((FB, wcT), (T, wgT)):
                for c in range(CHUNKS):
                    last = pe.matmul(to[:], w[:, c, :], perm[c][:], start=(c == 0), stop=(c == CHUNKS - 1))
                last.then_inc(s_put, 1)
            pe.wait_ge(s_putc, 1)
            for c in range(CHUNKS):
                last = pe.matmul(G[0][:], wmax[:, c:c + 1].to_broadcast([P, P]), perm[c][:],
                                 start=(c == 0), stop=(c == CHUNKS - 1))
            last.then_inc(s_put, 1)
            pe.wait_ge(s_putc, 2)
            for m in range(CHUNKS):
                for c in range(CHUNKS):
                    last = pe.matmul(G[1][:, m * P:(m + 1) * P], perm[c][:, m * P:(m + 1) * P], wd[:, c, :],
                                     start=(c == 0), stop=(c == CHUNKS - 1))
            last.then_inc(s_put, 1)
            pe.wait_ge(s_putc, 3)
            for m in range(CHUNKS):
                for c in range(CHUNKS):
                    last = pe.matmul(G[2][:, m * V_COLS:(m + 1) * V_COLS], perm[c][:, m * P:(m + 1) * P],
                                     table[:, c, :], start=(c == 0), stop=(c == CHUNKS - 1))
            last.then_inc(s_put, 1)

            def gnn_x_transposed(at):
                pe.wait_ge(s_xn, at.b + 1)
                wait(pe, s_x2, at.b)
                for j in range(TILES):
                    last = pe.transpose(P1[:, j * P:(j + 1) * P], xn[:, j, :], ident[:])
                last.then_inc(s_p1, 1)

            def gnn_y(at, layer):
                h = (xT, hT[0])[layer]
                if layer == 0:
                    pe.wait_ge(s_xT, at.b + 1)
                else:
                    pe.wait_ge(s_h, 2 * at.b + 1)
                    pe.wait_ge(s_u, 2 * at.b + 1)
                for j in range(TILES):
                    last = pe.matmul(P1[:, j * P:(j + 1) * P], h[:, j * P:(j + 1) * P], w_rel[layer][:],
                                     start=True, stop=True)
                last.then_inc(s_p1, 1)

            def gnn_degree(at):
                pe.wait_ge(s_mask, at.b + 1)
                wait(pe, s_v, 2 * at.b)
                for i in range(TILES):
                    last = pe.matmul(P2[:], onesb[:], mask[:, i, :], start=(i == 0), stop=(i == TILES - 1))
                last.then_inc(s_p2, 1)

            def gnn_root(at, layer):
                h = (xT, hT[0])[layer]
                if layer == 0:
                    pe.wait_ge(s_deg, 2 * at.b + 1)
                else:
                    pe.wait_ge(s_v, 2 * at.b + 1)
                pe.matmul(P2[:], w_root[layer][:], h[:], start=True, stop=True).then_inc(s_p2, 1)

            def gnn_aggregate(at, layer):
                pe.wait_ge(s_yhi, 2 * at.b + layer + 1)
                pe.wait_ge(s_yrest, 2 * at.b + layer + 1)
                pe.wait_ge(s_ymid, 2 * at.b + layer + 1)
                pe.wait_ge(s_ylo, 2 * at.b + layer + 1)
                for i in range(TILES):
                    for part in range(PARTS):
                        last = pe.matmul(P1[:], yp[part][:, i, :], mask[:, i, :],
                                         start=(i == 0 and part == 0), stop=(i == TILES - 1 and part == PARTS - 1))
                last.then_inc(s_p1, 1)

            def gnn_back(at):
                pe.wait_ge(s_h, 2 * at.b + 2)
                pe.wait_ge(s_u, 2 * at.b + 2)
                for j in range(TILES):
                    last = pe.transpose(P1[:, j * P:(j + 1) * P], hT[1][:, j * P:(j + 1) * P], ident[:])
                last.then_inc(s_p1, 1)

            def transpose_hots(at, j, group):
                pair = 2 * (at.b * TILES + j) + group
                pe.wait_ge(s_hot, pair + 1)
                wait(pe, s_hotT, pair)
                for k in range(8):
                    last = pe.transpose(H[:, k * P:(k + 1) * P], hot[:, 8 * group + k, :], identb[:])
                last.then_inc(s_H, 1)

            def transpose_t(at, j):
                pe.wait_ge(s_round, at.b * ROUNDS + (j + 1) * TOP)
                event = at.b * T_EVENTS + (0, 2, 3, 4)[j]
                wait(pe, s_Tc, event)
                for c in range(CHUNKS):
                    last = pe.transpose(T[:, c * P:(c + 1) * P], acc[j % 2][:, c * P:(c + 1) * P], ident[:])
                last.then_inc(s_T, 1)

            def transpose_z(at):
                pe.wait_ge(s_z, at.b + 1)
                wait(pe, s_Tc, at.b * T_EVENTS + 1)
                for j in range(TILES):
                    last = pe.transpose(T[:, j * P:(j + 1) * P], z[:, j, :], ident[:])
                last.then_inc(s_T, 1)

            def ffn_in(at, c):
                pe.wait_ge(s_Tc, at.b * T_EVENTS + 2)
                for n, w in ((0, wc), (1, wg)):
                    wait(pe, s_Fa, 8 * at.b + 2 * c + n)
                    if c == 0 and n == 0:
                        wait(pe, s_out, at.b)
                    pe.matmul(FB[:], w[:, c * P:(c + 1) * P], zT[:], start=True, stop=True).then_inc(s_F, 1)

            def ffn_out(at):
                pe.wait_ge(s_fused, 4 * at.b + 4)
                pe.wait_ge(s_Fa, 8 * at.b + 8)
                for j in range(TILES):
                    o = FB[:, j * P:(j + 1) * P]
                    pe.matmul(o, row0[:], bd_s[:], start=True, stop=False)
                    for c in range(CHUNKS):
                        last = pe.matmul(o, fused[c][:, j * P:(j + 1) * P], wd[:, c, :],
                                         start=False, stop=(c == CHUNKS - 1))
                last.then_inc(s_F, 1)

            def tick(at, finish, gnn):
                before, after = at.plus(-1), at.plus(1)
                for j in range(TILES):
                    for k in range(TOP):
                        i = j * TOP + k
                        s, r = divmod(i, SLOT_ROUNDS)
                        if k % 8 == 0:
                            pe.wait_ge(s_hotT, 2 * (at.b * TILES + j) + k // 8 + 1)
                        wait(pe, s_round, bank_rounds_before(i, at))
                        for part in range(PARTS):
                            last = pe.matmul(G[i % 3][:], hotT[j % 2][:, k, :], wt[part][:],
                                             start=(part == 0), stop=(part == PARTS - 1))
                        last.then_inc(s_gath, 1)
                        if s % 2 == 0 and r == 2:
                            if j > 0:
                                transpose_t(at, j - 1)
                            elif finish:
                                transpose_t(before, TILES - 1)
                        if finish and s in (0, 1) and r == 3:
                            ffn_in(before, 2 * s)
                            ffn_in(before, 2 * s + 1)
                        if finish and s == 6 and r == 3:
                            ffn_out(before)
                        if s % 2 == 1 and r == 4:
                            if j < TILES - 1:
                                transpose_hots(at, j + 1, 0)
                            elif gnn:
                                transpose_hots(after, 0, 0)
                        if s % 2 == 1 and r == 7:
                            if j < TILES - 1:
                                transpose_hots(at, j + 1, 1)
                            elif gnn:
                                transpose_hots(after, 0, 1)
                        if s == 3 and r == 6:
                            transpose_z(at)
                        if gnn and r == 7:
                            if s == 0:
                                gnn_x_transposed(after)
                            if s == 1:
                                gnn_y(after, 0)
                                gnn_degree(after)
                            if s == 2:
                                gnn_root(after, 0)
                                gnn_aggregate(after, 0)
                            if s == 3:
                                gnn_y(after, 1)
                            if s == 4:
                                gnn_root(after, 1)
                                gnn_aggregate(after, 1)
                            if s == 5:
                                gnn_back(after)

            first = fixed(0)
            gnn_x_transposed(first)
            gnn_y(first, 0)
            gnn_degree(first)
            gnn_root(first, 0)
            gnn_aggregate(first, 0)
            gnn_y(first, 1)
            gnn_root(first, 1)
            gnn_aggregate(first, 1)
            gnn_back(first)
            transpose_hots(first, 0, 0)
            transpose_hots(first, 0, 1)
            pe.wait_ge(s_putc, 8)
            pe.wait_ge(s_setup_done, 1)
            pe.matmul(T[:, 0:1], onesb[:], over1b[:], start=True, stop=True).then_inc(s_over, 1)
            pe.wait_ge(s_over, 2)
            tick(first, False, True)
            tick(fixed(1), True, True)
            with pe.Fori(0, 5) as i:
                tick(At(i * 2 + 2, 0, i + 1), True, True)
                tick(At(i * 2 + 3, 1, i + 1), True, True)
            tick(fixed(12), True, True)
            tick(fixed(13), True, True)
            tick(fixed(14), True, True)
            tick(fixed(15), True, False)
            transpose_t(fixed(15), TILES - 1)
            for c in range(CHUNKS):
                ffn_in(fixed(15), c)
            ffn_out(fixed(15))

            pe.wait_ge(q_fb, 1)
            pe.wait_ge(s_Tc, T_EVENTS * BATCHES)
            pe.matmul(T[:, 0:NCOLS], below[:], fb[:], start=True, stop=True)
            pe.matmul(T[:, NCOLS:2 * NCOLS], onesb[:], fb[:], start=True, stop=True).then_inc(q_rank, 1)
            pe.wait_ge(s_out, BATCHES)
            pe.matmul(FB[:, 0:NCOLS], zerof[:], zerof[:, 0:NCOLS], start=True, stop=False)
            with pe.Fori(0, NCOLS // 2) as i:
                for q in range(2):
                    pe.wait_ge(q_hot, i * 2 + q + 1)
                    pe.matmul(FB[:, 0:NCOLS], at_slot[q][:], at_tile[q][:], start=False, stop=False)\
                        .then_inc(q_hotu, 1)
            pe.matmul(FB[:, 0:NCOLS], zerof[:], zerof[:, 0:NCOLS], start=False, stop=True).then_inc(q_list, 1)
            pe.wait_ge(q_n, 1)
            tiles = pe.value_load(n_tiles_m[0:1, 0:1], min_val=1, max_val=NCOLS)
            pe.wait_ge(q_n, 2)
            with pe.Fori(0, tiles) as g:
                pe.wait_ge(q_z, g + 1)
                pe.transpose(T[:, 0:P], g_z[:], ident[:]).then_inc(q_zTp, 1)
                with pe.Fori(0, D // 8) as h:
                    for k in range(8):
                        pe.wait_ge(q_rd, g * (D + 1) + h * 8 + k)
                        hot_d = identb[:, bass.ds(h * 8 + k, 1)].to_broadcast([P, P])
                        for part in range(PARTS):
                            last = pe.matmul(G[k % 2][:], hot_d, wt[part][:],
                                             start=(part == 0), stop=(part == PARTS - 1))
                        last.then_inc(q_wg, 1)
                pe.wait_ge(q_rd, g * (D + 1) + D + 1)
                pe.wait_ge(q_zT, g + 1)
                for c in range(CHUNKS):
                    last = pe.transpose(T[:, c * P:(c + 1) * P], g_acc[:, c * P:(c + 1) * P], ident[:])
                last.then_inc(q_tTp, 1)
                for n, w in ((0, wc), (1, wg)):
                    pe.wait_ge(q_Fa, g * 2 + n)
                    for c in range(CHUNKS):
                        last = pe.matmul(FB[:, c * P:(c + 1) * P], w[:, c * P:(c + 1) * P], g_zT[:],
                                         start=True, stop=True)
                    last.then_inc(q_F, 1)
                pe.wait_ge(q_fu, g + 1)
                pe.wait_ge(q_Fa, g * 2 + 2)
                pe.matmul(FB[:, 0:P], row0[:], bd_s[:], start=True, stop=False)
                for c in range(CHUNKS):
                    last = pe.matmul(FB[:, 0:P], g_fu[:, c, :], wd[:, c, :], start=False, stop=(c == CHUNKS - 1))
                last.then_inc(q_o, 1)

        @block.scalar
        def _(act):
            act.wait_ge(s_wload, LOADED)
            act.activation(share[:, 0:CHUNKS], al[:], ACT.Tanh, scale=0.5).then_inc(s_share, 1)
            for n, (to, of) in enumerate(((wcT, FB), (wgT, T))):
                act.wait_ge(s_wT, n + 1)
                act.activation(to[:].rearrange("p c d -> p (c d)"), of[:], ACT.Copy).then_inc(s_wTc, 1)
            puts = [(wt[part][:], G[part][:]) for part in range(PARTS)] + [
                (wc[:], FB[:]), (wg[:], T[:]), (wmax_all[:], G[0][:]),
                (wd[:].rearrange("p c d -> p (c d)"), G[1][:]),
                (feat[:].rearrange("p c v -> p (c v)"), G[2][:, 0:CHUNKS * V_COLS])]
            for n, (to, of) in enumerate(puts):
                act.wait_ge(s_put, n + 1)
                if n == 6:
                    act.wait_ge(s_put, 8)
                act.activation(to, of, ACT.Copy).then_inc(s_putc, 1)

            def split_hi(at, layer):
                pe_event = 6 * at.b + (2, 4)[layer]
                act.wait_ge(s_p1, pe_event)
                act.activation(yp[0][:].rearrange("p j d -> p (j d)"), P1[:], ACT.Copy).then_inc(s_yhi, 1)

            def split_mid(at, layer):
                act.wait_ge(s_yrest, 2 * at.b + layer + 1)
                act.activation(yp[1][:].rearrange("p j d -> p (j d)"), y_rest[:], ACT.Copy).then_inc(s_ymid, 1)

            def elu(at, layer):
                act.wait_ge(s_v, 2 * at.b + layer + 1)
                wait(act, s_h, 2 * at.b + layer)
                act.activation(ev[:], v[:], ACT.Exp, bias=bias[layer][:]).then_inc(s_eluact, 1)
                act.activation(rv[:], v[:], ACT.Relu, bias=bias[layer][:]).then_inc(s_eluact, 1)

            def copy_xT(at):
                act.wait_ge(s_p1, 6 * at.b + 1)
                act.activation(xT[:], P1[:], ACT.Copy).then_inc(s_xT, 1)

            def copy_hots(at, j):
                tile = at.b * TILES + j
                for group in range(2):
                    act.wait_ge(s_H, 2 * tile + group + 1)
                    wait(act, s_gath, (tile - 1) * TOP)
                    act.activation(hotT[j % 2][:, 8 * group:8 * group + 8, :].rearrange("p k n -> p (k n)"), H[:],
                                   ACT.Copy).then_inc(s_hotT, 1)

            def copy_t(at, j):
                event = at.b * T_EVENTS + (0, 2, 3, 4)[j]
                act.wait_ge(s_T, event + 1)
                act.activation(tT[at.parity][:, :, j * P:(j + 1) * P], T[:].rearrange("p (c n) -> p c n", c=CHUNKS),
                               ACT.Copy).then_inc(s_Tc, 1)

            def copy_z(at):
                act.wait_ge(s_T, at.b * T_EVENTS + 2)
                wait(act, s_F, 9 * (at.b - 1) + 8)
                act.activation(zT[:], T[:], ACT.Copy).then_inc(s_Tc, 1)

            def gelu_tanh(at, c):
                act.wait_ge(s_F, 9 * at.b + 2 * c + 1)
                wait(act, s_fused, 4 * (at.b - 1) + c + 1)
                act.activation(cl[c][:], FB[:], ACT.Gelu, bias=feat[:, c, V_BC:V_BC + 1]).then_inc(s_Fa, 1)
                act.wait_ge(s_F, 9 * at.b + 2 * c + 2)
                act.activation(gt[c][:], FB[:], ACT.Tanh, bias=feat[:, c, V_BG:V_BG + 1], scale=0.5)\
                    .then_inc(s_Fa, 1)

            def lines(at, c):
                if c == 0:
                    act.wait_ge(s_Tc, T_EVENTS * at.b + T_EVENTS)
                n = 0
                for slot, func in LINE_ORDER[:DRAWN[c]]:
                    wait(act, s_pwl, ALL_STEPS * at.b + LINE_FREE[c][n])
                    act.activation(line[(c % 2) * 4 + n if c < 3 else n][:], tT[at.parity][:, c, :], ACT.Identity,
                                   bias=feat[:, c, V_SO + 2 * slot + func:V_SO + 2 * slot + func + 1],
                                   scale=feat[:, c, V_SS + 2 * slot + func:V_SS + 2 * slot + func + 1])\
                        .then_inc(s_line, 1)
                    n += 1

            LINE_ORDER = [(0, 0), (1, 0), (0, 1), (1, 1)] + [(m, f) for m in range(2, SLOTS) for f in range(2)]
            LINE_FREE = [[-5, -5, -4, -4], [-2, -1, 0, 0], [1, 1, 2, 2], [5, 5, 6, 6, 3, 3, 4, 4]]

            def tick(at, finish, gnn):
                before, after = at.plus(-1), at.plus(1)
                if finish:
                    copy_t(before, TILES - 1)
                    gelu_tanh(before, 0)
                    gelu_tanh(before, 1)
                if gnn:
                    copy_xT(after)
                if finish:
                    lines(before, 0)
                    gelu_tanh(before, 2)
                    gelu_tanh(before, 3)
                copy_hots(at, 1)
                if gnn:
                    split_hi(after, 0)
                copy_t(at, 0)
                if gnn:
                    split_mid(after, 0)
                if finish:
                    lines(before, 1)
                if gnn:
                    elu(after, 0)
                if finish:
                    lines(before, 2)
                copy_z(at)
                copy_hots(at, 2)
                if gnn:
                    split_hi(after, 1)
                copy_t(at, 1)
                if gnn:
                    split_mid(after, 1)
                if finish:
                    lines(before, 3)
                if gnn:
                    elu(after, 1)
                copy_hots(at, 3)
                copy_t(at, 2)
                if gnn:
                    copy_hots(after, 0)

            first = fixed(0)
            copy_xT(first)
            split_hi(first, 0)
            split_mid(first, 0)
            elu(first, 0)
            split_hi(first, 1)
            split_mid(first, 1)
            elu(first, 1)
            copy_hots(first, 0)
            act.wait_ge(s_over, 1)
            act.activation(over_all[:], T[:, 0:1], ACT.Copy).then_inc(s_over, 1)
            tick(first, False, True)
            tick(fixed(1), True, True)
            with act.Fori(0, 5) as i:
                tick(At(i * 2 + 2, 0, i + 1), True, True)
                tick(At(i * 2 + 3, 1, i + 1), True, True)
            tick(fixed(12), True, True)
            tick(fixed(13), True, True)
            tick(fixed(14), True, True)
            tick(fixed(15), True, False)
            copy_t(fixed(15), TILES - 1)
            for c in range(CHUNKS):
                gelu_tanh(fixed(15), c)
                lines(fixed(15), c)

            act.wait_ge(q_n, 1)
            tiles = act.value_load(n_tiles_m[0:1, 0:1], min_val=1, max_val=NCOLS)
            with act.Fori(0, tiles) as g:
                act.wait_ge(q_zTp, g + 1)
                act.activation(g_zT[:], T[:, 0:P], ACT.Copy).then_inc(q_zT, 1)
                act.wait_ge(q_tTp, g + 1)
                act.activation(line[0][:], T[:], ACT.Copy).then_inc(q_tT, 1)
                act.wait_ge(q_F, g * 2 + 1)
                for c in range(CHUNKS):
                    last = act.activation(g_cl[:, c, :], FB[:, c * P:(c + 1) * P], ACT.Gelu,
                                          bias=feat[:, c, V_BC:V_BC + 1])
                last.then_inc(q_Fa, 1)
                act.wait_ge(q_F, g * 2 + 2)
                for c in range(CHUNKS):
                    last = act.activation(g_gt[:, c, :], FB[:, c * P:(c + 1) * P], ACT.Tanh,
                                          bias=feat[:, c, V_BG:V_BG + 1], scale=0.5)
                last.then_inc(q_Fa, 1)

        @block.vector
        def _(dve):
            steps = [0]

            def chain(instruction):
                steps[0] += 1
                instruction.then_inc(s_setup_dve, 1)
                dve.wait_ge(s_setup_dve, steps[0])

            def meanvar(at, rows, s_st, s_mv, mv):
                for j in range(TILES):
                    last = dve.bn_stats(st[:, j, :], rows[:, j, :])
                last.then_inc(s_st, 1)
                wait_apart(dve, s_st, at.b + 1, s_wload)
                for j in range(TILES):
                    last = dve.bn_aggr(mv[:, j, :], st[:, j, :])
                last.then_inc(s_mv, 1)

            def normalise(rows_out, rows, mv, rs, s_done):
                for j in range(TILES):
                    last = dve.tensor_scalar(rows_out[:, j, :], rows[:, j, :], mv[:, j, 0:1], rs[:, j:j + 1],
                                             ALU.subtract, ALU.mult)
                last.then_inc(s_done, 1)

            def ln1_stats(at):
                dve.wait_ge(s_xin[at.parity], 16 * (at.half + 1))
                meanvar(at, xs[at.parity], s_ln1_st, s_ln1_mv, mv1)

            def ln1_apply(at):
                dve.wait_ge(s_ln1_rs, 2 * at.b + 2)
                wait(dve, s_p1, 6 * (at.b - 1) + 1)
                normalise(xn, xs[at.parity], mv1, rs1, s_xn)

            def split_rest(at, layer):
                dve.wait_ge(s_yhi, 2 * at.b + layer + 1)
                dve.tensor_tensor(y_rest[:], P1[:], yp[0][:].rearrange("p j d -> p (j d)"), ALU.subtract)\
                    .then_inc(s_yrest, 1)

            def split_lo(at, layer):
                dve.wait_ge(s_ymid, 2 * at.b + layer + 1)
                dve.tensor_tensor(yp[2][:].rearrange("p j d -> p (j d)"), y_rest[:],
                                  yp[1][:].rearrange("p j d -> p (j d)"), ALU.subtract).then_inc(s_ylo, 1)

            def degree(at):
                dve.wait_ge(s_p2, 3 * at.b + 1)
                dve.tensor_scalar(deg[:], P2[:], 1.0, None, ALU.max).then_inc(s_deg, 1)
                dve.wait_ge(s_deg, 2 * at.b + 1)
                dve.reciprocal(rdeg[:], deg[:]).then_inc(s_deg, 1)

            def mix(at, layer):
                dve.wait_ge(s_p1, 6 * at.b + (3, 5)[layer])
                dve.wait_ge(s_deg, 2 * at.b + 2)
                dve.tensor_tensor(u[:], P1[:], rdeg[:], ALU.mult).then_inc(s_u, 1)
                dve.wait_ge(s_u, 2 * at.b + layer + 1)
                dve.wait_ge(s_p2, 3 * at.b + layer + 2)
                wait(dve, s_eluact, 4 * at.b + 2 * layer)
                dve.tensor_tensor(v[:], u[:], P2[:], ALU.add).then_inc(s_v, 1)

            def residual(at):
                dve.wait_ge(s_p1, 6 * at.b + 6)
                wait(dve, s_x2d, 16 * (at.b - 1))
                wait(dve, s_keep, at.b - 1)
                dve.tensor_tensor(x2[at.parity][:].rearrange("p j d -> p (j d)"), P1[:],
                                  xs[at.parity][:].rearrange("p j d -> p (j d)"), ALU.add).then_inc(s_x2, 1)
                dve.wait_ge(s_x2, at.b + 1)
                meanvar(at, x2[at.parity], s_ln2_st, s_ln2_mv, mv2)

            def ln2_apply(at):
                dve.wait_ge(s_ln2_rs, 2 * at.b + 2)
                wait(dve, s_T, T_EVENTS * (at.b - 1) + 2)
                normalise(z, x2[at.parity], mv2, rs2, s_z)

            def find_top(at, j):
                tile = at.b * TILES + j
                q = j % 2
                if j == 0:
                    dve.wait_ge(s_z, at.b + 1)
                wait_apart(dve, s_hot, 2 * (tile - 1), s_wload)
                dve.max(top[q][:, 0:8], z[:, j, :]).then_inc(s_top, 1)
                wait_apart(dve, s_top, 5 * tile + 1, s_wload)
                dve.match_replace(z_left[:], top[q][:, 0:8], z[:, j, :], LOWEST).then_inc(s_top, 1)
                dve.max_index(top_at[q][:, 0:8], top[q][:, 0:8], z[:, j, :]).then_inc(s_top, 1)
                wait_apart(dve, s_top, 5 * tile + 2, s_wload)
                dve.max(top[q][:, 8:16], z_left[:]).then_inc(s_top, 1)
                wait_apart(dve, s_top, 5 * tile + 4, s_wload)
                dve.max_index(top_at[q][:, 8:16], top[q][:, 8:16], z_left[:]).then_inc(s_top, 1)

            def round_(at, j, k):
                i = j * TOP + k
                dve.wait_ge(s_gath, at.b * ROUNDS + i + 1)
                if k == 0:
                    wait(dve, s_T, at.b * T_EVENTS + (-1, 0, 1, 3)[j])
                    dve.tensor_scalar(acc[j % 2][:], G[i % 3][:], top[j % 2][:, 0:1], None, ALU.add)\
                        .then_inc(s_round, 1)
                else:
                    dve.wait_ge(s_round, at.b * ROUNDS + i)
                    dve.scalar_tensor_tensor(out=acc[j % 2][:], in0=G[i % 3][:], scalar=top[j % 2][:, k:k + 1],
                                             in1=acc[j % 2][:], op0=ALU.add, op1=ALU.max).then_inc(s_round, 1)

            def count_open(at, j):
                dve.wait_ge(s_round, at.b * ROUNDS + (j + 1) * TOP)
                wait(dve, s_flags, 4 * at.b)
                dve.scalar_tensor_tensor(out=beyond[:], in0=wmax_all[:], scalar=top[j % 2][:, TOP - 1:TOP],
                                         in1=acc[j % 2][:], op0=ALU.add, op1=ALU.is_gt,
                                         accum_out=open_n[:, j:j + 1]).then_inc(s_open, 1)

            def pwl(at, c, m):
                base = ALL_STEPS * at.b + sum(STEPS[:c])
                to = (cvx, ccv)[m % 2][c % 2]
                lines_due = 2 * m + 2 if m < 2 else m + 3
                first_line = 4 if c == 1 else 0
                dve.wait_ge(s_line, ALL_DRAWN * at.b + sum(DRAWN[:c]) + lines_due)
                if m < 2:
                    wait(dve, s_fused, 4 * at.b + c - 1)
                    dve.tensor_tensor(to[:], line[first_line + 2 * m][:], line[first_line + 2 * m + 1][:], ALU.max)\
                        .then_inc(s_pwl, 1)
                else:
                    dve.wait_ge(s_pwl, base + m - 1)
                    dve.tensor_tensor(to[:], to[:], line[m + 2][:], ALU.max).then_inc(s_pwl, 1)

            def output(at):
                dve.wait_ge(s_F, 9 * at.b + 9)
                dve.wait_ge(s_keep, at.b + 1)
                wait(dve, s_outd, 16 * at.b)
                dve.tensor_tensor(o_s[:].rearrange("p j d -> p (j d)"), FB[:],
                                  x2_before[:].rearrange("p j d -> p (j d)"), ALU.add).then_inc(s_out, 1)

            def tick(at, finish, gnn, ahead):
                before, after = at.plus(-1), at.plus(1)
                for j in range(TILES):
                    for k in range(TOP):
                        s, r = divmod(j * TOP + k, SLOT_ROUNDS)
                        if gnn and r == 0:
                            if s == 2:
                                degree(after)
                            if s == 3:
                                mix(after, 0)
                            if s == 5:
                                mix(after, 1)
                            if s == 6:
                                residual(after)
                        if finish and s == 7 and r == 1:
                            output(before)
                        round_(at, j, k)
                        if s % 2 == 0 and r == 0 and j < TILES - 1:
                            find_top(at, j + 1)
                        if finish and 1 <= s <= 4 and 2 <= r <= 7:
                            for m in range((r - 2) * STEPS[s - 1] // 6, (r - 1) * STEPS[s - 1] // 6):
                                pwl(before, s - 1, m)
                        if gnn and s in (2, 4) and r == 1:
                            split_rest(after, s // 2 - 1)
                        if gnn and s in (2, 4) and r == 3:
                            split_lo(after, s // 2 - 1)
                        if gnn and s == 6 and r == 4:
                            ln2_apply(after)
                        if gnn and s == 6 and r == 5:
                            find_top(after, 0)
                        if ahead and s == 7 and r == 3:
                            ln1_stats(at.plus(2))
                        if ahead and s == 7 and r == 6:
                            ln1_apply(at.plus(2))
                    count_open(at, j)

            dve.wait_ge(s_wload, LOADED)
            first = fixed(0)
            ln1_stats(first)
            ln1_apply(first)
            chain(dve.reduce_max(wmax[:], wt_f[:], AX_X))
            chain(dve.tensor_reduce(wmin[:], wt_f[:], AX_X, ALU.min))
            rest = wt_r[:].rearrange("p (c d) -> p c d", c=CHUNKS)
            chain(dve.tensor_copy(wt_fp[0][:], wt_f[:]))
            chain(dve.tensor_tensor(rest, wt_f[:], wt_fp[0][:], ALU.subtract))
            chain(dve.tensor_copy(wt_fp[1][:], rest))
            dve.tensor_tensor(wt_fp[2][:], rest, wt_fp[1][:], ALU.subtract).then_inc(s_wtf, 1)
            dve.wait_ge(s_share, 1)
            chain(dve.tensor_scalar(share[:, 0:CHUNKS], share[:, 0:CHUNKS], 0.5, 0.5, ALU.mult, ALU.add))
            chain(dve.tensor_scalar(share[:, CHUNKS:FC], share[:, 0:CHUNKS], 1.0, None, ALU.subtract))
            chain(dve.tensor_tensor(slope[:], slope[:], share[:][:, :, None].to_broadcast([P, FC, LINES]), ALU.mult))
            chain(dve.tensor_tensor(offs[:], offs[:], share[:][:, :, None].to_broadcast([P, FC, LINES]), ALU.mult))
            chain(dve.tensor_tensor(lo_hi[:, 0, :], wmin[:], bt_s[:], ALU.add))
            chain(dve.tensor_tensor(lo_hi[:, 1, :], wmax[:], bt_s[:], ALU.add))
            chain(dve.tensor_scalar(lo_hi[:, 0, :], lo_hi[:, 0, :], Z_LO, None, ALU.add))
            chain(dve.tensor_scalar(lo_hi[:, 1, :], lo_hi[:, 1, :], Z_HI, None, ALU.add))
            for e, end in ((0, end_a), (1, end_b)):
                for f in range(2):
                    part = slice(f * CHUNKS, (f + 1) * CHUNKS)
                    at_end = lo_hi[:, e, :][:, :, None].to_broadcast([P, CHUNKS, LINES])
                    chain(dve.tensor_tensor(end[:, part, :], slope[:, part, :], at_end, ALU.mult))
                chain(dve.tensor_tensor(end[:], end[:], offs[:], ALU.add))
            da, db, cross, low, one = [w[:].rearrange("p (f a b) -> p f a b", a=LINES, b=LINES) for w in work]
            for d, end in ((da, end_a), (db, end_b)):
                chain(dve.tensor_tensor(d, end[:][:, :, :, None].to_broadcast([P, FC, LINES, LINES]),
                                        end[:][:, :, None, :].to_broadcast([P, FC, LINES, LINES]), ALU.subtract))
            chain(dve.tensor_tensor(low, da, db, ALU.subtract))
            chain(dve.tensor_scalar(one, low, 0.0, None, ALU.is_equal))
            chain(dve.tensor_tensor(low, low, one, ALU.add))
            chain(dve.reciprocal(cross, low))
            chain(dve.tensor_tensor(cross, cross, da, ALU.mult))
            chain(dve.tensor_scalar(low, db, 0.0, 2.0, ALU.is_le, ALU.mult))
            chain(dve.tensor_tensor(low, low, cross, ALU.max))
            chain(dve.tensor_scalar(one, da, 0.0, None, ALU.is_lt))
            chain(dve.tensor_tensor(low, low, one, ALU.mult))
            chain(dve.reduce_max(need[:], low, AX_X))
            chain(dve.tensor_scalar(low, cross, -1.0, 1.0, ALU.mult, ALU.add))
            chain(dve.tensor_scalar(one, db, 0.0, None, ALU.is_lt))
            chain(dve.tensor_tensor(low, low, one, ALU.mult))
            chain(dve.tensor_scalar(one, da, 0.0, None, ALU.is_ge))
            chain(dve.tensor_tensor(low, low, one, ALU.mult))
            chain(dve.reduce_max(picked[:], low, AX_X))
            chain(dve.tensor_tensor(need[:], need[:], picked[:], ALU.add))
            chain(dve.tensor_scalar(need[:], need[:], 1.0 + MARGIN, None, ALU.is_le))
            chain(dve.memset(rank[:, :, 0:1], 0.0))
            for k in range(1, LINES):
                chain(dve.tensor_tensor(rank[:, :, k], rank[:, :, k - 1], need[:, :, k - 1], ALU.add))
            chain(dve.tensor_tensor(count[:], rank[:, :, LINES - 1], need[:, :, LINES - 1], ALU.add))
            chain(dve.tensor_tensor(key[:], count[:, 0:CHUNKS], count[:, CHUNKS:FC], ALU.max))
            chain(dve.tensor_tensor(key_sum[:], count[:, 0:CHUNKS], count[:, CHUNKS:FC], ALU.add))
            chain(dve.tensor_scalar(key[:], key[:], float(4 * LINES), None, ALU.mult))
            chain(dve.tensor_tensor(key[:], key[:], key_sum[:], ALU.add))
            chain(dve.tensor_scalar(key[:], key[:], float(FFN), None, ALU.mult))
            chain(dve.tensor_tensor(key[:], key[:], tok[:, 0:CHUNKS], ALU.add))
            dve.tensor_scalar(key_half[:], key[:], 0.5, None, ALU.subtract).then_inc(s_key, 1)
            for f in range(2):
                part = slice(f * CHUNKS, (f + 1) * CHUNKS)
                chain(dve.tensor_tensor(picked[:, part, :], slope[:, part, :],
                                        bt_s[:][:, :, None].to_broadcast([P, CHUNKS, LINES]), ALU.mult))
            chain(dve.tensor_tensor(offs[:], offs[:], picked[:], ALU.add))
            for m in range(SLOTS):
                chain(dve.tensor_scalar(pick[:], rank[:], float(m), None, ALU.is_equal))
                chain(dve.tensor_tensor(pick[:], pick[:], need[:], ALU.mult))
                for of, to in ((slope, slot_sl), (offs, slot_of)):
                    chain(dve.tensor_tensor(picked[:], pick[:], of[:], ALU.mult))
                    chain(dve.reduce_sum(to[:, m, :], picked[:], AX_X))
                    if m:
                        chain(dve.tensor_scalar(empty[:], count[:], float(m), None, ALU.is_le))
                        chain(dve.tensor_tensor(empty[:], empty[:], to[:, 0, :], ALU.mult))
                        chain(dve.tensor_tensor(to[:, m, :], to[:, m, :], empty[:], ALU.add))
            for f in range(2):
                part = slice(f * CHUNKS, (f + 1) * CHUNKS)
                chain(dve.tensor_copy(table[:, :, V_SL + f * LINES:V_SL + (f + 1) * LINES], slope[:, part, :]))
                chain(dve.tensor_copy(table[:, :, V_OF + f * LINES:V_OF + (f + 1) * LINES], offs[:, part, :]))
                chain(dve.tensor_copy(table[:, :, V_N + f], count[:, part]))
                for m in range(SLOTS):
                    chain(dve.tensor_copy(table[:, :, V_SS + 2 * m + f], slot_sl[:, m, part]))
                    chain(dve.tensor_copy(table[:, :, V_SO + 2 * m + f], slot_of[:, m, part]))
            chain(dve.tensor_copy(table[:, :, V_BC], bc_s[:]))
            chain(dve.tensor_scalar(table[:, :, V_BG], bg_s[:], 0.5, None, ALU.mult))
            dve.wait_ge(s_keyr, 1)
            dve.wait_ge(s_key, 1)
            for c in range(CHUNKS):
                chain(dve.tensor_scalar(wt_r[:], G[0][:], key_half[:, c:c + 1], None, ALU.is_lt))
                chain(dve.reduce_sum(place[:, c:c + 1], wt_r[:], AX_X))
            chain(dve.tensor_copy(wt_r[:], place_i[:]))
            for c in range(CHUNKS):
                chain(dve.tensor_scalar(perm[c][:], wt_r[:], place[:, c:c + 1], None, ALU.is_equal))
                last = dve.tensor_copy(permb[:, c, :], perm[c][:])
            last.then_inc(s_perm, 1)
            for m in range(CHUNKS):
                chain(dve.memset(planned[:, m, :], float(PLAN[m])))
            dve.wait_ge(s_putc, 8)
            chain(dve.tensor_tensor(over[:], feat[:, :, V_N:V_N + 2], planned[:], ALU.is_gt))
            chain(dve.reduce_max(over1[:], over[:].rearrange("p c f -> p (c f)"), AX_X))
            dve.tensor_copy(over1b[:], over1[:]).then_inc(s_setup_done, 1)

            split_rest(first, 0)
            split_lo(first, 0)
            degree(first)
            mix(first, 0)
            split_rest(first, 1)
            split_lo(first, 1)
            mix(first, 1)
            residual(first)
            ln2_apply(first)
            find_top(first, 0)
            ln1_stats(fixed(1))
            ln1_apply(fixed(1))
            tick(first, False, True, True)
            tick(fixed(1), True, True, True)
            with dve.Fori(0, 5) as i:
                tick(At(i * 2 + 2, 0, i + 1), True, True, True)
                tick(At(i * 2 + 3, 1, i + 1), True, True, True)
            tick(fixed(12), True, True, True)
            tick(fixed(13), True, True, True)
            tick(fixed(14), True, True, False)
            tick(fixed(15), True, False, False)
            for c in range(CHUNKS):
                for m in range(STEPS[c]):
                    pwl(fixed(15), c, m)
            output(fixed(15))

            gsteps = [0]

            def gchain(instruction):
                gsteps[0] += 1
                instruction.then_inc(q_dve, 1)
                dve.wait_ge(q_dve, gsteps[0])

            dve.wait_ge(s_flags, 4 * BATCHES)
            gchain(dve.tensor_scalar(ff[:], flags[:], 0.5, None, ALU.is_gt))
            dve.tensor_copy(fb[:], ff[:]).then_inc(q_fb, 1)
            dve.wait_ge(q_rank, 1)
            gchain(dve.tensor_copy(total[:], T[:, NCOLS:2 * NCOLS]))
            gchain(dve.tensor_copy(tot[0][:], T[:, NCOLS:2 * NCOLS]))
            n, q = 1, 0
            while n < NCOLS:
                gchain(dve.tensor_copy(tot[1 - q][:, 0:n], tot[q][:, 0:n]))
                gchain(dve.tensor_tensor(tot[1 - q][:, n:NCOLS], tot[q][:, n:NCOLS], tot[q][:, 0:NCOLS - n], ALU.add))
                n, q = 2 * n, 1 - q
            gchain(dve.tensor_tensor(rk[:], tot[q][:], total[:], ALU.subtract))
            gchain(dve.tensor_tensor(rk[:], rk[:], T[:, 0:NCOLS], ALU.add))
            gchain(dve.tensor_copy(rk_i[:], rk[:]))
            gchain(dve.tensor_scalar(rk_c_i[:], rk_i[:], 7, None, ALU.logical_shift_right))
            gchain(dve.tensor_scalar(rk_s_i[:], rk_i[:], P - 1, None, ALU.bitwise_and))
            gchain(dve.tensor_copy(rk_c[:], rk_c_i[:]))
            gchain(dve.tensor_copy(rk_s[:], rk_s_i[:]))
            gchain(dve.tensor_tensor(tok[:], tok[:], ff[:], ALU.mult))
            gchain(dve.tensor_scalar(n_tiles_f[:], tot[q][:, NCOLS - 1:NCOLS], float(P - 1), float(P), ALU.add, ALU.max))
            gchain(dve.tensor_copy(n_tiles_i[:], n_tiles_f[:]))
            dve.tensor_scalar(n_tiles_m[:], n_tiles_i[:], 7, None, ALU.logical_shift_right).then_inc(q_n, 1)
            with dve.Fori(0, NCOLS // 2) as i:
                for p in range(2):
                    col = i * 2 + p
                    dve.wait_ge(q_hotu, i * 2)
                    dve.tensor_scalar(at_slot[p][:], iota[:], rk_s[:, bass.ds(col, 1)], None, ALU.is_equal)
                    dve.tensor_scalar(at_tile[p][:], iota[:, 0:NCOLS], rk_c[:, bass.ds(col, 1)],
                                      tok[:, bass.ds(col, 1)], ALU.is_equal, ALU.mult).then_inc(q_hot, 1)
            dve.wait_ge(q_list, 1)
            gchain(dve.tensor_copy(got[:], FB[:, 0:NCOLS]))
            gchain(dve.tensor_scalar(hole[:], got[:], 0.5, float(4 * BATCHES * NODES), ALU.is_lt, ALU.mult))
            gchain(dve.tensor_scalar(src[:], got[:], -1.0, 0.0, ALU.add, ALU.max))
            dve.tensor_tensor(dst[:], src[:], hole[:], ALU.add).then_inc(q_n, 1)
            dve.wait_ge(q_n, 2)
            tiles = dve.value_load(n_tiles_m[0:1, 0:1], min_val=1, max_val=NCOLS)
            G_STEPS = 2 + 2 * CHUNKS * (2 * LINES - 1) + 4
            with dve.Fori(0, tiles) as g:
                gdone = [gsteps[0]]

                def link(instruction):
                    gdone[0] += 1
                    instruction.then_inc(q_dve, 1)
                    dve.wait_ge(q_dve, g * G_STEPS + gdone[0])

                dve.wait_ge(q_st, g * 16)
                link(dve.tensor_copy(src_i[:], src[:, bass.ds(g, 1)]))
                dve.tensor_copy(dst_i[:], dst[:, bass.ds(g, 1)]).then_inc(q_idx, 1)
                dve.wait_ge(q_gath, g * 16 + 16)
                dve.bn_stats(g_st[:], g_x[:]).then_inc(q_dve, 1)
                gdone[0] += 1
                wait_apart(dve, q_dve, g * G_STEPS + gdone[0], s_wload)
                dve.bn_aggr(g_mv[:], g_st[:]).then_inc(q_mv, 1)
                dve.wait_ge(q_mv, g + 1)
                wait_apart(dve, q_rs, g * 2 + 2, s_wload)
                dve.tensor_scalar(g_z[:], g_x[:], g_mv[:, 0:1], g_rs[:], ALU.subtract, ALU.mult).then_inc(q_z, 1)
                dve.memset(g_acc[:], LOWEST).then_inc(q_rd, 1)
                wait_apart(dve, q_z, g + 1, s_wload)
                with dve.Fori(0, D // 8) as h:
                    for k in range(8):
                        done = g * (D + 1) + h * 8 + k + 1
                        dve.wait_ge(q_wg, g * D + h * 8 + k + 1)
                        dve.wait_ge(q_rd, done)
                        dve.scalar_tensor_tensor(out=g_acc[:], in0=G[k % 2][:], scalar=g_z[:, bass.ds(h * 8 + k, 1)],
                                                 in1=g_acc[:], op0=ALU.add, op1=ALU.max).then_inc(q_rd, 1)
                dve.wait_ge(q_tT, g + 1)
                for f in range(2):
                    for c in range(CHUNKS):
                        k, o = V_SL + f * LINES, V_OF + f * LINES
                        link(dve.tensor_scalar(g_pw[f][:, c, :], g_tT[:, c, :], feat[:, c, k:k + 1], feat[:, c, o:o + 1],
                                               ALU.mult, ALU.add))
                        for m in range(1, LINES):
                            link(dve.tensor_scalar(g_line[m % 2][:], g_tT[:, c, :], feat[:, c, k + m:k + m + 1],
                                                   feat[:, c, o + m:o + m + 1], ALU.mult, ALU.add))
                            link(dve.tensor_tensor(g_pw[f][:, c, :], g_pw[f][:, c, :], g_line[m % 2][:], ALU.max))
                dve.wait_ge(q_Fa, g * 2 + 2)
                link(dve.tensor_scalar(g_gt, g_gt, 0.5, 0.5, ALU.mult, ALU.add))
                link(dve.tensor_tensor(g_pw[0], g_pw[0], g_pw[1], ALU.subtract))
                link(dve.tensor_tensor(g_pw[0], g_pw[0], g_cl, ALU.subtract))
                link(dve.tensor_tensor(g_pw[0], g_pw[0], g_gt, ALU.mult))
                dve.tensor_tensor(g_fu, g_pw[0], g_cl, ALU.add).then_inc(q_fu, 1)
                dve.wait_ge(q_o, g + 1)
                dve.tensor_tensor(g_o[:], FB[:, 0:D], g_x[:], ALU.add).then_inc(q_os, 1)
                assert gdone[0] - gsteps[0] == G_STEPS


_INS = ["x", "adj", "L0_gnn_w_rel1", "L0_gnn_w_root1", "L0_gnn_b1", "L0_gnn_w_rel2", "L0_gnn_w_root2", "L0_gnn_b2",
        "L0_ffn_Wt", "L0_ffn_bt", "L0_ffn_sl_cvx", "L0_ffn_of_cvx", "L0_ffn_sl_ccv", "L0_ffn_of_ccv",
        "L0_ffn_alpha", "L0_ffn_Wc", "L0_ffn_bc", "L0_ffn_Wg", "L0_ffn_bg", "L0_ffn_Wd", "L0_ffn_bd"]
_OUTS = [((BATCHES, NODES, D), "float32")]


def kernel(**inputs):
    import numpy as _np
    import concourse.bacc as _bacc
    from concourse import mybir as _mybir
    from concourse.bass_utils import run_bass_kernel_spmd as _run

    nc = _bacc.Bacc("TRN2", target_bir_lowering=False, num_devices=1)
    arrays, args = {}, []
    for name in _INS:
        a = _np.ascontiguousarray(inputs[name])
        arrays[f"in_{name}_dram"] = a
        args.append(nc.dram_tensor(f"in_{name}_dram", a.shape, _mybir.dt.from_np(a.dtype), kind="ExternalInput").ap())
    for i, (shape, dtype) in enumerate(_OUTS):
        dt = _mybir.dt.from_np(_np.dtype(dtype))
        args.append(nc.dram_tensor(f"out_{i}_dram", shape, dt, kind="ExternalOutput").ap())
    build(nc, *args)
    r = _run(nc, [arrays], core_ids=[0])
    got = tuple(r.results[0][f"out_{i}_dram"] for i in range(len(_OUTS)))
    return got[0]
```

```python
from contextlib import ExitStack

import concourse.bass as bass
from concourse import mybir

F32 = mybir.dt.float32
BF16 = mybir.dt.bfloat16
I32 = mybir.dt.int32
U32 = mybir.dt.uint32
ALU = mybir.AluOpType
ACT = mybir.ActivationFunctionType
AX_X = mybir.AxisListType.X

P = 128
BATCHES = 16
TILES = 4
NODES = TILES * P
D = 128
FFN = 512
CHUNKS = FFN // P
LINES = 8
TOP = 16
PLAN = (2, 2, 2, 4)
SLOTS = max(PLAN)
DRAWN = [2 * n for n in PLAN]
STEPS = [2 * (n - 1) for n in PLAN]
V_SL, V_OF = 0, 2 * LINES
V_SS = 4 * LINES
V_SO = V_SS + 2 * SLOTS
V_BC, V_BG = V_SO + 2 * SLOTS, V_SO + 2 * SLOTS + 1
V_N = V_BG + 1
V_COLS = V_N + 2
PARTS = 3
ROUNDS = TILES * TOP
EPS = 1e-5
MARGIN = 1e-4
Z_LO, Z_HI = 1.4, 4.8
LOWEST = -3.0e38
T_EVENTS = 5
NCOLS = BATCHES * TILES
GROUPS = 4
DEEP = 8 * GROUPS
PWL_STEPS = 2 * (LINES - 1)
OPEN_FROM = 0.5
RING = 16

PE_HOTS = {2: (1, 0), 7: (1, 1), 18: (2, 0), 23: (2, 1), 34: (3, 0), 39: (3, 1)}
PE_HOTS_AFTER = {55: 0, 60: 1}
PE_T = {20: 0, 36: 1, 52: 2}
PE_T_BEFORE = 4
PE_Z = 25
PE_FFN_IN = (5, 8, 11, 13, 15, 17, 19, 22)
PE_FFN_OUT = (46, 47, 48, 49)
PE_AGG1 = (0, 1, 2, 3)
PE_Y2, PE_ROOT2 = 12, 14
PE_AGG2 = (21, 22, 24, 26)
PE_BACK = 35
PE_X, PE_Y1, PE_DEGREE, PE_SPREAD, PE_ROOT1 = 42, 45, 50, 57, 61
DVE_TOPS = {2: 2, 19: 3}
DVE_TOPS_AFTER = {43: 0, 46: 1}
DVE_MIX1, DVE_ELU1, DVE_REST2, DVE_LO2, DVE_MIX2, DVE_ELU2 = 5, 9, 15, 18, 28, 31
DVE_RESIDUAL, DVE_LN2 = 37, 41
DVE_OUTPUT = 53
DVE_LN1_STATS, DVE_LN1, DVE_REST1, DVE_LO1, DVE_DEGREE = 16, 33, 49, 55, 54
DVE_PWL = ((12, 13), (16, 17), (21, 23), (25, 26, 27, 29, 30, 32))


class Pass:

    def __init__(self, sem, name):
        self.free = sem(name + "_buffers_free")
        self.idx = sem(name + "_indices")
        self.rows = sem(name + "_rows_in")
        self.st = sem(name + "_stats")
        self.mv = sem(name + "_meanvar")
        self.rs = sem(name + "_rstd")
        self.z = sem(name + "_z")
        self.zTp = sem(name + "_zT_psum")
        self.zT = sem(name + "_zT")
        self.top = sem(name + "_top_found")
        self.hot = sem(name + "_hot_made")
        self.H = sem(name + "_hot_bank_full")
        self.hotT = sem(name + "_hotT_copied")
        self.gath = sem(name + "_round_gathered")
        self.round = sem(name + "_round_done")
        self.merged = sem(name + "_even_odd_merged")
        self.open = sem(name + "_open_counted")
        self.tTp = sem(name + "_tT_psum")
        self.tT = sem(name + "_tT")
        self.F = sem(name + "_ffn_psum")
        self.Fa = sem(name + "_gelu_tanh")
        self.line = sem(name + "_convex_line")
        self.drawn = sem(name + "_concave_line")
        self.pwl = sem(name + "_pwl_step")
        self.mix = sem(name + "_gate_steps")
        self.fused = sem(name + "_fused")
        self.o = sem(name + "_out_psum")
        self.os = sem(name + "_out_summed")
        self.stored = sem(name + "_stored")


class At:

    def __init__(self, b, parity, half):
        self.b, self.parity, self.half = b, parity, half

    def plus(self, n):
        h = self.half + (self.parity + n) // 2
        return At(self.b + n, (self.parity + n) % 2, h)


def fixed(b):
    return At(b, b % 2, b // 2)


def wait(engine, semaphore, value):
    if isinstance(value, int) and value <= 0:
        return
    engine.wait_ge(semaphore, value)


def wait_apart(engine, semaphore, value, held):
    if isinstance(value, int):
        wait(engine, semaphore, value)
        return
    register = engine.to_reg(value)
    engine.wait_ge(held, 1)
    engine.wait_ge(semaphore, register)


def build(nc, x, adj, w_rel1, w_root1, b1, w_rel2, w_root2, b2, Wt, bt, sl_cvx, of_cvx,
          sl_ccv, of_ccv, alpha, Wc, bc, Wg, bg, Wd, bd, out):
    ctx = ExitStack()
    with ctx:
        def sb(name, shape, dt=F32):
            return ctx.enter_context(nc.sbuf_tensor(name, shape, dt))

        def bank(name, shape=(P, 512), dt=F32):
            return ctx.enter_context(nc.psum_tensor(name, list(shape), dt))

        def sem(name):
            return ctx.enter_context(nc.semaphore(name))

        ident = sb("ident", [P, P])
        identb = sb("identb", [P, P], BF16)
        onesb = sb("onesb", [P, P], BF16)
        below = sb("below", [P, P], BF16)
        zerof = sb("zerof", [P, P])
        row0 = sb("row0", [P, P])
        iota_i = sb("iota_i", [P, P], I32)
        iota = sb("iota", [P, P])
        minus_half = sb("minus_half", [P, TILES])
        unit = sb("unit", [P, 1])
        w_root = [sb("w_root1_s", [P, D]), sb("w_root2_s", [P, D])]
        w_rel = [sb("w_rel1_s", [P, D]), sb("w_rel2_s", [P, D])]
        bias = [sb("b1_s", [P, 1]), sb("b2_s", [P, 1])]
        wc = sb("wc", [P, FFN])
        wg = sb("wg", [P, FFN])
        wd = sb("wd", [P, CHUNKS, D])
        bc_s = sb("bc_s", [P, CHUNKS])
        bg_s = sb("bg_s", [P, CHUNKS])
        bd_s = sb("bd_s", [P, D])
        bt_s = sb("bt_s", [P, CHUNKS])
        al = sb("al", [P, CHUNKS])
        wt_f = sb("wt_f", [P, CHUNKS, D])
        wt_r = sb("wt_r", [P, FFN])
        wcT = sb("wcT", [P, CHUNKS, D])
        wgT = sb("wgT", [P, CHUNKS, D])
        wt = [sb(f"wt{p}", [P, FFN], BF16) for p in range(PARTS)]
        wmax = sb("wmax", [P, CHUNKS])
        wmin = sb("wmin", [P, CHUNKS])
        wmax_all = sb("wmax_all", [P, FFN])
        FC = 2 * CHUNKS
        table = sb("table", [P, CHUNKS, V_COLS])
        feat = sb("feat", [P, CHUNKS, V_COLS])
        slope = sb("slope", [P, FC, LINES])
        offs = sb("offs", [P, FC, LINES])
        share = sb("share", [P, FC])
        end_a = sb("end_a", [P, FC, LINES])
        end_b = sb("end_b", [P, FC, LINES])
        need = sb("need", [P, FC, LINES])
        rank = sb("rank", [P, FC, LINES])
        count = sb("count", [P, FC])
        pick = sb("pick", [P, FC, LINES])
        picked = sb("picked", [P, FC, LINES])
        empty = sb("empty", [P, FC])
        lo_hi = sb("lo_hi", [P, 2, CHUNKS])
        slot_sl = sb("slot_sl", [P, SLOTS, FC])
        slot_of = sb("slot_of", [P, SLOTS, FC])
        key = sb("key", [P, CHUNKS])
        key_half = sb("key_half", [P, CHUNKS])
        key_sum = sb("key_sum", [P, CHUNKS])
        place = sb("place", [P, CHUNKS])
        place_i = sb("place_i", [P, FFN], I32)
        wt_fp = [sb(f"wt_f{p}", [P, CHUNKS, D], BF16) for p in range(PARTS)]
        permb = sb("permb", [P, CHUNKS, FFN], BF16)
        planned = sb("planned", [P, CHUNKS, 2])
        over = sb("over", [P, CHUNKS, 2])
        over1 = sb("over1", [P, 1])
        over1b = sb("over1b", [P, 1], BF16)
        over_all = sb("over_all", [P, 1])

        xs = [sb(f"x{q}", [P, TILES, D]) for q in range(2)]
        adjs = [sb(f"adj{q}", [P, TILES, NODES], I32) for q in range(2)]
        mask = sb("mask", [P, TILES, NODES], BF16)
        st1 = sb("st1", [P, TILES, 6])
        st2 = sb("st2", [P, TILES, 6])
        mv1 = sb("mv1", [P, TILES, 2])
        ve1 = sb("ve1", [P, TILES])
        rs1 = sb("rs1", [P, TILES])
        mv2 = sb("mv2", [P, TILES, 2])
        ve2 = sb("ve2", [P, TILES])
        rs2 = sb("rs2", [P, TILES])
        xn = sb("xn", [P, TILES, D])
        xT = sb("xT", [P, NODES])
        hT = [sb(f"h{q}T", [P, NODES]) for q in range(2)]
        yp = [sb(f"y{p}", [P, TILES, D], BF16) for p in range(PARTS)]
        y_rest = sb("y_rest", [P, NODES])
        rdeg = sb("rdeg", [P, NODES])
        deg = sb("deg", [P, TILES])
        deg_inv = sb("deg_inv", [P, TILES])
        u = sb("u", [P, NODES])
        v = sb("v", [P, NODES])
        ev = sb("ev", [P, NODES])
        rv = sb("rv", [P, NODES])
        em = sb("em", [P, NODES])
        x2 = [sb(f"x2{q}", [P, TILES, D]) for q in range(2)]
        x2_before = sb("x2_before", [P, TILES, D])
        z = sb("z", [P, TILES, D])
        z_left = sb("z_left", [P, D])
        top = [sb(f"top{q}", [P, TOP]) for q in range(TILES)]
        top_at = [sb(f"top_at{q}", [P, TOP], U32) for q in range(TILES)]
        zmax = [sb(f"zmax{q}", [P, TILES]) for q in range(2)]
        hot = sb("hot", [P, TOP, P], BF16)
        hotT = [sb(f"hotT{q}", [P, TOP, P], BF16) for q in range(2)]
        acc = [[sb(f"acc{q}{r}", [P, FFN]) for r in range(2)] for q in range(2)]
        beyond = sb("beyond", [P, FFN], BF16)
        open_n = sb("open_n", [P, TILES])
        fl_a = sb("fl_a", [P, TILES])
        fl_b = sb("fl_b", [P, TILES])
        fl_c = sb("fl_c", [P, TILES])
        flags = sb("flags", [P, NCOLS])
        tT = [sb(f"tT{q}", [P, CHUNKS, NODES]) for q in range(2)]
        zT = sb("zT", [P, NODES])
        cl = [sb(f"cl{c}", [P, NODES]) for c in range(CHUNKS)]
        gt = [sb(f"gt{c}", [P, NODES]) for c in range(CHUNKS)]
        line = [sb(f"line{n}", [P, NODES]) for n in range(2 * SLOTS)]
        cvx = [sb(f"cvx{q}", [P, NODES]) for q in range(2)]
        ccv = [sb(f"ccv{q}", [P, NODES]) for q in range(2)]
        trop = sb("trop", [P, NODES])
        diff = sb("diff", [P, NODES])
        fused = [sb(f"fused{c}", [P, NODES]) for c in range(CHUNKS)]
        o_s = sb("o_s", [P, TILES, D])

        fb = sb("fb", [P, NCOLS], BF16)
        ff = sb("ff", [P, NCOLS])
        tot = [sb(f"tot{q}", [P, NCOLS]) for q in range(2)]
        total = sb("total", [P, NCOLS])
        rk = sb("rk", [P, NCOLS])
        rk_i = sb("rk_i", [P, NCOLS], I32)
        rk_c_i = sb("rk_c_i", [P, NCOLS], I32)
        rk_s_i = sb("rk_s_i", [P, NCOLS], I32)
        rk_c = sb("rk_c", [P, NCOLS])
        rk_s = sb("rk_s", [P, NCOLS])
        tok_i = sb("tok_i", [P, NCOLS], I32)
        tok = sb("tok", [P, NCOLS])
        n_tiles_f = sb("n_tiles_f", [P, 1])
        n_tiles_i = sb("n_tiles_i", [P, 1], I32)
        n_tiles_s = sb("n_tiles_s", [P, 1], I32)
        n_tiles_m = sb("n_tiles_m", [P, 1], I32)
        at_slot = tT[0][:].rearrange("p c (a b) -> p (c a) b", b=P)
        at_tile = tT[1][:].rearrange("p c (a b) -> p (c a) b", b=P)
        got = sb("got", [P, NCOLS])
        hole = sb("hole", [P, NCOLS])
        src = sb("src", [P, NCOLS])
        dst = sb("dst", [P, NCOLS])
        src_i = sb("src_i", [P, 1], U32)
        dst_i = sb("dst_i", [P, 1], U32)
        g_x = sb("g_x", [P, D])
        g_st = sb("g_st", [P, 6])
        g_mv = sb("g_mv", [P, 2])
        g_ve = sb("g_ve", [P, 1])
        g_rs = sb("g_rs", [P, 1])
        g_z = sb("g_z", [P, D])
        g_zT = sb("g_zT", [P, P])
        g_acc = acc[0]
        g_tT, g_cl, g_gt, g_fu = [w[:].rearrange("p (c n) -> p c n", c=CHUNKS) for w in (line[0], cl[0], gt[0], fused[0])]
        g_pw = [line[1 + q][:].rearrange("p (c n) -> p c n", c=CHUNKS) for q in range(2)]
        g_convex = [line[3 + q][:].rearrange("p (c n) -> p c n", c=CHUNKS) for q in range(4)]
        g_concave = [w[:].rearrange("p (c n) -> p c n", c=CHUNKS) for w in (line[7], cvx[0])]
        g_top = sb("g_top", [P, DEEP])
        g_at = sb("g_at", [P, DEEP], U32)
        g_left = [z_left, sb("g_left", [P, D])]
        g_open = sb("g_open", [P, 1])
        g_any = sb("g_any", [P, 1])
        g_anyb = sb("g_anyb", [P, 1], BF16)
        g_any_f = sb("g_any_f", [P, 1])
        g_any_i = sb("g_any_i", [P, 1], I32)
        g_mark = [sb(f"g_mark{q}", [P, 1]) for q in range(2)]
        g_o = sb("g_o", [P, D])

        x2_dram = nc.dram_tensor("x2_rows", [BATCHES * NODES, D], F32, kind="Internal").ap()

        G = [bank(f"gathered{q}") for q in range(3)]
        H = bank("hot_bank", (P, 1024), BF16)
        P1 = bank("gnn_bank1")
        P2 = bank("gnn_bank2")
        T = bank("transpose_bank")
        FB = bank("ffn_bank")

        s_const = sem("constants_made")
        s_wload = sem("weights_loaded")
        s_wtf = sem("wt_parts_made")
        s_wT = sem("wc_wg_transposed")
        s_wTc = sem("wc_wg_transposed_copied")
        s_key = sem("keys_made")
        s_keyr = sem("keys_spread")
        s_perm = sem("order_made")
        s_put = sem("put_in_order")
        s_putc = sem("put_in_order_copied")
        s_share = sem("tanh_alpha")
        s_setup_dve = sem("setup_dve")
        s_setup_done = sem("setup_done")
        s_over = sem("over_counted")
        s_xin = [sem(f"x_in{q}") for q in range(2)]
        s_adjin = [sem(f"adj_in{q}") for q in range(2)]
        s_mask = sem("mask_made")
        s_ln1_st = sem("ln1_stats")
        s_ln1_mv = sem("ln1_meanvar")
        s_ln1_rs = sem("ln1_rstd")
        s_xn = sem("xn_ready")
        s_p1 = sem("gnn_bank1_full")
        s_p2 = sem("gnn_bank2_full")
        s_xT = sem("xT_ready")
        s_yhi = sem("y_hi")
        s_yrest = sem("y_rest")
        s_ymid = sem("y_mid")
        s_ylo = sem("y_lo")
        s_deg = sem("degree")
        s_rdeg = sem("inverse_degree_copied")
        s_u = sem("u_ready")
        s_v = sem("v_ready")
        s_eluact = sem("elu_exp_relu")
        s_h = sem("h_ready")
        s_x2 = sem("x2_ready")
        s_ln2_st = sem("ln2_stats")
        s_ln2_mv = sem("ln2_meanvar")
        s_ln2_rs = sem("ln2_rstd")
        s_z = sem("z_ready")
        s_top = sem("top_found")
        s_zmax = sem("zmax_kept")
        s_hot = sem("hot_made")
        s_H = sem("hot_bank_full")
        s_hotT = sem("hotT_copied")
        s_gath = sem("round_gathered")
        s_round = sem("round_done")
        s_merged = sem("even_odd_merged")
        s_open = sem("open_counted")
        s_flags = sem("flags_ready")
        s_T = sem("transpose_bank_full")
        s_Tc = sem("transpose_bank_copied")
        s_F = sem("ffn_bank_full")
        s_Fa = sem("gelu_tanh_done")
        s_gate = sem("gate_ready")
        s_line = sem("line_ready")
        s_pwl = sem("pwl_step")
        s_trop = sem("trop_step")
        s_fused = sem("fused_ready")
        s_keep = sem("x2_kept")
        s_out = sem("out_summed")
        s_outd = sem("out_stored")
        s_x2d = sem("x2_stored")
        q_dve = sem("g_dve")
        q_rank = sem("g_flags_counted")
        q_fb = sem("g_flags_bf16")
        q_hot = sem("g_one_hots")
        q_hotu = sem("g_one_hots_used")
        q_list = sem("g_list")
        q_n = sem("g_tiles_known")
        q_anyb = sem("g_any_open_bf16")
        q_anyc = sem("g_any_open_counted")
        q_any = sem("g_any_open")
        deep, full = Pass(sem, "deep"), Pass(sem, "full")

        x_t = x.rearrange("b (j p) d -> b p j d", p=P)
        adj_t = adj.rearrange("b (j p) m -> b p j m", p=P)
        out_t = out.rearrange("b (j p) d -> b p j d", p=P)
        out_rows = out.rearrange("b n d -> (b n) d")
        x2_t = x2_dram.rearrange("(b j p) d -> b p j d", j=TILES, p=P)
        weight_loads = [
            (w_root[0][:], w_root1), (w_root[1][:], w_root2), (w_rel[0][:], w_rel1[1]), (w_rel[1][:], w_rel2[1]),
            (bias[0][:], b1.rearrange("(p o) -> p o", o=1)), (bias[1][:], b2.rearrange("(p o) -> p o", o=1)),
            (wt_f[:], Wt.rearrange("(c p) d -> p c d", p=P)),
            (wc[:], Wc), (wg[:], Wg), (wd[:], Wd.rearrange("(c p) d -> p c d", p=P)),
            (bc_s[:], bc.rearrange("(c p) -> p c", p=P)), (bg_s[:], bg.rearrange("(c p) -> p c", p=P)),
            (bt_s[:], bt.rearrange("(c p) -> p c", p=P)), (al[:], alpha.rearrange("(c p) -> p c", p=P)),
            (bd_s[0:1, :], bd.rearrange("(o d) -> o d", o=1)),
            (slope[:, 0:CHUNKS, :], sl_cvx.rearrange("(c p) q -> p c q", p=P)),
            (slope[:, CHUNKS:FC, :], sl_ccv.rearrange("(c p) q -> p c q", p=P)),
            (offs[:, 0:CHUNKS, :], of_cvx.rearrange("(c p) q -> p c q", p=P)),
            (offs[:, CHUNKS:FC, :], of_ccv.rearrange("(c p) q -> p c q", p=P)),
        ]
        LOADED = 16 * len(weight_loads)
        N_CONST = 13
        ALL_STEPS, ALL_DRAWN = sum(STEPS), sum(DRAWN)
        perm = fused
        work = [u, v, ev, rv, em]

        def bank_rounds_before(i, at):
            if i >= 3:
                return at.b * ROUNDS + i - 2
            return (at.b - 1) * ROUNDS + {0: 64, 1: 62, 2: 63}[i]

        block = ctx.enter_context(nc.Block())

        @block.sync
        def _(sp):
            def load_x(at):
                wait(sp, s_x2, at.b - 1)
                sp.dma_start(xs[at.parity][:], x_t[at.b]).then_inc(s_xin[at.parity], 16)

            def load_adj(at):
                wait(sp, s_mask, at.b - 1)
                sp.dma_start(adjs[at.parity][:], adj_t[at.b]).then_inc(s_adjin[at.parity], 16)

            def store_x2(at):
                sp.wait_ge(s_x2, at.b + 1)
                sp.dma_start(x2_t[at.b], x2[at.parity][:]).then_inc(s_x2d, 16)

            def store_out(at):
                sp.wait_ge(s_out, at.b + 1)
                sp.dma_start(out_t[at.b], o_s[:]).then_inc(s_outd, 16)

            def tick(at, finish, gnn, load):
                if load:
                    load_adj(at.plus(3))
                if gnn:
                    store_x2(at.plus(1))
                if load:
                    load_x(at.plus(3))
                if finish:
                    store_out(at.plus(-1))

            load_x(fixed(0))
            load_adj(fixed(0))
            sp.wait_ge(s_const, N_CONST)
            for to, of in weight_loads:
                sp.dma_start(to, of, allow_slow_non_contiguous=True).then_inc(s_wload, 16)
            load_x(fixed(1))
            load_adj(fixed(1))
            load_adj(fixed(2))
            store_x2(fixed(0))
            load_x(fixed(2))
            tick(fixed(0), False, True, True)
            tick(fixed(1), True, True, True)
            with sp.Fori(0, 5) as i:
                tick(At(i * 2 + 2, 0, i + 1), True, True, True)
                tick(At(i * 2 + 3, 1, i + 1), True, True, True)
            tick(fixed(12), True, True, True)
            tick(fixed(13), True, True, False)
            tick(fixed(14), True, True, False)
            tick(fixed(15), True, False, False)
            store_out(fixed(15))
            sp.wait_ge(s_outd, 16 * BATCHES)
            sp.wait_ge(s_x2d, 16 * BATCHES)

        @block.gpsimd
        def _(pool):
            pool.memset(ident[:], 0.0).then_inc(s_const, 1)
            pool.memset(identb[:], 0.0).then_inc(s_const, 1)
            pool.memset(onesb[:], 1.0).then_inc(s_const, 1)
            pool.memset(below[:], 1.0).then_inc(s_const, 1)
            pool.memset(row0[:], 1.0).then_inc(s_const, 1)
            pool.memset(zerof[:], 0.0).then_inc(s_const, 1)
            pool.memset(bd_s[:], 0.0).then_inc(s_const, 1)
            pool.memset(minus_half[:], -0.5).then_inc(s_const, 1)
            pool.memset(unit[:], 1.0).then_inc(s_const, 1)
            pool.wait_ge(s_const, 9)
            pool.affine_select(out=ident[:], in_=ident[:], compare_op=ALU.not_equal, fill=1.0, base=0,
                               pattern=[[-1, P]], channel_multiplier=1).then_inc(s_const, 1)
            pool.affine_select(out=identb[:], in_=identb[:], compare_op=ALU.not_equal, fill=1.0, base=0,
                               pattern=[[-1, P]], channel_multiplier=1).then_inc(s_const, 1)
            pool.affine_select(out=below[:], in_=below[:], compare_op=ALU.is_gt, fill=0.0, base=0,
                               pattern=[[1, P]], channel_multiplier=-1).then_inc(s_const, 1)
            pool.affine_select(out=row0[:], in_=row0[:], compare_op=ALU.is_ge, fill=0.0, base=0,
                               pattern=[[0, P]], channel_multiplier=-1).then_inc(s_const, 1)
            pool.iota(iota_i[:], pattern=[[1, P]], base=0, channel_multiplier=0).then_inc(s_const, 1)
            pool.iota(place_i[:], pattern=[[1, FFN]], base=0, channel_multiplier=0).then_inc(s_const, 1)
            pool.iota(tok_i[:], pattern=[[P, NCOLS]], base=1, channel_multiplier=1).then_inc(s_const, 1)
            pool.wait_ge(s_const, N_CONST + 3)
            pool.tensor_copy(iota[:], iota_i[:]).then_inc(s_const, 1)
            pool.tensor_copy(tok[:], tok_i[:]).then_inc(s_const, 1)
            pool.wait_ge(s_const, N_CONST + 5)

            def make_mask(at):
                pool.wait_ge(s_adjin[at.parity], 16 * (at.half + 1))
                wait_apart(pool, s_p1, 6 * (at.b - 1) + 5, s_const)
                pool.tensor_scalar(mask[:], adjs[at.parity][:], 1, None, ALU.is_equal).then_inc(s_mask, 1)

            def rstd(at, meanvar, s_mv, ve, rs, s_rs):
                wait_apart(pool, s_mv, at.b + 1, s_const)
                pool.tensor_scalar(ve[:], meanvar[:, :, 1], EPS, None, ALU.add).then_inc(s_rs, 1)
                pool.wait_ge(s_rs, 2 * at.b + 1)
                pool.tensor_tensor(rs[:], ve[:], minus_half[:], ALU.pow).then_inc(s_rs, 1)

            def one_hots(at, j):
                tile = at.b * TILES + j
                for group in range(2):
                    wait_apart(pool, s_top, 5 * tile + (3 if group == 0 else 5), s_const)
                    if group == 0:
                        pool.tensor_copy(zmax[at.parity][:, j:j + 1], top[j][:, 0:1]).then_inc(s_zmax, 1)
                    wait_apart(pool, s_H, 2 * (tile - 1) + group + 1, s_const)
                    for k in range(8 * group, 8 * group + 8):
                        last = pool.tensor_scalar(hot[:, k, :], iota[:], top_at[j][:, k:k + 1], None, ALU.is_equal)
                    last.then_inc(s_hot, 1)

            def fuse(at, c):
                wait_apart(pool, s_Fa, 8 * at.b + 2 * c + 2, s_const)
                pool.tensor_scalar(gt[c][:], gt[c][:], 0.5, 0.5, ALU.mult, ALU.add).then_inc(s_gate, 1)
                pool.wait_ge(s_pwl, ALL_STEPS * at.b + sum(STEPS[:c + 1]))
                wait(pool, s_fused, 4 * at.b + c)
                pool.tensor_tensor(trop[:], cvx[c % 2][:], ccv[c % 2][:], ALU.subtract).then_inc(s_trop, 1)
                pool.wait_ge(s_trop, 12 * at.b + 3 * c + 1)
                pool.tensor_tensor(diff[:], trop[:], cl[c][:], ALU.subtract).then_inc(s_trop, 1)
                pool.wait_ge(s_trop, 12 * at.b + 3 * c + 2)
                pool.wait_ge(s_gate, 4 * at.b + c + 1)
                pool.tensor_tensor(trop[:], diff[:], gt[c][:], ALU.mult).then_inc(s_trop, 1)
                pool.wait_ge(s_trop, 12 * at.b + 3 * c + 3)
                wait(pool, s_F, 9 * at.b)
                pool.tensor_tensor(fused[c][:], trop[:], cl[c][:], ALU.add).then_inc(s_fused, 1)

            def note(at):
                wait_apart(pool, s_zmax, 4 * at.b + 4, s_const)
                pool.tensor_scalar(fl_a[:], zmax[at.parity][:], Z_LO, over_all[:], ALU.is_lt, ALU.add).then_inc(s_flags, 1)
                pool.tensor_scalar(fl_b[:], zmax[at.parity][:], Z_HI, None, ALU.is_gt).then_inc(s_flags, 1)
                pool.wait_ge(s_flags, 4 * at.b + 2)
                pool.tensor_tensor(fl_c[:], fl_a[:], fl_b[:], ALU.add).then_inc(s_flags, 1)
                pool.wait_ge(s_flags, 4 * at.b + 3)
                pool.wait_ge(s_open, 4 * at.b + 4)
                pool.tensor_tensor(flags[:, bass.ds(at.b * TILES, TILES)], fl_c[:], open_n[:], ALU.add)\
                    .then_inc(s_flags, 1)

            def tick(at, finish, gnn, ahead):
                before, after = at.plus(-1), at.plus(1)
                if finish:
                    note(before)
                one_hots(at, 2)
                if finish:
                    fuse(before, 0)
                    fuse(before, 1)
                if ahead:
                    rstd(at.plus(2), mv1, s_ln1_mv, ve1, rs1, s_ln1_rs)
                one_hots(at, 3)
                if finish:
                    fuse(before, 2)
                    fuse(before, 3)
                if gnn:
                    rstd(after, mv2, s_ln2_mv, ve2, rs2, s_ln2_rs)
                if ahead:
                    make_mask(at.plus(2))
                if gnn:
                    one_hots(after, 0)
                    one_hots(after, 1)

            make_mask(fixed(0))
            rstd(fixed(0), mv1, s_ln1_mv, ve1, rs1, s_ln1_rs)
            make_mask(fixed(1))
            rstd(fixed(0), mv2, s_ln2_mv, ve2, rs2, s_ln2_rs)
            rstd(fixed(1), mv1, s_ln1_mv, ve1, rs1, s_ln1_rs)
            one_hots(fixed(0), 0)
            one_hots(fixed(0), 1)
            pool.wait_ge(s_over, 2)
            tick(fixed(0), False, True, True)
            tick(fixed(1), True, True, True)
            with pool.Fori(0, 5) as i:
                tick(At(i * 2 + 2, 0, i + 1), True, True, True)
                tick(At(i * 2 + 3, 1, i + 1), True, True, True)
            tick(fixed(12), True, True, True)
            tick(fixed(13), True, True, True)
            tick(fixed(14), True, True, False)
            tick(fixed(15), True, False, False)
            note(fixed(15))
            for c in range(CHUNKS):
                fuse(fixed(15), c)

            pool.wait_ge(q_n, 1)
            tiles = pool.value_load(n_tiles_m[0:1, 0:1], min_val=1, max_val=NCOLS)
            pool.wait_ge(s_x2d, 16 * BATCHES)
            pool.wait_ge(s_outd, 16 * BATCHES)

            def general(g, s, mark):
                wait_apart(pool, s.idx, g * 2 + 2, s_const)
                pool.indirect_dma_start(out=g_x[:], out_offset=None, in_=x2_dram,
                                        in_offset=bass.IndirectOffsetOnAxis(ap=src_i[:], axis=0))\
                    .then_inc(s.rows, 16)
                wait_apart(pool, s.mv, g + 1, s_const)
                pool.tensor_scalar(g_ve[:], g_mv[:, 1:2], EPS, None, ALU.add).then_inc(s.rs, 1)
                pool.wait_ge(s.rs, g * 2 + 1)
                pool.tensor_tensor(g_rs[:], g_ve[:], minus_half[:, 0:1], ALU.pow).then_inc(s.rs, 1)
                wait_apart(pool, s.os, g + 1, s_const)
                pool.indirect_dma_start(out=out_rows, in_=g_o[:], in_offset=None,
                                        out_offset=bass.IndirectOffsetOnAxis(ap=dst_i[:], axis=0),
                                        bounds_check=BATCHES * NODES - 1, oob_is_err=False)\
                    .then_inc(s.stored, 16)
                wait_apart(pool, s.stored, g * 16 + 16, s_const)
                pool.memset(mark[:], 0.0).then_inc(s.free, 1)

            pool.memset(g_mark[0][:], 0.0).then_inc(deep.free, 1)
            with pool.Fori(0, tiles) as g:
                general(g, deep, g_mark[0])
            pool.wait_ge(q_any, 1)
            some = pool.value_load(g_any_i[0:1, 0:1], min_val=0, max_val=1)
            with pool.If(some > 0):
                pool.memset(g_mark[1][:], 0.0).then_inc(full.free, 1)
                with pool.Fori(0, tiles) as g:
                    general(g, full, g_mark[1])

        @block.tensor
        def _(pe):
            pe.wait_ge(s_wload, LOADED)
            pe.wait_ge(s_const, N_CONST + 5)
            for to, w in ((FB, wc), (T, wg)):
                for c in range(CHUNKS):
                    last = pe.transpose(to[:, c * P:(c + 1) * P], w[:, c * P:(c + 1) * P], ident[:])
                last.then_inc(s_wT, 1)
            pe.wait_ge(s_key, 1)
            for c in range(CHUNKS):
                last = pe.matmul(G[0][:, c * P:(c + 1) * P], key[:, c:c + 1].to_broadcast([P, P]), ident[:],
                                 start=True, stop=True)
            last.then_inc(s_keyr, 1)
            pe.wait_ge(s_wtf, 1)
            pe.wait_ge(s_perm, 1)
            pe.wait_ge(s_wTc, 2)
            for part in range(PARTS):
                for c in range(CHUNKS):
                    last = pe.matmul(G[part][:], wt_fp[part][:, c, :], permb[:, c, :],
                                     start=(c == 0), stop=(c == CHUNKS - 1))
                last.then_inc(s_put, 1)
            for to, w in ((FB, wcT), (T, wgT)):
                for c in range(CHUNKS):
                    last = pe.matmul(to[:], w[:, c, :], perm[c][:], start=(c == 0), stop=(c == CHUNKS - 1))
                last.then_inc(s_put, 1)
            pe.wait_ge(s_putc, 1)
            for c in range(CHUNKS):
                last = pe.matmul(G[0][:], wmax[:, c:c + 1].to_broadcast([P, P]), perm[c][:],
                                 start=(c == 0), stop=(c == CHUNKS - 1))
            last.then_inc(s_put, 1)
            pe.wait_ge(s_putc, 2)
            for m in range(CHUNKS):
                for c in range(CHUNKS):
                    last = pe.matmul(G[1][:, m * P:(m + 1) * P], perm[c][:, m * P:(m + 1) * P], wd[:, c, :],
                                     start=(c == 0), stop=(c == CHUNKS - 1))
            last.then_inc(s_put, 1)
            pe.wait_ge(s_putc, 3)
            for m in range(CHUNKS):
                for c in range(CHUNKS):
                    last = pe.matmul(G[2][:, m * V_COLS:(m + 1) * V_COLS], perm[c][:, m * P:(m + 1) * P],
                                     table[:, c, :], start=(c == 0), stop=(c == CHUNKS - 1))
            last.then_inc(s_put, 1)

            def gnn_x_transposed(at):
                pe.wait_ge(s_xn, at.b + 1)
                wait(pe, s_x2, at.b)
                for j in range(TILES):
                    last = pe.transpose(P1[:, j * P:(j + 1) * P], xn[:, j, :], ident[:])
                last.then_inc(s_p1, 1)

            def gnn_y(at, layer):
                h = (xT, hT[0])[layer]
                if layer == 0:
                    pe.wait_ge(s_xT, at.b + 1)
                else:
                    pe.wait_ge(s_h, 2 * at.b + 1)
                    pe.wait_ge(s_u, 2 * at.b + 1)
                for j in range(TILES):
                    last = pe.matmul(P1[:, j * P:(j + 1) * P], h[:, j * P:(j + 1) * P], w_rel[layer][:],
                                     start=True, stop=True)
                last.then_inc(s_p1, 1)

            def gnn_degree(at):
                pe.wait_ge(s_mask, at.b + 1)
                wait(pe, s_v, 2 * at.b)
                for j in range(TILES):
                    for i in range(TILES):
                        last = pe.matmul(P2[:, j:j + 1], mask[:, i, j * P:(j + 1) * P], onesb[:, 0:1],
                                         start=(i == 0), stop=(i == TILES - 1))
                last.then_inc(s_p2, 1)

            def gnn_spread(at):
                pe.wait_ge(s_deg, 2 * at.b + 2)
                for j in range(TILES):
                    last = pe.matmul(P2[:, j * P:(j + 1) * P], deg_inv[:, j:j + 1].to_broadcast([P, P]), ident[:],
                                     start=True, stop=True)
                last.then_inc(s_p2, 1)

            def gnn_root(at, layer):
                h = (xT, hT[0])[layer]
                if layer == 0:
                    pe.wait_ge(s_rdeg, at.b + 1)
                else:
                    pe.wait_ge(s_v, 2 * at.b + 1)
                pe.matmul(P2[:], w_root[layer][:], h[:], start=True, stop=True).then_inc(s_p2, 1)

            def gnn_aggregate(at, layer, i):
                if i == 0:
                    pe.wait_ge(s_yhi, 2 * at.b + layer + 1)
                    pe.wait_ge(s_yrest, 2 * at.b + layer + 1)
                    pe.wait_ge(s_ymid, 2 * at.b + layer + 1)
                    pe.wait_ge(s_ylo, 2 * at.b + layer + 1)
                for part in range(PARTS):
                    last = pe.matmul(P1[:], yp[part][:, i, :], mask[:, i, :],
                                     start=(i == 0 and part == 0), stop=(i == TILES - 1 and part == PARTS - 1))
                if i == TILES - 1:
                    last.then_inc(s_p1, 1)

            def gnn_back(at):
                pe.wait_ge(s_h, 2 * at.b + 2)
                pe.wait_ge(s_u, 2 * at.b + 2)
                for j in range(TILES):
                    last = pe.transpose(P1[:, j * P:(j + 1) * P], hT[1][:, j * P:(j + 1) * P], ident[:])
                last.then_inc(s_p1, 1)

            def transpose_hots(at, j, group):
                pair = 2 * (at.b * TILES + j) + group
                pe.wait_ge(s_hot, pair + 1)
                wait(pe, s_hotT, pair)
                for k in range(8):
                    last = pe.transpose(H[:, k * P:(k + 1) * P], hot[:, 8 * group + k, :], identb[:])
                last.then_inc(s_H, 1)

            def transpose_t(at, j):
                pe.wait_ge(s_merged, at.b * TILES + j + 1)
                event = at.b * T_EVENTS + (0, 2, 3, 4)[j]
                wait(pe, s_Tc, event)
                for c in range(CHUNKS):
                    last = pe.transpose(T[:, c * P:(c + 1) * P], acc[j % 2][0][:, c * P:(c + 1) * P], ident[:])
                last.then_inc(s_T, 1)

            def transpose_z(at):
                pe.wait_ge(s_z, at.b + 1)
                wait(pe, s_Tc, at.b * T_EVENTS + 1)
                for j in range(TILES):
                    last = pe.transpose(T[:, j * P:(j + 1) * P], z[:, j, :], ident[:])
                last.then_inc(s_T, 1)

            def ffn_in(at, n):
                if n == 0:
                    pe.wait_ge(s_Tc, at.b * T_EVENTS + 2)
                    wait(pe, s_out, at.b)
                wait(pe, s_Fa, 8 * at.b + n)
                w, c = (wc, wg)[n % 2], n // 2
                pe.matmul(FB[:], w[:, c * P:(c + 1) * P], zT[:], start=True, stop=True).then_inc(s_F, 1)

            def ffn_out(at, j):
                if j == 0:
                    pe.wait_ge(s_fused, 4 * at.b + 4)
                    pe.wait_ge(s_Fa, 8 * at.b + 8)
                o = FB[:, j * P:(j + 1) * P]
                pe.matmul(o, row0[:], bd_s[:], start=True, stop=False)
                for c in range(CHUNKS):
                    last = pe.matmul(o, fused[c][:, j * P:(j + 1) * P], wd[:, c, :],
                                     start=False, stop=(c == CHUNKS - 1))
                if j == TILES - 1:
                    last.then_inc(s_F, 1)

            def tick(at, finish, gnn, ahead):
                before, after, second = at.plus(-1), at.plus(1), at.plus(2)
                for i in range(ROUNDS):
                    j, k = divmod(i, TOP)
                    if k % 8 == 0:
                        pe.wait_ge(s_hotT, 2 * (at.b * TILES + j) + k // 8 + 1)
                    wait(pe, s_round, bank_rounds_before(i, at))
                    for part in range(PARTS):
                        last = pe.matmul(G[i % 3][:], hotT[j % 2][:, k, :], wt[part][:],
                                         start=(part == 0), stop=(part == PARTS - 1))
                    last.then_inc(s_gath, 1)
                    if i in PE_HOTS:
                        transpose_hots(at, *PE_HOTS[i])
                    if gnn and i in PE_HOTS_AFTER:
                        transpose_hots(after, 0, PE_HOTS_AFTER[i])
                    if finish and i == PE_T_BEFORE:
                        transpose_t(before, TILES - 1)
                    if i in PE_T:
                        transpose_t(at, PE_T[i])
                    if i == PE_Z:
                        transpose_z(at)
                    if finish and i in PE_FFN_IN:
                        ffn_in(before, PE_FFN_IN.index(i))
                    if finish and i in PE_FFN_OUT:
                        ffn_out(before, PE_FFN_OUT.index(i))
                    if gnn and i in PE_AGG1:
                        gnn_aggregate(after, 0, PE_AGG1.index(i))
                    if gnn and i == PE_Y2:
                        gnn_y(after, 1)
                    if gnn and i == PE_ROOT2:
                        gnn_root(after, 1)
                    if gnn and i in PE_AGG2:
                        gnn_aggregate(after, 1, PE_AGG2.index(i))
                    if gnn and i == PE_BACK:
                        gnn_back(after)
                    if ahead and i == PE_X:
                        gnn_x_transposed(second)
                    if ahead and i == PE_Y1:
                        gnn_y(second, 0)
                    if ahead and i == PE_DEGREE:
                        gnn_degree(second)
                    if ahead and i == PE_SPREAD:
                        gnn_spread(second)
                    if ahead and i == PE_ROOT1:
                        gnn_root(second, 0)

            first, next_ = fixed(0), fixed(1)
            gnn_x_transposed(first)
            gnn_y(first, 0)
            gnn_degree(first)
            gnn_spread(first)
            gnn_root(first, 0)
            for i in range(TILES):
                gnn_aggregate(first, 0, i)
            gnn_y(first, 1)
            gnn_root(first, 1)
            for i in range(TILES):
                gnn_aggregate(first, 1, i)
            gnn_back(first)
            gnn_x_transposed(next_)
            gnn_y(next_, 0)
            gnn_degree(next_)
            gnn_spread(next_)
            gnn_root(next_, 0)
            transpose_hots(first, 0, 0)
            transpose_hots(first, 0, 1)
            pe.wait_ge(s_putc, 8)
            pe.wait_ge(s_setup_done, 1)
            pe.matmul(T[:, 0:1], onesb[:], over1b[:], start=True, stop=True).then_inc(s_over, 1)
            pe.wait_ge(s_over, 2)
            tick(first, False, True, True)
            tick(fixed(1), True, True, True)
            with pe.Fori(0, 5) as i:
                tick(At(i * 2 + 2, 0, i + 1), True, True, True)
                tick(At(i * 2 + 3, 1, i + 1), True, True, True)
            tick(fixed(12), True, True, True)
            tick(fixed(13), True, True, True)
            tick(fixed(14), True, True, False)
            tick(fixed(15), True, False, False)
            transpose_t(fixed(15), TILES - 1)
            for n in range(2 * CHUNKS):
                ffn_in(fixed(15), n)
            for j in range(TILES):
                ffn_out(fixed(15), j)

            pe.wait_ge(q_fb, 1)
            pe.wait_ge(s_Tc, T_EVENTS * BATCHES)
            pe.matmul(T[:, 0:NCOLS], below[:], fb[:], start=True, stop=True)
            pe.matmul(T[:, NCOLS:2 * NCOLS], onesb[:], fb[:], start=True, stop=True).then_inc(q_rank, 1)
            pe.wait_ge(s_out, BATCHES)
            pe.matmul(FB[:, 0:NCOLS], zerof[:], zerof[:, 0:NCOLS], start=True, stop=False).then_inc(q_hotu, RING)
            with pe.Fori(0, NCOLS // RING) as i:
                for q in range(RING):
                    pe.wait_ge(q_hot, i * RING + q + 1)
                    pe.matmul(FB[:, 0:NCOLS], at_slot[:, q, :], at_tile[:, q, 0:NCOLS], start=False, stop=False)\
                        .then_inc(q_hotu, 1)
            pe.matmul(FB[:, 0:NCOLS], zerof[:], zerof[:, 0:NCOLS], start=False, stop=True).then_inc(q_list, 1)
            pe.wait_ge(q_n, 1)
            tiles = pe.value_load(n_tiles_m[0:1, 0:1], min_val=1, max_val=NCOLS)
            pe.wait_ge(q_n, 2)

            def ffn_product(g, s, n):
                if n == 0:
                    pe.wait_ge(s.zT, g + 1)
                    pe.wait_ge(s.free, g + 1)
                else:
                    pe.wait_ge(s.Fa, g * 2 + 1)
                for c in range(CHUNKS):
                    last = pe.matmul(FB[:, c * P:(c + 1) * P], (wc, wg)[n][:, c * P:(c + 1) * P], g_zT[:],
                                     start=True, stop=True)
                last.then_inc(s.F, 1)

            def gather_deep(g, s):
                def transpose_group(q):
                    pe.wait_ge(s.hot, g * GROUPS + q + 1)
                    if q:
                        pe.wait_ge(s.hotT, g * GROUPS + q)
                    for k in range(8):
                        last = pe.transpose(H[:, k * P:(k + 1) * P], hot[:, 8 * (q % 2) + k, :], identb[:])
                    last.then_inc(s.H, 1)

                transpose_group(0)
                transpose_group(1)
                for q in range(GROUPS):
                    pe.wait_ge(s.hotT, g * GROUPS + q + 1)
                    for k in range(8):
                        n = 8 * q + k
                        if n >= 3:
                            pe.wait_ge(s.round, g * DEEP + n - 2)
                        for part in range(PARTS):
                            last = pe.matmul(G[n % 3][:], hotT[q // 2][:, 8 * (q % 2) + k, :], wt[part][:],
                                             start=(part == 0), stop=(part == PARTS - 1))
                        last.then_inc(s.gath, 1)
                    if q < 2:
                        transpose_group(q + 2)
                        ffn_product(g, s, q)
                pe.wait_ge(s.merged, g + 1)

            def gather_full(g, s):
                ffn_product(g, s, 0)
                ffn_product(g, s, 1)
                with pe.Fori(0, D // 8) as h:
                    for k in range(8):
                        pe.wait_ge(s.round, g * (D + 2) + h * 8 + k + 1)
                        hot_d = identb[:, bass.ds(h * 8 + k, 1)].to_broadcast([P, P])
                        for part in range(PARTS):
                            last = pe.matmul(G[k % 2][:], hot_d, wt[part][:],
                                             start=(part == 0), stop=(part == PARTS - 1))
                        last.then_inc(s.gath, 1)
                pe.wait_ge(s.round, g * (D + 2) + D + 2)

            def general(g, s, gather):
                pe.wait_ge(s.z, g + 1)
                pe.transpose(T[:, 0:P], g_z[:], ident[:]).then_inc(s.zTp, 1)
                gather(g, s)
                pe.wait_ge(s.zT, g + 1)
                for c in range(CHUNKS):
                    last = pe.transpose(T[:, c * P:(c + 1) * P], g_acc[0][:, c * P:(c + 1) * P], ident[:])
                last.then_inc(s.tTp, 1)
                pe.wait_ge(s.fused, g + 1)
                pe.wait_ge(s.Fa, g * 2 + 2)
                pe.matmul(FB[:, 0:P], row0[:], bd_s[:], start=True, stop=False)
                for c in range(CHUNKS):
                    last = pe.matmul(FB[:, 0:P], g_fu[:, c, :], wd[:, c, :], start=False, stop=(c == CHUNKS - 1))
                last.then_inc(s.o, 1)

            with pe.Fori(0, tiles) as g:
                general(g, deep, gather_deep)
            pe.wait_ge(q_anyb, 1)
            pe.matmul(T[:, 0:1], onesb[:], g_anyb[:], start=True, stop=True).then_inc(q_anyc, 1)
            pe.wait_ge(q_any, 1)
            some = pe.value_load(g_any_i[0:1, 0:1], min_val=0, max_val=1)
            with pe.If(some > 0):
                with pe.Fori(0, tiles) as g:
                    general(g, full, gather_full)

        @block.scalar
        def _(act):
            act.wait_ge(s_wload, LOADED)
            act.activation(share[:, 0:CHUNKS], al[:], ACT.Tanh, scale=0.5).then_inc(s_share, 1)
            for n, (to, of) in enumerate(((wcT, FB), (wgT, T))):
                act.wait_ge(s_wT, n + 1)
                act.activation(to[:].rearrange("p c d -> p (c d)"), of[:], ACT.Copy).then_inc(s_wTc, 1)
            puts = [(wt[part][:], G[part][:]) for part in range(PARTS)] + [
                (wc[:], FB[:]), (wg[:], T[:]), (wmax_all[:], G[0][:]),
                (wd[:].rearrange("p c d -> p (c d)"), G[1][:]),
                (feat[:].rearrange("p c v -> p (c v)"), G[2][:, 0:CHUNKS * V_COLS])]
            for n, (to, of) in enumerate(puts):
                act.wait_ge(s_put, n + 1)
                if n == 6:
                    act.wait_ge(s_put, 8)
                act.activation(to, of, ACT.Copy).then_inc(s_putc, 1)

            def split_hi(at, layer):
                pe_event = 6 * at.b + (2, 4)[layer]
                act.wait_ge(s_p1, pe_event)
                act.activation(yp[0][:].rearrange("p j d -> p (j d)"), P1[:], ACT.Copy).then_inc(s_yhi, 1)

            def split_mid(at, layer):
                act.wait_ge(s_yrest, 2 * at.b + layer + 1)
                act.activation(yp[1][:].rearrange("p j d -> p (j d)"), y_rest[:], ACT.Copy).then_inc(s_ymid, 1)

            def elu(at, layer):
                act.wait_ge(s_v, 2 * at.b + layer + 1)
                wait(act, s_h, 2 * at.b + layer)
                act.activation(ev[:], v[:], ACT.Exp, bias=bias[layer][:]).then_inc(s_eluact, 1)
                act.activation(rv[:], v[:], ACT.Relu, bias=bias[layer][:]).then_inc(s_eluact, 1)
                act.wait_ge(s_eluact, 6 * at.b + 3 * layer + 1)
                act.activation(em[:], ev[:], ACT.Relu, bias=unit[:], scale=-1.0).then_inc(s_eluact, 1)

            def copy_inverse_degree(at):
                act.wait_ge(s_p2, 4 * at.b + 2)
                wait(act, s_u, 2 * at.b)
                act.activation(rdeg[:], P2[:], ACT.Copy).then_inc(s_rdeg, 1)

            def keep_x2(at):
                wait(act, s_out, at.b)
                act.activation(x2_before[:].rearrange("p j d -> p (j d)"),
                               x2[at.parity][:].rearrange("p j d -> p (j d)"), ACT.Copy).then_inc(s_keep, 1)

            def copy_xT(at):
                act.wait_ge(s_p1, 6 * at.b + 1)
                act.activation(xT[:], P1[:], ACT.Copy).then_inc(s_xT, 1)

            def copy_hots(at, j, group):
                tile = at.b * TILES + j
                act.wait_ge(s_H, 2 * tile + group + 1)
                wait(act, s_gath, (tile - 1) * TOP)
                act.activation(hotT[j % 2][:, 8 * group:8 * group + 8, :].rearrange("p k n -> p (k n)"), H[:],
                               ACT.Copy).then_inc(s_hotT, 1)

            def copy_t(at, j):
                event = at.b * T_EVENTS + (0, 2, 3, 4)[j]
                act.wait_ge(s_T, event + 1)
                act.activation(tT[at.parity][:, :, j * P:(j + 1) * P], T[:].rearrange("p (c n) -> p c n", c=CHUNKS),
                               ACT.Copy).then_inc(s_Tc, 1)

            def copy_z(at):
                act.wait_ge(s_T, at.b * T_EVENTS + 2)
                wait(act, s_F, 9 * (at.b - 1) + 8)
                act.activation(zT[:], T[:], ACT.Copy).then_inc(s_Tc, 1)

            def gelu(at, c):
                act.wait_ge(s_F, 9 * at.b + 2 * c + 1)
                wait(act, s_fused, 4 * (at.b - 1) + c + 1)
                act.activation(cl[c][:], FB[:], ACT.Gelu, bias=feat[:, c, V_BC:V_BC + 1]).then_inc(s_Fa, 1)

            def tanh(at, c):
                act.wait_ge(s_F, 9 * at.b + 2 * c + 2)
                act.activation(gt[c][:], FB[:], ACT.Tanh, bias=feat[:, c, V_BG:V_BG + 1], scale=0.5)\
                    .then_inc(s_Fa, 1)

            def lines(at, c):
                if c == 0:
                    act.wait_ge(s_Tc, T_EVENTS * at.b + T_EVENTS)
                n = 0
                for slot, func in LINE_ORDER[:DRAWN[c]]:
                    wait(act, s_pwl, ALL_STEPS * at.b + LINE_FREE[c][n])
                    act.activation(line[(c % 2) * 4 + n if c < 3 else n][:], tT[at.parity][:, c, :], ACT.Identity,
                                   bias=feat[:, c, V_SO + 2 * slot + func:V_SO + 2 * slot + func + 1],
                                   scale=feat[:, c, V_SS + 2 * slot + func:V_SS + 2 * slot + func + 1])\
                        .then_inc(s_line, 1)
                    n += 1

            LINE_ORDER = [(0, 0), (1, 0), (0, 1), (1, 1)] + [(m, f) for m in range(2, SLOTS) for f in range(2)]
            LINE_FREE = [[-5, -5, -4, -4], [-2, -1, 0, 0], [1, 1, 2, 2], [5, 5, 6, 6, 3, 3, 4, 4]]

            def tick(at, finish, gnn, ahead):
                before, after, second = at.plus(-1), at.plus(1), at.plus(2)
                if finish:
                    keep_x2(before)
                copy_hots(at, 1, 0)
                if finish:
                    copy_t(before, TILES - 1)
                    gelu(before, 0)
                if gnn:
                    elu(after, 0)
                if finish:
                    lines(before, 0)
                    tanh(before, 0)
                copy_hots(at, 1, 1)
                if finish:
                    gelu(before, 1)
                    lines(before, 1)
                    tanh(before, 1)
                if gnn:
                    split_hi(after, 1)
                if finish:
                    gelu(before, 2)
                if gnn:
                    split_mid(after, 1)
                if finish:
                    lines(before, 2)
                    tanh(before, 2)
                copy_hots(at, 2, 0)
                if finish:
                    gelu(before, 3)
                copy_t(at, 0)
                if finish:
                    tanh(before, 3)
                copy_hots(at, 2, 1)
                copy_z(at)
                if finish:
                    lines(before, 3)
                if gnn:
                    elu(after, 1)
                copy_hots(at, 3, 0)
                copy_t(at, 1)
                copy_hots(at, 3, 1)
                if ahead:
                    copy_xT(second)
                    split_hi(second, 0)
                    split_mid(second, 0)
                copy_t(at, 2)
                if gnn:
                    copy_hots(after, 0, 0)
                if ahead:
                    copy_inverse_degree(second)
                if gnn:
                    copy_hots(after, 0, 1)

            first, next_ = fixed(0), fixed(1)
            copy_xT(first)
            split_hi(first, 0)
            split_mid(first, 0)
            copy_inverse_degree(first)
            elu(first, 0)
            split_hi(first, 1)
            split_mid(first, 1)
            elu(first, 1)
            copy_xT(next_)
            split_hi(next_, 0)
            split_mid(next_, 0)
            copy_inverse_degree(next_)
            copy_hots(first, 0, 0)
            copy_hots(first, 0, 1)
            act.wait_ge(s_over, 1)
            act.activation(over_all[:], T[:, 0:1], ACT.Copy).then_inc(s_over, 1)
            tick(first, False, True, True)
            tick(fixed(1), True, True, True)
            with act.Fori(0, 5) as i:
                tick(At(i * 2 + 2, 0, i + 1), True, True, True)
                tick(At(i * 2 + 3, 1, i + 1), True, True, True)
            tick(fixed(12), True, True, True)
            tick(fixed(13), True, True, True)
            tick(fixed(14), True, True, False)
            tick(fixed(15), True, False, False)
            keep_x2(fixed(15))
            copy_t(fixed(15), TILES - 1)
            for c in range(CHUNKS):
                gelu(fixed(15), c)
                tanh(fixed(15), c)
                lines(fixed(15), c)

            act.wait_ge(q_n, 1)
            tiles = act.value_load(n_tiles_m[0:1, 0:1], min_val=1, max_val=NCOLS)

            def general(g, s, is_deep):
                def copy_group(q):
                    act.wait_ge(s.H, g * GROUPS + q + 1)
                    act.activation(hotT[q // 2][:, 8 * (q % 2):8 * (q % 2) + 8, :].rearrange("p k n -> p (k n)"),
                                   H[:], ACT.Copy).then_inc(s.hotT, 1)

                act.wait_ge(s.zTp, g + 1)
                act.activation(g_zT[:], T[:, 0:P], ACT.Copy).then_inc(s.zT, 1)
                if is_deep:
                    copy_group(0)
                    copy_group(1)
                    copy_group(2)
                act.wait_ge(s.F, g * 2 + 1)
                for c in range(CHUNKS):
                    last = act.activation(g_cl[:, c, :], FB[:, c * P:(c + 1) * P], ACT.Gelu,
                                          bias=feat[:, c, V_BC:V_BC + 1])
                last.then_inc(s.Fa, 1)
                if is_deep:
                    copy_group(3)
                act.wait_ge(s.F, g * 2 + 2)
                for c in range(CHUNKS):
                    last = act.activation(g_gt[:, c, :], FB[:, c * P:(c + 1) * P], ACT.Tanh,
                                          bias=feat[:, c, V_BG:V_BG + 1], scale=0.5)
                last.then_inc(s.Fa, 1)
                act.wait_ge(s.tTp, g + 1)
                act.activation(line[0][:], T[:], ACT.Copy).then_inc(s.tT, 1)
                act.wait_ge(s.tT, g + 1)
                for m in range(LINES):
                    if m > 4:
                        act.wait_ge(s.pwl, g * PWL_STEPS + 2 * (m - 5) + 1)
                    to = g_convex[m % 4] if m else g_pw[0]
                    for c in range(CHUNKS):
                        last = act.activation(to[:, c, :], g_tT[:, c, :], ACT.Identity,
                                              bias=feat[:, c, V_OF + m:V_OF + m + 1],
                                              scale=feat[:, c, V_SL + m:V_SL + m + 1])
                    last.then_inc(s.line, 1)

            with act.Fori(0, tiles) as g:
                general(g, deep, True)
            act.wait_ge(q_any, 1)
            some = act.value_load(g_any_i[0:1, 0:1], min_val=0, max_val=1)
            with act.If(some > 0):
                with act.Fori(0, tiles) as g:
                    general(g, full, False)

        @block.vector
        def _(dve):
            steps = [0]

            def chain(instruction):
                steps[0] += 1
                instruction.then_inc(s_setup_dve, 1)
                dve.wait_ge(s_setup_dve, steps[0])

            def meanvar(at, rows, st, s_st, s_mv, mv):
                for j in range(TILES):
                    last = dve.bn_stats(st[:, j, :], rows[:, j, :])
                last.then_inc(s_st, 1)
                wait_apart(dve, s_st, at.b + 1, s_wload)
                for j in range(TILES):
                    last = dve.bn_aggr(mv[:, j, :], st[:, j, :])
                last.then_inc(s_mv, 1)

            def normalise(rows_out, rows, mv, rs, s_done):
                for j in range(TILES):
                    last = dve.tensor_scalar(rows_out[:, j, :], rows[:, j, :], mv[:, j, 0:1], rs[:, j:j + 1],
                                             ALU.subtract, ALU.mult)
                last.then_inc(s_done, 1)

            def ln1_stats(at):
                dve.wait_ge(s_xin[at.parity], 16 * (at.half + 1))
                meanvar(at, xs[at.parity], st1, s_ln1_st, s_ln1_mv, mv1)

            def ln1_apply(at):
                dve.wait_ge(s_ln1_rs, 2 * at.b + 2)
                wait(dve, s_p1, 6 * (at.b - 1) + 1)
                normalise(xn, xs[at.parity], mv1, rs1, s_xn)

            def split_rest(at, layer):
                dve.wait_ge(s_yhi, 2 * at.b + layer + 1)
                dve.tensor_tensor(y_rest[:], P1[:], yp[0][:].rearrange("p j d -> p (j d)"), ALU.subtract)\
                    .then_inc(s_yrest, 1)

            def split_lo(at, layer):
                dve.wait_ge(s_ymid, 2 * at.b + layer + 1)
                dve.tensor_tensor(yp[2][:].rearrange("p j d -> p (j d)"), y_rest[:],
                                  yp[1][:].rearrange("p j d -> p (j d)"), ALU.subtract).then_inc(s_ylo, 1)

            def degree(at):
                dve.wait_ge(s_p2, 4 * at.b + 1)
                dve.tensor_scalar(deg[:], P2[:, 0:TILES], 1.0, None, ALU.max).then_inc(s_deg, 1)
                dve.wait_ge(s_deg, 2 * at.b + 1)
                dve.reciprocal(deg_inv[:], deg[:]).then_inc(s_deg, 1)

            def mix(at, layer):
                dve.wait_ge(s_p1, 6 * at.b + (3, 5)[layer])
                dve.wait_ge(s_rdeg, at.b + 1)
                dve.tensor_tensor(u[:], P1[:], rdeg[:], ALU.mult).then_inc(s_u, 1)
                dve.wait_ge(s_u, 2 * at.b + layer + 1)
                dve.wait_ge(s_p2, 4 * at.b + layer + 3)
                wait(dve, s_eluact, 6 * at.b + 3 * layer)
                dve.tensor_tensor(v[:], u[:], P2[:], ALU.add).then_inc(s_v, 1)

            def elu(at, layer):
                dve.wait_ge(s_eluact, 6 * at.b + 3 * layer + 3)
                dve.tensor_tensor(hT[layer][:], rv[:], em[:], ALU.subtract).then_inc(s_h, 1)

            def residual(at):
                dve.wait_ge(s_p1, 6 * at.b + 6)
                wait(dve, s_x2d, 16 * (at.b - 1))
                wait(dve, s_keep, at.b - 1)
                dve.tensor_tensor(x2[at.parity][:].rearrange("p j d -> p (j d)"), P1[:],
                                  xs[at.parity][:].rearrange("p j d -> p (j d)"), ALU.add).then_inc(s_x2, 1)
                dve.wait_ge(s_x2, at.b + 1)
                meanvar(at, x2[at.parity], st2, s_ln2_st, s_ln2_mv, mv2)

            def ln2_apply(at):
                dve.wait_ge(s_ln2_rs, 2 * at.b + 2)
                wait(dve, s_T, T_EVENTS * (at.b - 1) + 2)
                normalise(z, x2[at.parity], mv2, rs2, s_z)

            def find_top(at, j):
                tile = at.b * TILES + j
                if j == 0:
                    dve.wait_ge(s_z, at.b + 1)
                wait_apart(dve, s_hot, 2 * (tile - 3), s_wload)
                dve.max(top[j][:, 0:8], z[:, j, :]).then_inc(s_top, 1)
                wait_apart(dve, s_top, 5 * tile + 1, s_wload)
                dve.match_replace(z_left[:], top[j][:, 0:8], z[:, j, :], LOWEST).then_inc(s_top, 1)
                dve.max_index(top_at[j][:, 0:8], top[j][:, 0:8], z[:, j, :]).then_inc(s_top, 1)
                wait_apart(dve, s_top, 5 * tile + 2, s_wload)
                dve.max(top[j][:, 8:16], z_left[:]).then_inc(s_top, 1)
                wait_apart(dve, s_top, 5 * tile + 4, s_wload)
                dve.max_index(top_at[j][:, 8:16], top[j][:, 8:16], z_left[:]).then_inc(s_top, 1)

            def round_(at, i):
                j, k = divmod(i, TOP)
                to = acc[j % 2][k % 2]
                dve.wait_ge(s_gath, at.b * ROUNDS + i + 1)
                if k < 2:
                    if k == 0:
                        wait(dve, s_T, at.b * T_EVENTS + (-1, 0, 1, 3)[j])
                    dve.tensor_scalar(to[:], G[i % 3][:], top[j][:, k:k + 1], None, ALU.add).then_inc(s_round, 1)
                else:
                    dve.wait_ge(s_round, at.b * ROUNDS + i - 1)
                    dve.scalar_tensor_tensor(out=to[:], in0=G[i % 3][:], scalar=top[j][:, k:k + 1],
                                             in1=to[:], op0=ALU.add, op1=ALU.max).then_inc(s_round, 1)

            def merge(at, j):
                even, odd = acc[j % 2]
                dve.wait_ge(s_round, at.b * ROUNDS + (j + 1) * TOP)
                dve.tensor_tensor(even[:], even[:], odd[:], ALU.max).then_inc(s_merged, 1)

            def count_open(at, j):
                dve.wait_ge(s_merged, at.b * TILES + j + 1)
                wait(dve, s_flags, 4 * at.b)
                dve.scalar_tensor_tensor(out=beyond[:], in0=wmax_all[:], scalar=top[j][:, TOP - 1:TOP],
                                         in1=acc[j % 2][0][:], op0=ALU.add, op1=ALU.is_gt,
                                         accum_out=open_n[:, j:j + 1]).then_inc(s_open, 1)

            def pwl(at, c, m):
                base = ALL_STEPS * at.b + sum(STEPS[:c])
                to = (cvx, ccv)[m % 2][c % 2]
                lines_due = 2 * m + 2 if m < 2 else m + 3
                first_line = 4 if c == 1 else 0
                dve.wait_ge(s_line, ALL_DRAWN * at.b + sum(DRAWN[:c]) + lines_due)
                if m < 2:
                    wait(dve, s_fused, 4 * at.b + c - 1)
                    dve.tensor_tensor(to[:], line[first_line + 2 * m][:], line[first_line + 2 * m + 1][:], ALU.max)\
                        .then_inc(s_pwl, 1)
                else:
                    dve.wait_ge(s_pwl, base + m - 1)
                    dve.tensor_tensor(to[:], to[:], line[m + 2][:], ALU.max).then_inc(s_pwl, 1)

            def output(at):
                dve.wait_ge(s_F, 9 * at.b + 9)
                dve.wait_ge(s_keep, at.b + 1)
                wait(dve, s_outd, 16 * at.b)
                dve.tensor_tensor(o_s[:].rearrange("p j d -> p (j d)"), FB[:],
                                  x2_before[:].rearrange("p j d -> p (j d)"), ALU.add).then_inc(s_out, 1)

            def tick(at, finish, gnn, ahead):
                before, after, second = at.plus(-1), at.plus(1), at.plus(2)
                for i in range(ROUNDS):
                    round_(at, i)
                    j, k = divmod(i, TOP)
                    if k == 0 and j > 0:
                        merge(at, j - 1)
                    if k == 1 and j > 0:
                        count_open(at, j - 1)
                    if finish and i == 0:
                        merge(before, TILES - 1)
                    if finish and i == 1:
                        count_open(before, TILES - 1)
                    if i in DVE_TOPS:
                        find_top(at, DVE_TOPS[i])
                    if gnn and i == DVE_MIX1:
                        mix(after, 0)
                    if gnn and i == DVE_ELU1:
                        elu(after, 0)
                    if gnn and i == DVE_REST2:
                        split_rest(after, 1)
                    if gnn and i == DVE_LO2:
                        split_lo(after, 1)
                    if gnn and i == DVE_MIX2:
                        mix(after, 1)
                    if gnn and i == DVE_ELU2:
                        elu(after, 1)
                    if gnn and i == DVE_RESIDUAL:
                        residual(after)
                    if gnn and i == DVE_LN2:
                        ln2_apply(after)
                    if gnn and i in DVE_TOPS_AFTER:
                        find_top(after, DVE_TOPS_AFTER[i])
                    if ahead and i == DVE_LN1_STATS:
                        ln1_stats(second)
                    if ahead and i == DVE_LN1:
                        ln1_apply(second)
                    if ahead and i == DVE_REST1:
                        split_rest(second, 0)
                    if ahead and i == DVE_DEGREE:
                        degree(second)
                    if ahead and i == DVE_LO1:
                        split_lo(second, 0)
                    if finish and i == DVE_OUTPUT:
                        output(before)
                    if finish:
                        for c in range(CHUNKS):
                            if i in DVE_PWL[c]:
                                pwl(before, c, DVE_PWL[c].index(i))

            dve.wait_ge(s_wload, LOADED)
            first, next_ = fixed(0), fixed(1)
            ln1_stats(first)
            ln1_apply(first)
            chain(dve.reduce_max(wmax[:], wt_f[:], AX_X))
            chain(dve.tensor_reduce(wmin[:], wt_f[:], AX_X, ALU.min))
            rest = wt_r[:].rearrange("p (c d) -> p c d", c=CHUNKS)
            chain(dve.tensor_copy(wt_fp[0][:], wt_f[:]))
            chain(dve.tensor_tensor(rest, wt_f[:], wt_fp[0][:], ALU.subtract))
            chain(dve.tensor_copy(wt_fp[1][:], rest))
            dve.tensor_tensor(wt_fp[2][:], rest, wt_fp[1][:], ALU.subtract).then_inc(s_wtf, 1)
            dve.wait_ge(s_share, 1)
            chain(dve.tensor_scalar(share[:, 0:CHUNKS], share[:, 0:CHUNKS], 0.5, 0.5, ALU.mult, ALU.add))
            chain(dve.tensor_scalar(share[:, CHUNKS:FC], share[:, 0:CHUNKS], 1.0, None, ALU.subtract))
            chain(dve.tensor_tensor(slope[:], slope[:], share[:][:, :, None].to_broadcast([P, FC, LINES]), ALU.mult))
            chain(dve.tensor_tensor(offs[:], offs[:], share[:][:, :, None].to_broadcast([P, FC, LINES]), ALU.mult))
            chain(dve.tensor_tensor(lo_hi[:, 0, :], wmin[:], bt_s[:], ALU.add))
            chain(dve.tensor_tensor(lo_hi[:, 1, :], wmax[:], bt_s[:], ALU.add))
            chain(dve.tensor_scalar(lo_hi[:, 0, :], lo_hi[:, 0, :], Z_LO, None, ALU.add))
            chain(dve.tensor_scalar(lo_hi[:, 1, :], lo_hi[:, 1, :], Z_HI, None, ALU.add))
            for e, end in ((0, end_a), (1, end_b)):
                for f in range(2):
                    part = slice(f * CHUNKS, (f + 1) * CHUNKS)
                    at_end = lo_hi[:, e, :][:, :, None].to_broadcast([P, CHUNKS, LINES])
                    chain(dve.tensor_tensor(end[:, part, :], slope[:, part, :], at_end, ALU.mult))
                chain(dve.tensor_tensor(end[:], end[:], offs[:], ALU.add))
            da, db, cross, low, one = [w[:].rearrange("p (f a b) -> p f a b", a=LINES, b=LINES) for w in work]
            for d, end in ((da, end_a), (db, end_b)):
                chain(dve.tensor_tensor(d, end[:][:, :, :, None].to_broadcast([P, FC, LINES, LINES]),
                                        end[:][:, :, None, :].to_broadcast([P, FC, LINES, LINES]), ALU.subtract))
            chain(dve.tensor_tensor(low, da, db, ALU.subtract))
            chain(dve.tensor_scalar(one, low, 0.0, None, ALU.is_equal))
            chain(dve.tensor_tensor(low, low, one, ALU.add))
            chain(dve.reciprocal(cross, low))
            chain(dve.tensor_tensor(cross, cross, da, ALU.mult))
            chain(dve.tensor_scalar(low, db, 0.0, 2.0, ALU.is_le, ALU.mult))
            chain(dve.tensor_tensor(low, low, cross, ALU.max))
            chain(dve.tensor_scalar(one, da, 0.0, None, ALU.is_lt))
            chain(dve.tensor_tensor(low, low, one, ALU.mult))
            chain(dve.reduce_max(need[:], low, AX_X))
            chain(dve.tensor_scalar(low, cross, -1.0, 1.0, ALU.mult, ALU.add))
            chain(dve.tensor_scalar(one, db, 0.0, None, ALU.is_lt))
            chain(dve.tensor_tensor(low, low, one, ALU.mult))
            chain(dve.tensor_scalar(one, da, 0.0, None, ALU.is_ge))
            chain(dve.tensor_tensor(low, low, one, ALU.mult))
            chain(dve.reduce_max(picked[:], low, AX_X))
            chain(dve.tensor_tensor(need[:], need[:], picked[:], ALU.add))
            chain(dve.tensor_scalar(need[:], need[:], 1.0 + MARGIN, None, ALU.is_le))
            chain(dve.memset(rank[:, :, 0:1], 0.0))
            for k in range(1, LINES):
                chain(dve.tensor_tensor(rank[:, :, k], rank[:, :, k - 1], need[:, :, k - 1], ALU.add))
            chain(dve.tensor_tensor(count[:], rank[:, :, LINES - 1], need[:, :, LINES - 1], ALU.add))
            chain(dve.tensor_tensor(key[:], count[:, 0:CHUNKS], count[:, CHUNKS:FC], ALU.max))
            chain(dve.tensor_tensor(key_sum[:], count[:, 0:CHUNKS], count[:, CHUNKS:FC], ALU.add))
            chain(dve.tensor_scalar(key[:], key[:], float(4 * LINES), None, ALU.mult))
            chain(dve.tensor_tensor(key[:], key[:], key_sum[:], ALU.add))
            chain(dve.tensor_scalar(key[:], key[:], float(FFN), None, ALU.mult))
            chain(dve.tensor_tensor(key[:], key[:], tok[:, 0:CHUNKS], ALU.add))
            dve.tensor_scalar(key_half[:], key[:], 0.5, None, ALU.subtract).then_inc(s_key, 1)
            for f in range(2):
                part = slice(f * CHUNKS, (f + 1) * CHUNKS)
                chain(dve.tensor_tensor(picked[:, part, :], slope[:, part, :],
                                        bt_s[:][:, :, None].to_broadcast([P, CHUNKS, LINES]), ALU.mult))
            chain(dve.tensor_tensor(offs[:], offs[:], picked[:], ALU.add))
            for m in range(SLOTS):
                chain(dve.tensor_scalar(pick[:], rank[:], float(m), None, ALU.is_equal))
                chain(dve.tensor_tensor(pick[:], pick[:], need[:], ALU.mult))
                for of, to in ((slope, slot_sl), (offs, slot_of)):
                    chain(dve.tensor_tensor(picked[:], pick[:], of[:], ALU.mult))
                    chain(dve.reduce_sum(to[:, m, :], picked[:], AX_X))
                    if m:
                        chain(dve.tensor_scalar(empty[:], count[:], float(m), None, ALU.is_le))
                        chain(dve.tensor_tensor(empty[:], empty[:], to[:, 0, :], ALU.mult))
                        chain(dve.tensor_tensor(to[:, m, :], to[:, m, :], empty[:], ALU.add))
            for f in range(2):
                part = slice(f * CHUNKS, (f + 1) * CHUNKS)
                chain(dve.tensor_copy(table[:, :, V_SL + f * LINES:V_SL + (f + 1) * LINES], slope[:, part, :]))
                chain(dve.tensor_copy(table[:, :, V_OF + f * LINES:V_OF + (f + 1) * LINES], offs[:, part, :]))
                chain(dve.tensor_copy(table[:, :, V_N + f], count[:, part]))
                for m in range(SLOTS):
                    chain(dve.tensor_copy(table[:, :, V_SS + 2 * m + f], slot_sl[:, m, part]))
                    chain(dve.tensor_copy(table[:, :, V_SO + 2 * m + f], slot_of[:, m, part]))
            chain(dve.tensor_copy(table[:, :, V_BC], bc_s[:]))
            chain(dve.tensor_scalar(table[:, :, V_BG], bg_s[:], 0.5, None, ALU.mult))
            dve.wait_ge(s_keyr, 1)
            dve.wait_ge(s_key, 1)
            for c in range(CHUNKS):
                chain(dve.tensor_scalar(wt_r[:], G[0][:], key_half[:, c:c + 1], None, ALU.is_lt))
                chain(dve.reduce_sum(place[:, c:c + 1], wt_r[:], AX_X))
            chain(dve.tensor_copy(wt_r[:], place_i[:]))
            for c in range(CHUNKS):
                chain(dve.tensor_scalar(perm[c][:], wt_r[:], place[:, c:c + 1], None, ALU.is_equal))
                last = dve.tensor_copy(permb[:, c, :], perm[c][:])
            last.then_inc(s_perm, 1)
            for m in range(CHUNKS):
                chain(dve.memset(planned[:, m, :], float(PLAN[m])))
            dve.wait_ge(s_putc, 8)
            chain(dve.tensor_tensor(over[:], feat[:, :, V_N:V_N + 2], planned[:], ALU.is_gt))
            chain(dve.reduce_max(over1[:], over[:].rearrange("p c f -> p (c f)"), AX_X))
            dve.tensor_copy(over1b[:], over1[:]).then_inc(s_setup_done, 1)

            split_rest(first, 0)
            split_lo(first, 0)
            degree(first)
            mix(first, 0)
            elu(first, 0)
            split_rest(first, 1)
            split_lo(first, 1)
            mix(first, 1)
            elu(first, 1)
            residual(first)
            ln1_stats(next_)
            ln2_apply(first)
            find_top(first, 0)
            find_top(first, 1)
            ln1_apply(next_)
            split_rest(next_, 0)
            split_lo(next_, 0)
            degree(next_)
            tick(first, False, True, True)
            tick(fixed(1), True, True, True)
            with dve.Fori(0, 5) as i:
                tick(At(i * 2 + 2, 0, i + 1), True, True, True)
                tick(At(i * 2 + 3, 1, i + 1), True, True, True)
            tick(fixed(12), True, True, True)
            tick(fixed(13), True, True, True)
            tick(fixed(14), True, True, False)
            tick(fixed(15), True, False, False)
            merge(fixed(15), TILES - 1)
            count_open(fixed(15), TILES - 1)
            for c in range(CHUNKS):
                for m in range(STEPS[c]):
                    pwl(fixed(15), c, m)
            output(fixed(15))

            gsteps = [0]

            def gchain(instruction):
                gsteps[0] += 1
                instruction.then_inc(q_dve, 1)
                dve.wait_ge(q_dve, gsteps[0])

            dve.wait_ge(s_flags, 4 * BATCHES)
            gchain(dve.tensor_scalar(ff[:], flags[:], 0.5, None, ALU.is_gt))
            dve.tensor_copy(fb[:], ff[:]).then_inc(q_fb, 1)
            dve.wait_ge(q_rank, 1)
            gchain(dve.tensor_copy(total[:], T[:, NCOLS:2 * NCOLS]))
            gchain(dve.tensor_copy(tot[0][:], T[:, NCOLS:2 * NCOLS]))
            n, q = 1, 0
            while n < NCOLS:
                gchain(dve.tensor_copy(tot[1 - q][:, 0:n], tot[q][:, 0:n]))
                gchain(dve.tensor_tensor(tot[1 - q][:, n:NCOLS], tot[q][:, n:NCOLS], tot[q][:, 0:NCOLS - n], ALU.add))
                n, q = 2 * n, 1 - q
            gchain(dve.tensor_tensor(rk[:], tot[q][:], total[:], ALU.subtract))
            gchain(dve.tensor_tensor(rk[:], rk[:], T[:, 0:NCOLS], ALU.add))
            gchain(dve.tensor_copy(rk_i[:], rk[:]))
            gchain(dve.tensor_scalar(rk_c_i[:], rk_i[:], 7, None, ALU.logical_shift_right))
            gchain(dve.tensor_scalar(rk_s_i[:], rk_i[:], P - 1, None, ALU.bitwise_and))
            gchain(dve.tensor_copy(rk_c[:], rk_c_i[:]))
            gchain(dve.tensor_copy(rk_s[:], rk_s_i[:]))
            gchain(dve.tensor_tensor(tok[:], tok[:], ff[:], ALU.mult))
            gchain(dve.tensor_scalar(n_tiles_f[:], tot[q][:, NCOLS - 1:NCOLS], float(P - 1), float(P), ALU.add, ALU.max))
            gchain(dve.tensor_copy(n_tiles_i[:], n_tiles_f[:]))
            dve.tensor_scalar(n_tiles_m[:], n_tiles_i[:], 7, None, ALU.logical_shift_right).then_inc(q_n, 1)
            with dve.Fori(0, NCOLS // RING) as i:
                for p in range(RING):
                    col = i * RING + p
                    dve.wait_ge(q_hotu, col + 1)
                    dve.tensor_scalar(at_slot[:, p, :], iota[:], rk_s[:, bass.ds(col, 1)], None, ALU.is_equal)
                    dve.tensor_scalar(at_tile[:, p, 0:NCOLS], iota[:, 0:NCOLS], rk_c[:, bass.ds(col, 1)],
                                      tok[:, bass.ds(col, 1)], ALU.is_equal, ALU.mult).then_inc(q_hot, 1)
            dve.wait_ge(q_list, 1)
            gchain(dve.tensor_copy(got[:], FB[:, 0:NCOLS]))
            gchain(dve.tensor_scalar(hole[:], got[:], 0.5, float(4 * BATCHES * NODES), ALU.is_lt, ALU.mult))
            gchain(dve.tensor_scalar(src[:], got[:], -1.0, 0.0, ALU.add, ALU.max))
            dve.tensor_tensor(dst[:], src[:], hole[:], ALU.add).then_inc(q_n, 1)
            dve.wait_ge(q_n, 2)
            tiles = dve.value_load(n_tiles_m[0:1, 0:1], min_val=1, max_val=NCOLS)

            def search_deep(g, s):
                def find(q):
                    rows = (g_z, g_left[0], g_left[1], g_left[0])[q]
                    base = g * (3 * GROUPS - 1) + 3 * q
                    part = slice(8 * q, 8 * q + 8)
                    if q:
                        wait_apart(dve, s.top, base, s_wload)
                    dve.max(g_top[:, part], rows[:]).then_inc(s.top, 1)
                    wait_apart(dve, s.top, base + 1, s_wload)
                    dve.max_index(g_at[:, part], g_top[:, part], rows[:]).then_inc(s.top, 1)
                    if q < GROUPS - 1:
                        dve.match_replace(g_left[q % 2][:], g_top[:, part], rows[:], LOWEST).then_inc(s.top, 1)

                def one_hots(q):
                    dve.wait_ge(s.top, g * (3 * GROUPS - 1) + 3 * q + 2)
                    if q >= 2:
                        dve.wait_ge(s.H, g * GROUPS + q - 1)
                    for k in range(8):
                        last = dve.tensor_scalar(hot[:, 8 * (q % 2) + k, :], iota[:], g_at[:, 8 * q + k:8 * q + k + 1],
                                                 None, ALU.is_equal)
                    last.then_inc(s.hot, 1)

                def rounds(q):
                    for k in range(8):
                        n = 8 * q + k
                        to = g_acc[n % 2]
                        dve.wait_ge(s.gath, g * DEEP + n + 1)
                        if n < 2:
                            dve.tensor_scalar(to[:], G[n % 3][:], g_top[:, n:n + 1], None, ALU.add)\
                                .then_inc(s.round, 1)
                        else:
                            dve.wait_ge(s.round, g * DEEP + n - 1)
                            dve.scalar_tensor_tensor(out=to[:], in0=G[n % 3][:], scalar=g_top[:, n:n + 1],
                                                     in1=to[:], op0=ALU.add, op1=ALU.max).then_inc(s.round, 1)

                for q in range(3):
                    find(q)
                    one_hots(q)
                rounds(0)
                find(3)
                one_hots(3)
                rounds(1)
                rounds(2)
                rounds(3)
                dve.wait_ge(s.round, g * DEEP + DEEP)
                dve.tensor_tensor(g_acc[0][:], g_acc[0][:], g_acc[1][:], ALU.max).then_inc(s.merged, 1)
                dve.wait_ge(s.merged, g + 1)
                dve.scalar_tensor_tensor(out=beyond[:], in0=wmax_all[:], scalar=g_top[:, DEEP - 1:DEEP],
                                         in1=g_acc[0][:], op0=ALU.add, op1=ALU.is_gt,
                                         accum_out=g_open[:]).then_inc(s.open, 1)
                dve.wait_ge(s.open, g * 2 + 1)
                dve.tensor_tensor(g_any[:], g_any[:], g_open[:], ALU.max).then_inc(s.open, 1)

            def search_full(g, s):
                dve.memset(g_acc[0][:], LOWEST).then_inc(s.round, 2)
                with dve.Fori(0, D // 8) as h:
                    for k in range(8):
                        dve.wait_ge(s.gath, g * D + h * 8 + k + 1)
                        dve.wait_ge(s.round, g * (D + 2) + h * 8 + k + 2)
                        dve.scalar_tensor_tensor(out=g_acc[0][:], in0=G[k % 2][:], scalar=g_z[:, bass.ds(h * 8 + k, 1)],
                                                 in1=g_acc[0][:], op0=ALU.add, op1=ALU.max).then_inc(s.round, 1)

            def general(g, s, search):
                dve.wait_ge(s.free, g + 1)
                dve.tensor_copy(src_i[:], src[:, bass.ds(g, 1)]).then_inc(s.idx, 1)
                dve.tensor_copy(dst_i[:], dst[:, bass.ds(g, 1)]).then_inc(s.idx, 1)
                dve.wait_ge(s.rows, g * 16 + 16)
                dve.bn_stats(g_st[:], g_x[:]).then_inc(s.st, 1)
                wait_apart(dve, s.st, g + 1, s_wload)
                dve.bn_aggr(g_mv[:], g_st[:]).then_inc(s.mv, 1)
                dve.wait_ge(s.mv, g + 1)
                wait_apart(dve, s.rs, g * 2 + 2, s_wload)
                dve.tensor_scalar(g_z[:], g_x[:], g_mv[:, 0:1], g_rs[:], ALU.subtract, ALU.mult).then_inc(s.z, 1)
                wait_apart(dve, s.z, g + 1, s_wload)
                search(g, s)
                dve.wait_ge(s.Fa, g * 2 + 2)
                dve.tensor_scalar(g_gt, g_gt, 0.5, 0.5, ALU.mult, ALU.add).then_inc(s.mix, 1)

                def draw(m):
                    to = g_concave[m % 2] if m else g_pw[1]
                    if m > 2:
                        dve.wait_ge(s.pwl, g * PWL_STEPS + 2 * (m - 2))
                    k, o = V_SL + LINES + m, V_OF + LINES + m
                    for c in range(CHUNKS):
                        last = dve.tensor_scalar(to[:, c, :], g_tT[:, c, :], feat[:, c, k:k + 1], feat[:, c, o:o + 1],
                                                 ALU.mult, ALU.add)
                    last.then_inc(s.drawn, 1)

                dve.wait_ge(s.tT, g + 1)
                draw(0)
                draw(1)
                for m in range(1, LINES):
                    if m < LINES - 1:
                        draw(m + 1)
                    for f, lines_of, drawn in ((0, g_convex[m % 4], s.line), (1, g_concave[m % 2], s.drawn)):
                        dve.wait_ge(drawn, g * LINES + m + 1)
                        if m > 1:
                            dve.wait_ge(s.pwl, g * PWL_STEPS + 2 * (m - 2) + f + 1)
                        dve.tensor_tensor(g_pw[f], g_pw[f], lines_of, ALU.max).then_inc(s.pwl, 1)
                dve.wait_ge(s.pwl, g * PWL_STEPS + PWL_STEPS)
                dve.tensor_tensor(g_pw[0], g_pw[0], g_pw[1], ALU.subtract).then_inc(s.mix, 1)
                dve.wait_ge(s.mix, g * 4 + 2)
                dve.tensor_tensor(g_pw[0], g_pw[0], g_cl, ALU.subtract).then_inc(s.mix, 1)
                dve.wait_ge(s.mix, g * 4 + 3)
                dve.tensor_tensor(g_pw[0], g_pw[0], g_gt, ALU.mult).then_inc(s.mix, 1)
                dve.wait_ge(s.mix, g * 4 + 4)
                dve.tensor_tensor(g_fu, g_pw[0], g_cl, ALU.add).then_inc(s.fused, 1)
                dve.wait_ge(s.o, g + 1)
                dve.tensor_tensor(g_o[:], FB[:, 0:D], g_x[:], ALU.add).then_inc(s.os, 1)

            gchain(dve.memset(g_any[:], 0.0))
            with dve.Fori(0, tiles) as g:
                general(g, deep, search_deep)
            gchain(dve.tensor_scalar(g_any_f[:], g_any[:], OPEN_FROM, None, ALU.is_gt))
            dve.tensor_copy(g_anyb[:], g_any_f[:]).then_inc(q_anyb, 1)
            dve.wait_ge(q_anyc, 1)
            gchain(dve.tensor_scalar(g_any_f[:], T[:, 0:1], 0.5, None, ALU.is_gt))
            dve.tensor_copy(g_any_i[:], g_any_f[:]).then_inc(q_any, 1)
            dve.wait_ge(q_any, 1)
            some = dve.value_load(g_any_i[0:1, 0:1], min_val=0, max_val=1)
            with dve.If(some > 0):
                with dve.Fori(0, tiles) as g:
                    general(g, full, search_full)


_INS = ["x", "adj", "L0_gnn_w_rel1", "L0_gnn_w_root1", "L0_gnn_b1", "L0_gnn_w_rel2", "L0_gnn_w_root2", "L0_gnn_b2",
        "L0_ffn_Wt", "L0_ffn_bt", "L0_ffn_sl_cvx", "L0_ffn_of_cvx", "L0_ffn_sl_ccv", "L0_ffn_of_ccv",
        "L0_ffn_alpha", "L0_ffn_Wc", "L0_ffn_bc", "L0_ffn_Wg", "L0_ffn_bg", "L0_ffn_Wd", "L0_ffn_bd"]
_OUTS = [((BATCHES, NODES, D), "float32")]


def kernel(**inputs):
    import numpy as _np
    import concourse.bacc as _bacc
    from concourse import mybir as _mybir
    from concourse.bass_utils import run_bass_kernel_spmd as _run

    nc = _bacc.Bacc("TRN2", target_bir_lowering=False, num_devices=1)
    arrays, args = {}, []
    for name in _INS:
        a = _np.ascontiguousarray(inputs[name])
        arrays[f"in_{name}_dram"] = a
        args.append(nc.dram_tensor(f"in_{name}_dram", a.shape, _mybir.dt.from_np(a.dtype), kind="ExternalInput").ap())
    for i, (shape, dtype) in enumerate(_OUTS):
        dt = _mybir.dt.from_np(_np.dtype(dtype))
        args.append(nc.dram_tensor(f"out_{i}_dram", shape, dt, kind="ExternalOutput").ap())
    build(nc, *args)
    r = _run(nc, [arrays], core_ids=[0])
    got = tuple(r.results[0][f"out_{i}_dram"] for i in range(len(_OUTS)))
    return got[0]
```

```python
from contextlib import ExitStack

import concourse.bass as bass
from concourse import mybir

F32 = mybir.dt.float32
BF16 = mybir.dt.bfloat16
I32 = mybir.dt.int32
U32 = mybir.dt.uint32
ALU = mybir.AluOpType
ACT = mybir.ActivationFunctionType
AX_X = mybir.AxisListType.X

P = 128
BATCHES = 16
TILES = 4
NODES = TILES * P
D = 128
FFN = 512
CHUNKS = FFN // P
LINES = 8
FOUND = 16
TOP = 15
PLAN = (2, 2, 2, 4)
SLOTS = max(PLAN)
DRAWN = [2 * n for n in PLAN]
STEPS = [2 * (n - 1) for n in PLAN]
V_SL, V_OF = 0, 2 * LINES
V_SS = 4 * LINES
V_SO = V_SS + 2 * SLOTS
V_BC, V_BG = V_SO + 2 * SLOTS, V_SO + 2 * SLOTS + 1
V_N = V_BG + 1
V_COLS = V_N + 2
PARTS = 3
ROUNDS = TILES * TOP
EPS = 1e-5
MARGIN = 1e-4
Z_LO, Z_HI = 1.5, 5.2
LOWEST = -3.0e38
T_EVENTS = 5
T_OF_TILE, T_OF_Z = (0, 1, 3, 4), 2
NCOLS = BATCHES * TILES
GROUPS = 4
DEEP = 8 * GROUPS
EXTRA = [(c, m, f) for c in range(CHUNKS) for m in range(2, PLAN[c]) for f in range(2)]
OPEN_FROM = 0.5
RING = NCOLS // CHUNKS

PE_HOTS = {2: (1, 0), 7: (1, 1), 17: (2, 0), 22: (2, 1), 32: (3, 0), 38: (3, 1)}
PE_HOTS_AFTER = {51: 0, 56: 1}
PE_T = {19: 0, 34: 1, 49: 2}
PE_T_BEFORE = 4
PE_Z = 39
PE_FFN_IN = (9, 12, 15, 18, 21, 24, 30, 33)
PE_FFN_OUT = (48, 50, 52, 54)
PE_AGG1 = (0, 1, 2, 3)
PE_Y2, PE_ROOT2 = 11, 13
PE_AGG2 = (20, 22, 23, 25)
PE_BACK = 33
PE_X, PE_Y1, PE_DEGREE, PE_SPREAD, PE_ROOT1 = 41, 45, 43, 53, 59
DVE_TOPS = {2: 2, 17: 3}
DVE_TOPS_AFTER = {42: 0, 50: 1}
DVE_MIX1, DVE_ELU1, DVE_REST2, DVE_LO2, DVE_MIX2, DVE_ELU2 = 5, 8, 14, 17, 26, 30
DVE_RESIDUAL = 35
DVE_OUTPUT = 57
DVE_LN1_STATS, DVE_REST1, DVE_LO1, DVE_DEGREE = 14, 48, 52, 50
DVE_PWL = ((12, 13), (17, 18), (23, 24), (28, 29, 32, 33, 34, 35))


class Pass:

    def __init__(self, sem, name, lines, drawn, pwl_steps):
        self.lines, self.drawn_lines, self.pwl_steps = lines, drawn, pwl_steps
        self.free = sem(name + "_buffers_free")
        self.idx = sem(name + "_indices")
        self.rows = sem(name + "_rows_in")
        self.st = sem(name + "_stats")
        self.mv = sem(name + "_meanvar")
        self.rs = sem(name + "_rstd")
        self.z = sem(name + "_z")
        self.zTp = sem(name + "_zT_psum")
        self.zT = sem(name + "_zT")
        self.top = sem(name + "_top_found")
        self.hot = sem(name + "_hot_made")
        self.H = sem(name + "_hot_bank_full")
        self.hotT = sem(name + "_hotT_copied")
        self.gath = sem(name + "_round_gathered")
        self.round = sem(name + "_round_done")
        self.merged = sem(name + "_even_odd_merged")
        self.open = sem(name + "_open_counted")
        self.tTp = sem(name + "_tT_psum")
        self.tT = sem(name + "_tT")
        self.F = sem(name + "_ffn_psum")
        self.Fa = sem(name + "_gelu_tanh")
        self.line = sem(name + "_convex_line")
        self.drawn = sem(name + "_concave_line")
        self.pwl = sem(name + "_pwl_step")
        self.mix = sem(name + "_gate_steps")
        self.fused = sem(name + "_fused")
        self.o = sem(name + "_out_psum")
        self.os = sem(name + "_out_summed")
        self.stored = sem(name + "_stored")


class At:

    def __init__(self, b, parity, half):
        self.b, self.parity, self.half = b, parity, half

    def plus(self, n):
        h = self.half + (self.parity + n) // 2
        return At(self.b + n, (self.parity + n) % 2, h)


def fixed(b):
    return At(b, b % 2, b // 2)


def wait(engine, semaphore, value):
    if isinstance(value, int) and value <= 0:
        return
    engine.wait_ge(semaphore, value)


def wait_apart(engine, semaphore, value, held):
    if isinstance(value, int):
        wait(engine, semaphore, value)
        return
    register = engine.to_reg(value)
    engine.wait_ge(held, 1)
    engine.wait_ge(semaphore, register)


def build(nc, x, adj, w_rel1, w_root1, b1, w_rel2, w_root2, b2, Wt, bt, sl_cvx, of_cvx,
          sl_ccv, of_ccv, alpha, Wc, bc, Wg, bg, Wd, bd, out):
    ctx = ExitStack()
    with ctx:
        def sb(name, shape, dt=F32):
            return ctx.enter_context(nc.sbuf_tensor(name, shape, dt))

        def bank(name, shape=(P, 512), dt=F32):
            return ctx.enter_context(nc.psum_tensor(name, list(shape), dt))

        def sem(name):
            return ctx.enter_context(nc.semaphore(name))

        ident = sb("ident", [P, P])
        identb = sb("identb", [P, P], BF16)
        onesb = sb("onesb", [P, P], BF16)
        below = sb("below", [P, P], BF16)
        zerof = sb("zerof", [P, P])
        row0 = sb("row0", [P, P])
        iota_i = sb("iota_i", [P, P], I32)
        iota = sb("iota", [P, P])
        minus_half = sb("minus_half", [P, TILES])
        unit = sb("unit", [P, 1])
        half = sb("half", [P, 1])
        w_root = [sb("w_root1_s", [P, D]), sb("w_root2_s", [P, D])]
        w_rel = [sb("w_rel1_s", [P, D]), sb("w_rel2_s", [P, D])]
        bias = [sb("b1_s", [P, 1]), sb("b2_s", [P, 1])]
        wc = sb("wc", [P, FFN])
        wg = sb("wg", [P, FFN])
        wd = sb("wd", [P, CHUNKS, D])
        bc_s = sb("bc_s", [P, CHUNKS])
        bg_s = sb("bg_s", [P, CHUNKS])
        bd_s = sb("bd_s", [P, D])
        bt_s = sb("bt_s", [P, CHUNKS])
        al = sb("al", [P, CHUNKS])
        wt_f = sb("wt_f", [P, CHUNKS, D])
        wt_r = sb("wt_r", [P, FFN])
        wcT = sb("wcT", [P, CHUNKS, D])
        wgT = sb("wgT", [P, CHUNKS, D])
        wt = [sb(f"wt{p}", [P, FFN], BF16) for p in range(PARTS)]
        wmax = sb("wmax", [P, CHUNKS])
        wmin = sb("wmin", [P, CHUNKS])
        wmax_all = sb("wmax_all", [P, FFN])
        FC = 2 * CHUNKS
        table = sb("table", [P, CHUNKS, V_COLS])
        feat = sb("feat", [P, CHUNKS, V_COLS])
        slope = sb("slope", [P, FC, LINES])
        offs = sb("offs", [P, FC, LINES])
        share = sb("share", [P, FC])
        end_a = sb("end_a", [P, FC, LINES])
        end_b = sb("end_b", [P, FC, LINES])
        need = sb("need", [P, FC, LINES])
        rank = sb("rank", [P, FC, LINES])
        count = sb("count", [P, FC])
        pick = sb("pick", [P, FC, LINES])
        picked = sb("picked", [P, FC, LINES])
        empty = sb("empty", [P, FC])
        lo_hi = sb("lo_hi", [P, 2, CHUNKS])
        slot_sl = sb("slot_sl", [P, SLOTS, FC])
        slot_of = sb("slot_of", [P, SLOTS, FC])
        key = sb("key", [P, CHUNKS])
        key_half = sb("key_half", [P, CHUNKS])
        key_sum = sb("key_sum", [P, CHUNKS])
        place = sb("place", [P, CHUNKS])
        place_i = sb("place_i", [P, FFN], I32)
        wt_fp = [sb(f"wt_f{p}", [P, CHUNKS, D], BF16) for p in range(PARTS)]
        permb = sb("permb", [P, CHUNKS, FFN], BF16)
        planned = sb("planned", [P, CHUNKS, 2])
        over = sb("over", [P, CHUNKS, 2])
        over1 = sb("over1", [P, 1])
        over1b = sb("over1b", [P, 1], BF16)
        over_all = sb("over_all", [P, 1])

        xs = [sb(f"x{q}", [P, TILES, D]) for q in range(2)]
        adjs = [sb(f"adj{q}", [P, TILES, NODES], I32) for q in range(2)]
        mask = sb("mask", [P, TILES, NODES], BF16)
        st1 = sb("st1", [P, TILES, 6])
        st2 = sb("st2", [P, TILES, 6])
        mv1 = sb("mv1", [P, TILES, 2])
        ve1 = sb("ve1", [P, TILES])
        rs1 = sb("rs1", [P, TILES])
        neg1 = sb("neg1", [P, TILES])
        shift1 = sb("shift1", [P, TILES])
        mv2 = sb("mv2", [P, TILES, 2])
        ve2 = sb("ve2", [P, TILES])
        rs2 = sb("rs2", [P, TILES])
        neg2 = sb("neg2", [P, TILES])
        shift2 = sb("shift2", [P, TILES])
        xn = sb("xn", [P, TILES, D])
        xT = sb("xT", [P, NODES])
        hT = [sb(f"h{q}T", [P, NODES]) for q in range(2)]
        yp = [sb(f"y{p}", [P, TILES, D], BF16) for p in range(PARTS)]
        y_rest = sb("y_rest", [P, NODES])
        rdeg = sb("rdeg", [P, NODES])
        deg = sb("deg", [P, TILES])
        deg_inv = sb("deg_inv", [P, TILES])
        u = sb("u", [P, NODES])
        v = sb("v", [P, NODES])
        ev = sb("ev", [P, NODES])
        rv = sb("rv", [P, NODES])
        em = sb("em", [P, NODES])
        x2 = [sb(f"x2{q}", [P, TILES, D]) for q in range(2)]
        x2_before = sb("x2_before", [P, TILES, D])
        z = sb("z", [P, TILES, D])
        z_left = sb("z_left", [P, D])
        top = [sb(f"top{q}", [P, FOUND]) for q in range(TILES)]
        top_at = [sb(f"top_at{q}", [P, FOUND], U32) for q in range(TILES)]
        zmax = [sb(f"zmax{q}", [P, TILES]) for q in range(2)]
        hot = sb("hot", [P, FOUND, P], BF16)
        hotT = [sb(f"hotT{q}", [P, FOUND, P], BF16) for q in range(2)]
        acc = [[sb(f"acc{q}{r}", [P, FFN]) for r in range(2)] for q in range(2)]
        beyond = sb("beyond", [P, FFN], BF16)
        open_n = sb("open_n", [P, TILES])
        fl_a = sb("fl_a", [P, TILES])
        fl_b = sb("fl_b", [P, TILES])
        outside = sb("outside", [P, NCOLS])
        flags = sb("flags", [P, NCOLS])
        tT = [sb(f"tT{q}", [P, CHUNKS, NODES]) for q in range(2)]
        zT = sb("zT", [P, NODES])
        cl = [sb(f"cl{c}", [P, NODES]) for c in range(CHUNKS)]
        gt = [sb(f"gt{c}", [P, NODES]) for c in range(CHUNKS)]
        line = [sb(f"line{n}", [P, NODES]) for n in range(2 * SLOTS)]
        cvx = [sb(f"cvx{q}", [P, NODES]) for q in range(2)]
        ccv = [sb(f"ccv{q}", [P, NODES]) for q in range(2)]
        trop = sb("trop", [P, NODES])
        diff = sb("diff", [P, NODES])
        fused = [sb(f"fused{c}", [P, NODES]) for c in range(CHUNKS)]
        o_s = sb("o_s", [P, TILES, D])

        fb = sb("fb", [P, NCOLS], BF16)
        ff = sb("ff", [P, NCOLS])
        tot = [sb(f"tot{q}", [P, NCOLS]) for q in range(2)]
        total = sb("total", [P, NCOLS])
        rk = sb("rk", [P, NCOLS])
        rk_i = sb("rk_i", [P, NCOLS], I32)
        rk_c_i = sb("rk_c_i", [P, NCOLS], I32)
        rk_s_i = sb("rk_s_i", [P, NCOLS], I32)
        rk_c = sb("rk_c", [P, NCOLS])
        rk_s = sb("rk_s", [P, NCOLS])
        tok_i = sb("tok_i", [P, NCOLS], I32)
        tok = sb("tok", [P, NCOLS])
        n_tiles_f = sb("n_tiles_f", [P, 1])
        n_tiles_i = sb("n_tiles_i", [P, 1], I32)
        n_tiles_m = sb("n_tiles_m", [P, 1], I32)
        at_slot = tT[0][:].rearrange("p c (a b) -> p (c a) b", b=P)
        at_tile = [w[:, p * NCOLS:(p + 1) * NCOLS] for w in (u, v) for p in range(RING // 2)]
        got = sb("got", [P, NCOLS])
        hole = sb("hole", [P, NCOLS])
        src = sb("src", [P, NCOLS])
        dst = sb("dst", [P, NCOLS])
        src_i = sb("src_i", [P, 1], U32)
        dst_i = sb("dst_i", [P, 1], U32)
        g_x = sb("g_x", [P, D])
        g_st = sb("g_st", [P, 6])
        g_mv = sb("g_mv", [P, 2])
        g_ve = sb("g_ve", [P, 1])
        g_rs = sb("g_rs", [P, 1])
        g_z = sb("g_z", [P, D])
        g_zT = sb("g_zT", [P, P])
        g_acc = acc[0]
        g_tT, g_cl, g_gt, g_fu = [w[:].rearrange("p (c n) -> p c n", c=CHUNKS) for w in (line[0], cl[0], gt[0], fused[0])]
        g_pw = [line[1 + q][:].rearrange("p (c n) -> p c n", c=CHUNKS) for q in range(2)]
        g_convex = [line[3 + q][:].rearrange("p (c n) -> p c n", c=CHUNKS) for q in range(4)]
        g_concave = [w[:].rearrange("p (c n) -> p c n", c=CHUNKS) for w in (line[7], cvx[0])]
        g_top = sb("g_top", [P, DEEP])
        g_at = sb("g_at", [P, DEEP], U32)
        g_left = [z_left, sb("g_left", [P, D])]
        g_open = sb("g_open", [P, 1])
        g_any = sb("g_any", [P, 1])
        g_anyb = sb("g_anyb", [P, 1], BF16)
        g_any_f = sb("g_any_f", [P, 1])
        g_any_i = sb("g_any_i", [P, 1], I32)
        g_mark = [sb(f"g_mark{q}", [P, 1]) for q in range(2)]
        g_o = sb("g_o", [P, D])

        x2_dram = nc.dram_tensor("x2_rows", [BATCHES * NODES, D], F32, kind="Internal").ap()

        G = [bank(f"gathered{q}") for q in range(3)]
        H = bank("hot_bank", (P, 1024), BF16)
        P1 = bank("gnn_bank1")
        P2 = bank("gnn_bank2")
        T = bank("transpose_bank")
        FB = bank("ffn_bank")

        s_const = sem("constants_made")
        s_wload = sem("weights_loaded")
        s_wtf = sem("wt_parts_made")
        s_wT = sem("wc_wg_transposed")
        s_wTc = sem("wc_wg_transposed_copied")
        s_key = sem("keys_made")
        s_keyr = sem("keys_spread")
        s_perm = sem("order_made")
        s_table = sem("table_made")
        s_put = sem("put_in_order")
        s_putc = sem("put_in_order_copied")
        s_share = sem("tanh_alpha")
        s_setup_dve = sem("setup_dve")
        s_setup_done = sem("setup_done")
        s_over = sem("over_counted")
        s_xin = [sem(f"x_in{q}") for q in range(2)]
        s_adjin = [sem(f"adj_in{q}") for q in range(2)]
        s_mask = sem("mask_made")
        s_ln1_st = sem("ln1_stats")
        s_ln1_mv = sem("ln1_meanvar")
        s_ln1_rs = sem("ln1_scale_shift")
        s_xn = sem("xn_ready")
        s_p1 = sem("gnn_bank1_full")
        s_p2 = sem("gnn_bank2_full")
        s_xT = sem("xT_ready")
        s_yhi = sem("y_hi")
        s_yrest = sem("y_rest")
        s_ymid = sem("y_mid")
        s_ylo = sem("y_lo")
        s_deg = sem("degree")
        s_rdeg = sem("inverse_degree_copied")
        s_u = sem("u_ready")
        s_v = sem("v_ready")
        s_eluact = sem("elu_exp_relu")
        s_h = sem("h_ready")
        s_x2 = sem("x2_ready")
        s_ln2_st = sem("ln2_stats")
        s_ln2_mv = sem("ln2_meanvar")
        s_ln2_rs = sem("ln2_scale_shift")
        s_z = sem("z_ready")
        s_top = sem("top_found")
        s_zmax = sem("zmax_kept")
        s_hot = sem("hot_made")
        s_H = sem("hot_bank_full")
        s_hotT = sem("hotT_copied")
        s_gath = sem("round_gathered")
        s_round = sem("round_done")
        s_merged = sem("even_odd_merged")
        s_open = sem("open_counted")
        s_flags = sem("flags_ready")
        s_T = sem("transpose_bank_full")
        s_Tc = sem("transpose_bank_copied")
        s_F = sem("ffn_bank_full")
        s_Fa = sem("gelu_tanh_done")
        s_gate = sem("gate_ready")
        s_line = sem("line_ready")
        s_pwl = sem("pwl_step")
        s_trop = sem("trop_step")
        s_fused = sem("fused_ready")
        s_keep = sem("x2_kept")
        s_out = sem("out_summed")
        s_outd = sem("out_stored")
        s_x2d = sem("x2_stored")
        q_dve = sem("g_dve")
        q_rank = sem("g_flags_counted")
        q_fb = sem("g_flags_bf16")
        q_hot = sem("g_one_hots")
        q_hotu = sem("g_one_hots_used")
        q_list = sem("g_list")
        q_n = sem("g_tiles_known")
        q_anyb = sem("g_any_open_bf16")
        q_anyc = sem("g_any_open_counted")
        q_any = sem("g_any_open")
        deep = Pass(sem, "deep", 3, 2, 2 + len(EXTRA))
        full = Pass(sem, "full", LINES, LINES, 2 * (LINES - 1))

        x_t = x.rearrange("b (j p) d -> b p j d", p=P)
        adj_t = adj.rearrange("b (j p) m -> b p j m", p=P)
        out_t = out.rearrange("b (j p) d -> b p j d", p=P)
        out_rows = out.rearrange("b n d -> (b n) d")
        x2_t = x2_dram.rearrange("(b j p) d -> b p j d", j=TILES, p=P)
        weight_loads = [
            (w_root[0][:], w_root1), (w_root[1][:], w_root2), (w_rel[0][:], w_rel1[1]), (w_rel[1][:], w_rel2[1]),
            (bias[0][:], b1.rearrange("(p o) -> p o", o=1)), (bias[1][:], b2.rearrange("(p o) -> p o", o=1)),
            (wt_f[:], Wt.rearrange("(c p) d -> p c d", p=P)),
            (wc[:], Wc), (wg[:], Wg), (wd[:], Wd.rearrange("(c p) d -> p c d", p=P)),
            (bc_s[:], bc.rearrange("(c p) -> p c", p=P)), (bg_s[:], bg.rearrange("(c p) -> p c", p=P)),
            (bt_s[:], bt.rearrange("(c p) -> p c", p=P)), (al[:], alpha.rearrange("(c p) -> p c", p=P)),
            (bd_s[0:1, :], bd.rearrange("(o d) -> o d", o=1)),
            (slope[:, 0:CHUNKS, :], sl_cvx.rearrange("(c p) q -> p c q", p=P)),
            (slope[:, CHUNKS:FC, :], sl_ccv.rearrange("(c p) q -> p c q", p=P)),
            (offs[:, 0:CHUNKS, :], of_cvx.rearrange("(c p) q -> p c q", p=P)),
            (offs[:, CHUNKS:FC, :], of_ccv.rearrange("(c p) q -> p c q", p=P)),
        ]
        LOADED = 16 * len(weight_loads)
        N_CONST = 14
        ALL_STEPS, ALL_DRAWN = sum(STEPS), sum(DRAWN)
        perm = fused
        work = [u, v, ev, rv, em]

        def bank_rounds_before(i, at):
            return at.b * ROUNDS + i - 2

        assert ROUNDS % 3 == 0
        block = ctx.enter_context(nc.Block())

        @block.sync
        def _(sp):
            def load_x(at):
                wait(sp, s_x2, at.b - 1)
                sp.dma_start(xs[at.parity][:], x_t[at.b]).then_inc(s_xin[at.parity], 16)

            def load_adj(at):
                wait(sp, s_mask, at.b - 1)
                sp.dma_start(adjs[at.parity][:], adj_t[at.b]).then_inc(s_adjin[at.parity], 16)

            def store_x2(at):
                sp.wait_ge(s_x2, at.b + 1)
                sp.dma_start(x2_t[at.b], x2[at.parity][:]).then_inc(s_x2d, 16)

            def store_out(at):
                sp.wait_ge(s_out, at.b + 1)
                sp.dma_start(out_t[at.b], o_s[:]).then_inc(s_outd, 16)

            def tick(at, finish, gnn, load):
                if load:
                    load_adj(at.plus(3))
                if gnn:
                    store_x2(at.plus(1))
                if load:
                    load_x(at.plus(3))
                if finish:
                    store_out(at.plus(-1))

            load_x(fixed(0))
            load_adj(fixed(0))
            sp.wait_ge(s_const, N_CONST)
            for to, of in weight_loads:
                sp.dma_start(to, of, allow_slow_non_contiguous=True).then_inc(s_wload, 16)
            load_x(fixed(1))
            load_adj(fixed(1))
            load_adj(fixed(2))
            store_x2(fixed(0))
            load_x(fixed(2))
            tick(fixed(0), False, True, True)
            tick(fixed(1), True, True, True)
            with sp.Fori(0, 5) as i:
                tick(At(i * 2 + 2, 0, i + 1), True, True, True)
                tick(At(i * 2 + 3, 1, i + 1), True, True, True)
            tick(fixed(12), True, True, True)
            tick(fixed(13), True, True, False)
            tick(fixed(14), True, True, False)
            tick(fixed(15), True, False, False)
            store_out(fixed(15))
            sp.wait_ge(s_outd, 16 * BATCHES)
            sp.wait_ge(s_x2d, 16 * BATCHES)

        @block.gpsimd
        def _(pool):
            pool.memset(ident[:], 0.0).then_inc(s_const, 1)
            pool.memset(identb[:], 0.0).then_inc(s_const, 1)
            pool.memset(onesb[:], 1.0).then_inc(s_const, 1)
            pool.memset(below[:], 1.0).then_inc(s_const, 1)
            pool.memset(row0[:], 1.0).then_inc(s_const, 1)
            pool.memset(zerof[:], 0.0).then_inc(s_const, 1)
            pool.memset(bd_s[:], 0.0).then_inc(s_const, 1)
            pool.memset(minus_half[:], -0.5).then_inc(s_const, 1)
            pool.memset(unit[:], 1.0).then_inc(s_const, 1)
            pool.memset(half[:], 0.5).then_inc(s_const, 1)
            pool.wait_ge(s_const, 10)
            pool.affine_select(out=ident[:], in_=ident[:], compare_op=ALU.not_equal, fill=1.0, base=0,
                               pattern=[[-1, P]], channel_multiplier=1).then_inc(s_const, 1)
            pool.affine_select(out=identb[:], in_=identb[:], compare_op=ALU.not_equal, fill=1.0, base=0,
                               pattern=[[-1, P]], channel_multiplier=1).then_inc(s_const, 1)
            pool.affine_select(out=below[:], in_=below[:], compare_op=ALU.is_gt, fill=0.0, base=0,
                               pattern=[[1, P]], channel_multiplier=-1).then_inc(s_const, 1)
            pool.affine_select(out=row0[:], in_=row0[:], compare_op=ALU.is_ge, fill=0.0, base=0,
                               pattern=[[0, P]], channel_multiplier=-1).then_inc(s_const, 1)
            pool.iota(iota_i[:], pattern=[[1, P]], base=0, channel_multiplier=0).then_inc(s_const, 1)
            pool.iota(place_i[:], pattern=[[1, FFN]], base=0, channel_multiplier=0).then_inc(s_const, 1)
            pool.iota(tok_i[:], pattern=[[P, NCOLS]], base=1, channel_multiplier=1).then_inc(s_const, 1)
            pool.wait_ge(s_const, N_CONST + 3)
            pool.tensor_copy(iota[:], iota_i[:]).then_inc(s_const, 1)
            pool.tensor_copy(tok[:], tok_i[:]).then_inc(s_const, 1)
            pool.wait_ge(s_const, N_CONST + 5)

            def make_mask(at):
                pool.wait_ge(s_adjin[at.parity], 16 * (at.half + 1))
                wait_apart(pool, s_p1, 6 * (at.b - 1) + 5, s_const)
                pool.tensor_scalar(mask[:], adjs[at.parity][:], 1, None, ALU.is_equal).then_inc(s_mask, 1)

            def scale_shift(at, meanvar, s_mv, ve, neg, rs, shift, s_rs):
                wait_apart(pool, s_mv, at.b + 1, s_const)
                pool.tensor_scalar(ve[:], meanvar[:, :, 1], EPS, None, ALU.add).then_inc(s_rs, 1)
                pool.tensor_scalar(neg[:], meanvar[:, :, 0], -1.0, None, ALU.mult).then_inc(s_rs, 1)
                pool.wait_ge(s_rs, 4 * at.b + 1)
                pool.tensor_tensor(rs[:], ve[:], minus_half[:], ALU.pow).then_inc(s_rs, 1)
                pool.wait_ge(s_rs, 4 * at.b + 3)
                pool.tensor_tensor(shift[:], neg[:], rs[:], ALU.mult).then_inc(s_rs, 1)

            def one_hots(at, j, groups=(0, 1)):
                tile = at.b * TILES + j
                for group in groups:
                    wait_apart(pool, s_top, 5 * tile + (3 if group == 0 else 5), s_const)
                    if group == 0:
                        pool.tensor_copy(zmax[at.parity][:, j:j + 1], top[j][:, 0:1]).then_inc(s_zmax, 1)
                    wait_apart(pool, s_H, 2 * (tile - 1) + group + 1, s_const)
                    for k in range(8 * group, min(8 * group + 8, TOP)):
                        last = pool.tensor_scalar(hot[:, k, :], iota[:], top_at[j][:, k:k + 1], None, ALU.is_equal)
                    last.then_inc(s_hot, 1)

            def fuse(at, c):
                pool.wait_ge(s_pwl, ALL_STEPS * at.b + sum(STEPS[:c + 1]))
                wait(pool, s_fused, 4 * at.b + c)
                pool.tensor_tensor(trop[:], cvx[c % 2][:], ccv[c % 2][:], ALU.subtract).then_inc(s_trop, 1)
                pool.wait_ge(s_trop, 12 * at.b + 3 * c + 1)
                pool.tensor_tensor(diff[:], trop[:], cl[c][:], ALU.subtract).then_inc(s_trop, 1)
                pool.wait_ge(s_trop, 12 * at.b + 3 * c + 2)
                pool.wait_ge(s_gate, 4 * at.b + c + 1)
                pool.tensor_tensor(trop[:], diff[:], gt[c][:], ALU.mult).then_inc(s_trop, 1)
                pool.wait_ge(s_trop, 12 * at.b + 3 * c + 3)
                wait(pool, s_F, 9 * at.b)
                pool.tensor_tensor(fused[c][:], trop[:], cl[c][:], ALU.add).then_inc(s_fused, 1)

            def note(at):
                wait_apart(pool, s_zmax, 4 * at.b + 4, s_const)
                pool.tensor_scalar(fl_a[:], zmax[at.parity][:], Z_LO, over_all[:], ALU.is_lt, ALU.add).then_inc(s_flags, 1)
                pool.tensor_scalar(fl_b[:], zmax[at.parity][:], Z_HI, None, ALU.is_gt).then_inc(s_flags, 1)
                pool.wait_ge(s_flags, 4 * at.b + 2)
                columns = bass.ds(at.b * TILES, TILES)
                pool.tensor_tensor(outside[:, columns], fl_a[:], fl_b[:], ALU.add).then_inc(s_flags, 1)
                pool.wait_ge(s_flags, 4 * at.b + 3)
                pool.wait_ge(s_open, 4 * at.b + 4)
                pool.tensor_tensor(flags[:, columns], outside[:, columns], open_n[:], ALU.add)\
                    .then_inc(s_flags, 1)

            def tick(at, finish, gnn, ahead):
                before, after = at.plus(-1), at.plus(1)
                if finish:
                    note(before)
                one_hots(at, 2)
                if finish:
                    fuse(before, 0)
                if ahead:
                    scale_shift(at.plus(2), mv1, s_ln1_mv, ve1, neg1, rs1, shift1, s_ln1_rs)
                one_hots(at, 3, (0,))
                if finish:
                    fuse(before, 1)
                one_hots(at, 3, (1,))
                if ahead:
                    make_mask(at.plus(2))
                if finish:
                    fuse(before, 2)
                if gnn:
                    scale_shift(after, mv2, s_ln2_mv, ve2, neg2, rs2, shift2, s_ln2_rs)
                if finish:
                    fuse(before, 3)
                if gnn:
                    one_hots(after, 0)
                    one_hots(after, 1)

            make_mask(fixed(0))
            scale_shift(fixed(0), mv1, s_ln1_mv, ve1, neg1, rs1, shift1, s_ln1_rs)
            make_mask(fixed(1))
            scale_shift(fixed(0), mv2, s_ln2_mv, ve2, neg2, rs2, shift2, s_ln2_rs)
            scale_shift(fixed(1), mv1, s_ln1_mv, ve1, neg1, rs1, shift1, s_ln1_rs)
            one_hots(fixed(0), 0)
            one_hots(fixed(0), 1)
            pool.wait_ge(s_over, 2)
            tick(fixed(0), False, True, True)
            tick(fixed(1), True, True, True)
            with pool.Fori(0, 5) as i:
                tick(At(i * 2 + 2, 0, i + 1), True, True, True)
                tick(At(i * 2 + 3, 1, i + 1), True, True, True)
            tick(fixed(12), True, True, True)
            tick(fixed(13), True, True, True)
            tick(fixed(14), True, True, False)
            tick(fixed(15), True, False, False)
            note(fixed(15))
            for c in range(CHUNKS):
                fuse(fixed(15), c)

            pool.wait_ge(q_n, 1)
            tiles = pool.value_load(n_tiles_m[0:1, 0:1], min_val=1, max_val=NCOLS)
            pool.wait_ge(s_x2d, 16 * BATCHES)
            pool.wait_ge(s_outd, 16 * BATCHES)

            def general(g, s, mark):
                wait_apart(pool, s.idx, g * 2 + 2, s_const)
                pool.indirect_dma_start(out=g_x[:], out_offset=None, in_=x2_dram,
                                        in_offset=bass.IndirectOffsetOnAxis(ap=src_i[:], axis=0))\
                    .then_inc(s.rows, 16)
                wait_apart(pool, s.mv, g + 1, s_const)
                pool.tensor_scalar(g_ve[:], g_mv[:, 1:2], EPS, None, ALU.add).then_inc(s.rs, 1)
                pool.wait_ge(s.rs, g * 2 + 1)
                pool.tensor_tensor(g_rs[:], g_ve[:], minus_half[:, 0:1], ALU.pow).then_inc(s.rs, 1)
                if s is deep:
                    for q in range(2, GROUPS):
                        wait_apart(pool, s.top, g * (3 * GROUPS - 1) + 3 * q + 2, s_const)
                        wait_apart(pool, s.H, g * GROUPS + q - 1, s_const)
                        for k in range(8):
                            last = pool.tensor_scalar(hot[:, 8 * (q % 2) + k, :], iota[:],
                                                      g_at[:, 8 * q + k:8 * q + k + 1], None, ALU.is_equal)
                        last.then_inc(s.hot, 1)
                wait_apart(pool, s.os, g + 1, s_const)
                pool.indirect_dma_start(out=out_rows, in_=g_o[:], in_offset=None,
                                        out_offset=bass.IndirectOffsetOnAxis(ap=dst_i[:], axis=0),
                                        bounds_check=BATCHES * NODES - 1, oob_is_err=False)\
                    .then_inc(s.stored, 16)
                wait_apart(pool, s.stored, g * 16 + 16, s_const)
                pool.memset(mark[:], 0.0).then_inc(s.free, 1)

            pool.memset(g_mark[0][:], 0.0).then_inc(deep.free, 1)
            with pool.Fori(0, tiles) as g:
                general(g, deep, g_mark[0])
            pool.wait_ge(q_any, 1)
            some = pool.value_load(g_any_i[0:1, 0:1], min_val=0, max_val=1)
            with pool.If(some > 0):
                pool.memset(g_mark[1][:], 0.0).then_inc(full.free, 1)
                with pool.Fori(0, tiles) as g:
                    general(g, full, g_mark[1])

        @block.tensor
        def _(pe):
            def gnn_x_transposed(at):
                pe.wait_ge(s_xn, at.b + 1)
                wait(pe, s_x2, at.b)
                for j in range(TILES):
                    last = pe.transpose(P1[:, j * P:(j + 1) * P], xn[:, j, :], ident[:])
                last.then_inc(s_p1, 1)

            def gnn_y(at, layer):
                h = (xT, hT[0])[layer]
                if layer == 0:
                    pe.wait_ge(s_xT, at.b + 1)
                else:
                    pe.wait_ge(s_h, 2 * at.b + 1)
                    pe.wait_ge(s_u, 2 * at.b + 1)
                for j in range(TILES):
                    last = pe.matmul(P1[:, j * P:(j + 1) * P], h[:, j * P:(j + 1) * P], w_rel[layer][:],
                                     start=True, stop=True)
                last.then_inc(s_p1, 1)

            def gnn_degree(at):
                pe.wait_ge(s_mask, at.b + 1)
                wait(pe, s_v, 2 * at.b)
                for j in range(TILES):
                    for i in range(TILES):
                        last = pe.matmul(P2[:, j:j + 1], mask[:, i, j * P:(j + 1) * P], onesb[:, 0:1],
                                         start=(i == 0), stop=(i == TILES - 1))
                last.then_inc(s_p2, 1)

            def gnn_spread(at):
                pe.wait_ge(s_deg, 2 * at.b + 2)
                for j in range(TILES):
                    last = pe.matmul(P2[:, j * P:(j + 1) * P], deg_inv[:, j:j + 1].to_broadcast([P, P]), ident[:],
                                     start=True, stop=True)
                last.then_inc(s_p2, 1)

            def gnn_root(at, layer):
                h = (xT, hT[0])[layer]
                if layer == 0:
                    pe.wait_ge(s_rdeg, at.b + 1)
                else:
                    pe.wait_ge(s_v, 2 * at.b + 1)
                pe.matmul(P2[:], w_root[layer][:], h[:], start=True, stop=True).then_inc(s_p2, 1)

            def gnn_aggregate(at, layer, i):
                if i == 0:
                    pe.wait_ge(s_yhi, 2 * at.b + layer + 1)
                    pe.wait_ge(s_yrest, 2 * at.b + layer + 1)
                    pe.wait_ge(s_ymid, 2 * at.b + layer + 1)
                    pe.wait_ge(s_ylo, 2 * at.b + layer + 1)
                for part in range(PARTS):
                    last = pe.matmul(P1[:], yp[part][:, i, :], mask[:, i, :],
                                     start=(i == 0 and part == 0), stop=(i == TILES - 1 and part == PARTS - 1))
                if i == TILES - 1:
                    last.then_inc(s_p1, 1)

            def gnn_back(at):
                pe.wait_ge(s_h, 2 * at.b + 2)
                pe.wait_ge(s_u, 2 * at.b + 2)
                for j in range(TILES):
                    last = pe.transpose(P1[:, j * P:(j + 1) * P], hT[1][:, j * P:(j + 1) * P], ident[:])
                last.then_inc(s_p1, 1)

            def transpose_hots(at, j, group):
                pair = 2 * (at.b * TILES + j) + group
                pe.wait_ge(s_hot, pair + 1)
                wait(pe, s_hotT, pair)
                for k in range(min(8, TOP - 8 * group)):
                    last = pe.transpose(H[:, k * P:(k + 1) * P], hot[:, 8 * group + k, :], identb[:])
                last.then_inc(s_H, 1)

            def transpose_t(at, j):
                pe.wait_ge(s_merged, at.b * TILES + j + 1)
                event = at.b * T_EVENTS + T_OF_TILE[j]
                wait(pe, s_Tc, event)
                for c in range(CHUNKS):
                    last = pe.transpose(T[:, c * P:(c + 1) * P], acc[j % 2][0][:, c * P:(c + 1) * P], ident[:])
                last.then_inc(s_T, 1)

            def transpose_z(at):
                pe.wait_ge(s_z, at.b + 1)
                wait(pe, s_Tc, at.b * T_EVENTS + T_OF_Z)
                for j in range(TILES):
                    last = pe.transpose(T[:, j * P:(j + 1) * P], z[:, j, :], ident[:])
                last.then_inc(s_T, 1)

            def ffn_in(at, n):
                if n == 0:
                    pe.wait_ge(s_Tc, at.b * T_EVENTS + T_OF_Z + 1)
                    wait(pe, s_out, at.b)
                wait(pe, s_Fa, 8 * at.b + n)
                w, c = (wc, wg)[n % 2], n // 2
                pe.matmul(FB[:], w[:, c * P:(c + 1) * P], zT[:], start=True, stop=True).then_inc(s_F, 1)

            def ffn_out(at, j):
                if j == 0:
                    pe.wait_ge(s_fused, 4 * at.b + 4)
                    pe.wait_ge(s_Fa, 8 * at.b + 8)
                o = FB[:, j * P:(j + 1) * P]
                pe.matmul(o, row0[:], bd_s[:], start=True, stop=False)
                for c in range(CHUNKS):
                    last = pe.matmul(o, fused[c][:, j * P:(j + 1) * P], wd[:, c, :],
                                     start=False, stop=(c == CHUNKS - 1))
                if j == TILES - 1:
                    last.then_inc(s_F, 1)

            def tick(at, finish, gnn, ahead):
                before, after, second = at.plus(-1), at.plus(1), at.plus(2)
                for i in range(ROUNDS):
                    j, k = divmod(i, TOP)
                    if k % 8 == 0:
                        pe.wait_ge(s_hotT, 2 * (at.b * TILES + j) + k // 8 + 1)
                    wait(pe, s_round, bank_rounds_before(i, at))
                    for part in range(PARTS):
                        last = pe.matmul(G[i % 3][:], hotT[j % 2][:, k, :], wt[part][:],
                                         start=(part == 0), stop=(part == PARTS - 1))
                    last.then_inc(s_gath, 1)
                    if i in PE_HOTS:
                        transpose_hots(at, *PE_HOTS[i])
                    if gnn and i in PE_HOTS_AFTER:
                        transpose_hots(after, 0, PE_HOTS_AFTER[i])
                    if finish and i == PE_T_BEFORE:
                        transpose_t(before, TILES - 1)
                    if i in PE_T:
                        transpose_t(at, PE_T[i])
                    if i == PE_Z:
                        transpose_z(at)
                    if finish and i in PE_FFN_IN:
                        ffn_in(before, PE_FFN_IN.index(i))
                    if finish and i in PE_FFN_OUT:
                        ffn_out(before, PE_FFN_OUT.index(i))
                    if gnn and i in PE_AGG1:
                        gnn_aggregate(after, 0, PE_AGG1.index(i))
                    if gnn and i == PE_Y2:
                        gnn_y(after, 1)
                    if gnn and i == PE_ROOT2:
                        gnn_root(after, 1)
                    if gnn and i in PE_AGG2:
                        gnn_aggregate(after, 1, PE_AGG2.index(i))
                    if gnn and i == PE_BACK:
                        gnn_back(after)
                    if ahead and i == PE_X:
                        gnn_x_transposed(second)
                    if ahead and i == PE_Y1:
                        gnn_y(second, 0)
                    if ahead and i == PE_DEGREE:
                        gnn_degree(second)
                    if ahead and i == PE_SPREAD:
                        gnn_spread(second)
                    if ahead and i == PE_ROOT1:
                        gnn_root(second, 0)

            first, next_ = fixed(0), fixed(1)
            pe.wait_ge(s_wload, LOADED)
            pe.wait_ge(s_const, N_CONST + 5)
            for to, w in ((FB, wc), (T, wg)):
                for c in range(CHUNKS):
                    last = pe.transpose(to[:, c * P:(c + 1) * P], w[:, c * P:(c + 1) * P], ident[:])
                last.then_inc(s_wT, 1)
            gnn_x_transposed(first)
            gnn_y(first, 0)
            gnn_degree(first)
            gnn_spread(first)
            gnn_root(first, 0)
            for i in range(TILES):
                gnn_aggregate(first, 0, i)
            pe.wait_ge(s_key, 1)
            for c in range(CHUNKS):
                last = pe.matmul(G[0][:, c * P:(c + 1) * P], key[:, c:c + 1].to_broadcast([P, P]), ident[:],
                                 start=True, stop=True)
            last.then_inc(s_keyr, 1)
            gnn_y(first, 1)
            gnn_root(first, 1)
            pe.wait_ge(s_wtf, 1)
            pe.wait_ge(s_perm, 1)
            pe.wait_ge(s_wTc, 2)
            for part in range(PARTS):
                for c in range(CHUNKS):
                    last = pe.matmul(G[part][:], wt_fp[part][:, c, :], permb[:, c, :],
                                     start=(c == 0), stop=(c == CHUNKS - 1))
                last.then_inc(s_put, 1)
            for to, w in ((FB, wcT), (T, wgT)):
                for c in range(CHUNKS):
                    last = pe.matmul(to[:], w[:, c, :], perm[c][:], start=(c == 0), stop=(c == CHUNKS - 1))
                last.then_inc(s_put, 1)
                if to is FB:
                    for i in range(TILES):
                        gnn_aggregate(first, 1, i)
            pe.wait_ge(s_putc, 1)
            for c in range(CHUNKS):
                last = pe.matmul(G[0][:], wmax[:, c:c + 1].to_broadcast([P, P]), perm[c][:],
                                 start=(c == 0), stop=(c == CHUNKS - 1))
            last.then_inc(s_put, 1)
            gnn_back(first)
            pe.wait_ge(s_putc, 2)
            for m in range(CHUNKS):
                for c in range(CHUNKS):
                    last = pe.matmul(G[1][:, m * P:(m + 1) * P], perm[c][:, m * P:(m + 1) * P], wd[:, c, :],
                                     start=(c == 0), stop=(c == CHUNKS - 1))
            last.then_inc(s_put, 1)
            pe.wait_ge(s_putc, 3)
            pe.wait_ge(s_table, 1)
            for m in range(CHUNKS):
                for c in range(CHUNKS):
                    last = pe.matmul(G[2][:, m * V_COLS:(m + 1) * V_COLS], perm[c][:, m * P:(m + 1) * P],
                                     table[:, c, :], start=(c == 0), stop=(c == CHUNKS - 1))
            last.then_inc(s_put, 1)
            gnn_x_transposed(next_)
            gnn_degree(next_)
            pe.wait_ge(s_putc, 8)
            pe.wait_ge(s_setup_done, 1)
            pe.matmul(T[:, 0:1], onesb[:], over1b[:], start=True, stop=True).then_inc(s_over, 1)
            transpose_hots(first, 0, 0)
            gnn_y(next_, 0)
            gnn_spread(next_)
            transpose_hots(first, 0, 1)
            gnn_root(next_, 0)
            pe.wait_ge(s_over, 2)
            tick(first, False, True, True)
            tick(fixed(1), True, True, True)
            with pe.Fori(0, 5) as i:
                tick(At(i * 2 + 2, 0, i + 1), True, True, True)
                tick(At(i * 2 + 3, 1, i + 1), True, True, True)
            tick(fixed(12), True, True, True)
            tick(fixed(13), True, True, True)
            tick(fixed(14), True, True, False)
            tick(fixed(15), True, False, False)
            transpose_t(fixed(15), TILES - 1)

            ffn_in(fixed(15), 0)
            pe.wait_ge(q_fb, 1)
            pe.matmul(P2[:, 0:NCOLS], below[:], fb[:], start=True, stop=True)
            pe.matmul(P2[:, NCOLS:2 * NCOLS], onesb[:], fb[:], start=True, stop=True).then_inc(q_rank, 1)
            pe.matmul(P1[:, 0:NCOLS], zerof[:], zerof[:, 0:NCOLS], start=True, stop=False).then_inc(q_hotu, RING)
            ffn_in(fixed(15), 1)
            for i in range(NCOLS // RING):
                if i == 1:
                    for n in range(2, 2 * CHUNKS):
                        ffn_in(fixed(15), n)
                for q in range(RING):
                    pe.wait_ge(q_hot, i * RING + q + 1)
                    pe.matmul(P1[:, 0:NCOLS], at_slot[:, q, :], at_tile[q], start=False, stop=False)\
                        .then_inc(q_hotu, 1)
            pe.matmul(P1[:, 0:NCOLS], zerof[:], zerof[:, 0:NCOLS], start=False, stop=True).then_inc(q_list, 1)
            for j in range(TILES):
                ffn_out(fixed(15), j)

            pe.wait_ge(q_n, 1)
            tiles = pe.value_load(n_tiles_m[0:1, 0:1], min_val=1, max_val=NCOLS)
            pe.wait_ge(s_out, BATCHES)

            def ffn_product(g, s, n):
                if n == 0:
                    pe.wait_ge(s.zT, g + 1)
                    pe.wait_ge(s.free, g + 1)
                else:
                    pe.wait_ge(s.Fa, g * 2 + 1)
                for c in range(CHUNKS):
                    last = pe.matmul(FB[:, c * P:(c + 1) * P], (wc, wg)[n][:, c * P:(c + 1) * P], g_zT[:],
                                     start=True, stop=True)
                last.then_inc(s.F, 1)

            def gather_deep(g, s):
                def transpose_group(q):
                    pe.wait_ge(s.hot, g * GROUPS + q + 1)
                    if q:
                        pe.wait_ge(s.hotT, g * GROUPS + q)
                    for k in range(8):
                        last = pe.transpose(H[:, k * P:(k + 1) * P], hot[:, 8 * (q % 2) + k, :], identb[:])
                    last.then_inc(s.H, 1)

                transpose_group(0)
                transpose_group(1)
                for q in range(GROUPS):
                    pe.wait_ge(s.hotT, g * GROUPS + q + 1)
                    for k in range(8):
                        n = 8 * q + k
                        if n >= 3:
                            pe.wait_ge(s.round, g * DEEP + n - 2)
                        for part in range(PARTS):
                            last = pe.matmul(G[n % 3][:], hotT[q // 2][:, 8 * (q % 2) + k, :], wt[part][:],
                                             start=(part == 0), stop=(part == PARTS - 1))
                        last.then_inc(s.gath, 1)
                    if q < 2:
                        transpose_group(q + 2)
                        ffn_product(g, s, q)
                pe.wait_ge(s.merged, g + 1)

            def gather_full(g, s):
                ffn_product(g, s, 0)
                ffn_product(g, s, 1)
                with pe.Fori(0, D // 8) as h:
                    for k in range(8):
                        pe.wait_ge(s.round, g * (D + 2) + h * 8 + k + 1)
                        hot_d = identb[:, bass.ds(h * 8 + k, 1)].to_broadcast([P, P])
                        for part in range(PARTS):
                            last = pe.matmul(G[k % 2][:], hot_d, wt[part][:],
                                             start=(part == 0), stop=(part == PARTS - 1))
                        last.then_inc(s.gath, 1)
                pe.wait_ge(s.round, g * (D + 2) + D + 2)

            def general(g, s, gather):
                pe.wait_ge(s.z, g + 1)
                pe.transpose(T[:, 0:P], g_z[:], ident[:]).then_inc(s.zTp, 1)
                gather(g, s)
                pe.wait_ge(s.zT, g + 1)
                for c in range(CHUNKS):
                    last = pe.transpose(T[:, c * P:(c + 1) * P], g_acc[0][:, c * P:(c + 1) * P], ident[:])
                last.then_inc(s.tTp, 1)
                pe.wait_ge(s.fused, g + 1)
                pe.wait_ge(s.Fa, g * 2 + 2)
                pe.matmul(FB[:, 0:P], row0[:], bd_s[:], start=True, stop=False)
                for c in range(CHUNKS):
                    last = pe.matmul(FB[:, 0:P], g_fu[:, c, :], wd[:, c, :], start=False, stop=(c == CHUNKS - 1))
                last.then_inc(s.o, 1)

            with pe.Fori(0, tiles) as g:
                general(g, deep, gather_deep)
            pe.wait_ge(q_anyb, 1)
            pe.matmul(T[:, 0:1], onesb[:], g_anyb[:], start=True, stop=True).then_inc(q_anyc, 1)
            pe.wait_ge(q_any, 1)
            some = pe.value_load(g_any_i[0:1, 0:1], min_val=0, max_val=1)
            with pe.If(some > 0):
                with pe.Fori(0, tiles) as g:
                    general(g, full, gather_full)

        @block.scalar
        def _(act):
            def normalise(to, rows, rs, shift, s_done):
                for j in range(TILES):
                    last = act.activation(to[:, j, :], rows[:, j, :], ACT.Identity, bias=shift[:, j:j + 1],
                                          scale=rs[:, j:j + 1])
                last.then_inc(s_done, 1)

            def ln1_apply(at):
                act.wait_ge(s_ln1_rs, 4 * at.b + 4)
                wait(act, s_p1, 6 * (at.b - 1) + 1)
                normalise(xn, xs[at.parity], rs1, shift1, s_xn)

            def ln2_apply(at):
                act.wait_ge(s_ln2_rs, 4 * at.b + 4)
                wait(act, s_T, T_EVENTS * (at.b - 1) + T_OF_Z + 1)
                wait(act, s_top, 5 * TILES * at.b)
                normalise(z, x2[at.parity], rs2, shift2, s_z)

            def split_hi(at, layer):
                pe_event = 6 * at.b + (2, 4)[layer]
                act.wait_ge(s_p1, pe_event)
                act.activation(yp[0][:].rearrange("p j d -> p (j d)"), P1[:], ACT.Copy).then_inc(s_yhi, 1)

            def split_mid(at, layer):
                act.wait_ge(s_yrest, 2 * at.b + layer + 1)
                act.activation(yp[1][:].rearrange("p j d -> p (j d)"), y_rest[:], ACT.Copy).then_inc(s_ymid, 1)

            def elu(at, layer):
                act.wait_ge(s_v, 2 * at.b + layer + 1)
                wait(act, s_h, 2 * at.b + layer)
                act.activation(ev[:], v[:], ACT.Exp, bias=bias[layer][:]).then_inc(s_eluact, 1)
                act.activation(rv[:], v[:], ACT.Relu, bias=bias[layer][:]).then_inc(s_eluact, 1)
                act.wait_ge(s_eluact, 6 * at.b + 3 * layer + 1)
                act.activation(em[:], ev[:], ACT.Relu, bias=unit[:], scale=-1.0).then_inc(s_eluact, 1)

            def copy_inverse_degree(at):
                act.wait_ge(s_p2, 4 * at.b + 2)
                wait(act, s_u, 2 * at.b)
                act.activation(rdeg[:], P2[:], ACT.Copy).then_inc(s_rdeg, 1)

            def keep_x2(at):
                wait(act, s_out, at.b)
                act.activation(x2_before[:].rearrange("p j d -> p (j d)"),
                               x2[at.parity][:].rearrange("p j d -> p (j d)"), ACT.Copy).then_inc(s_keep, 1)

            def copy_xT(at):
                act.wait_ge(s_p1, 6 * at.b + 1)
                act.activation(xT[:], P1[:], ACT.Copy).then_inc(s_xT, 1)

            def copy_hots(at, j, group):
                tile = at.b * TILES + j
                act.wait_ge(s_H, 2 * tile + group + 1)
                wait(act, s_gath, (tile - 1) * TOP)
                end = min(8 * group + 8, TOP)
                act.activation(hotT[j % 2][:, 8 * group:end, :].rearrange("p k n -> p (k n)"),
                               H[:, 0:(end - 8 * group) * P], ACT.Copy).then_inc(s_hotT, 1)

            def copy_t(at, j):
                event = at.b * T_EVENTS + T_OF_TILE[j]
                act.wait_ge(s_T, event + 1)
                act.activation(tT[at.parity][:, :, j * P:(j + 1) * P], T[:].rearrange("p (c n) -> p c n", c=CHUNKS),
                               ACT.Copy).then_inc(s_Tc, 1)

            def copy_z(at):
                act.wait_ge(s_T, at.b * T_EVENTS + T_OF_Z + 1)
                wait(act, s_F, 9 * (at.b - 1) + 8)
                act.activation(zT[:], T[:], ACT.Copy).then_inc(s_Tc, 1)

            def gelu(at, c):
                act.wait_ge(s_F, 9 * at.b + 2 * c + 1)
                wait(act, s_fused, 4 * (at.b - 1) + c + 1)
                act.activation(cl[c][:], FB[:], ACT.Gelu, bias=feat[:, c, V_BC:V_BC + 1]).then_inc(s_Fa, 1)

            def tanh(at, c):
                act.wait_ge(s_F, 9 * at.b + 2 * c + 2)
                act.activation(gt[c][:], FB[:], ACT.Tanh, bias=feat[:, c, V_BG:V_BG + 1], scale=0.5)\
                    .then_inc(s_Fa, 1)
                act.wait_ge(s_Fa, 8 * at.b + 2 * c + 2)
                act.activation(gt[c][:], gt[c][:], ACT.Identity, bias=half[:], scale=0.5).then_inc(s_gate, 1)

            def lines(at, c, start, end):
                if c == 0 and start == 0:
                    act.wait_ge(s_Tc, T_EVENTS * at.b + T_EVENTS)
                for n in range(start, end):
                    slot, func = LINE_ORDER[n]
                    wait(act, s_pwl, ALL_STEPS * at.b + LINE_FREE[c][n])
                    act.activation(line[(c % 2) * 4 + n if c < 3 else n][:], tT[at.parity][:, c, :], ACT.Identity,
                                   bias=feat[:, c, V_SO + 2 * slot + func:V_SO + 2 * slot + func + 1],
                                   scale=feat[:, c, V_SS + 2 * slot + func:V_SS + 2 * slot + func + 1])\
                        .then_inc(s_line, 1)

            LINE_ORDER = [(0, 0), (1, 0), (0, 1), (1, 1)] + [(m, f) for m in range(2, SLOTS) for f in range(2)]
            LINE_FREE = [[-5, -5, -4, -4], [-2, -1, 0, 0], [1, 1, 2, 2], [5, 5, 6, 6, 3, 3, 4, 4]]

            def tick(at, finish, gnn, ahead):
                before, after, second = at.plus(-1), at.plus(1), at.plus(2)
                if finish:
                    keep_x2(before)
                copy_hots(at, 1, 0)
                if finish:
                    copy_t(before, TILES - 1)
                if gnn:
                    elu(after, 0)
                if finish:
                    gelu(before, 0)
                    lines(before, 0, 0, 4)
                copy_hots(at, 1, 1)
                if gnn:
                    split_hi(after, 1)
                if finish:
                    tanh(before, 0)
                    lines(before, 1, 0, 2)
                    gelu(before, 1)
                if gnn:
                    split_mid(after, 1)
                if finish:
                    lines(before, 1, 2, 4)
                    tanh(before, 1)
                copy_hots(at, 2, 0)
                if finish:
                    lines(before, 2, 0, 2)
                copy_t(at, 0)
                if finish:
                    gelu(before, 2)
                    lines(before, 2, 2, 4)
                copy_hots(at, 2, 1)
                if finish:
                    tanh(before, 2)
                    lines(before, 3, 0, 4)
                if gnn:
                    elu(after, 1)
                if finish:
                    gelu(before, 3)
                    lines(before, 3, 4, 8)
                    tanh(before, 3)
                copy_hots(at, 3, 0)
                copy_t(at, 1)
                if ahead:
                    ln1_apply(second)
                copy_hots(at, 3, 1)
                copy_z(at)
                if gnn:
                    ln2_apply(after)
                if ahead:
                    copy_xT(second)
                    split_hi(second, 0)
                    split_mid(second, 0)
                copy_t(at, 2)
                if gnn:
                    copy_hots(after, 0, 0)
                if ahead:
                    copy_inverse_degree(second)
                if gnn:
                    copy_hots(after, 0, 1)

            first, next_ = fixed(0), fixed(1)
            act.wait_ge(s_wload, LOADED)
            act.activation(share[:, 0:CHUNKS], al[:], ACT.Tanh, scale=0.5).then_inc(s_share, 1)
            for n, (to, of) in enumerate(((wcT, FB), (wgT, T))):
                act.wait_ge(s_wT, n + 1)
                act.activation(to[:].rearrange("p c d -> p (c d)"), of[:], ACT.Copy).then_inc(s_wTc, 1)
            ln1_apply(first)
            copy_xT(first)
            split_hi(first, 0)
            split_mid(first, 0)
            copy_inverse_degree(first)
            elu(first, 0)
            split_hi(first, 1)
            puts = [(wt[part][:], G[part][:]) for part in range(PARTS)] + [
                (wc[:], FB[:]), (wg[:], T[:]), (wmax_all[:], G[0][:]),
                (wd[:].rearrange("p c d -> p (c d)"), G[1][:]),
                (feat[:].rearrange("p c v -> p (c v)"), G[2][:, 0:CHUNKS * V_COLS])]
            for n, (to, of) in enumerate(puts):
                if n == 1:
                    split_mid(first, 1)
                if n == 4:
                    elu(first, 1)
                if n == 6:
                    ln2_apply(first)
                act.wait_ge(s_put, n + 1)
                act.activation(to, of, ACT.Copy).then_inc(s_putc, 1)
            ln1_apply(next_)
            copy_xT(next_)
            act.wait_ge(s_over, 1)
            act.activation(over_all[:], T[:, 0:1], ACT.Copy).then_inc(s_over, 1)
            copy_hots(first, 0, 0)
            split_hi(next_, 0)
            copy_inverse_degree(next_)
            split_mid(next_, 0)
            copy_hots(first, 0, 1)
            tick(first, False, True, True)
            tick(fixed(1), True, True, True)
            with act.Fori(0, 5) as i:
                tick(At(i * 2 + 2, 0, i + 1), True, True, True)
                tick(At(i * 2 + 3, 1, i + 1), True, True, True)
            tick(fixed(12), True, True, True)
            tick(fixed(13), True, True, True)
            tick(fixed(14), True, True, False)
            tick(fixed(15), True, False, False)
            keep_x2(fixed(15))
            copy_t(fixed(15), TILES - 1)
            for c in range(CHUNKS):
                gelu(fixed(15), c)
                tanh(fixed(15), c)
                lines(fixed(15), c, 0, DRAWN[c])

            act.wait_ge(q_n, 1)
            tiles = act.value_load(n_tiles_m[0:1, 0:1], min_val=1, max_val=NCOLS)

            def general(g, s, is_deep):
                def copy_group(q):
                    act.wait_ge(s.H, g * GROUPS + q + 1)
                    act.activation(hotT[q // 2][:, 8 * (q % 2):8 * (q % 2) + 8, :].rearrange("p k n -> p (k n)"),
                                   H[:], ACT.Copy).then_inc(s.hotT, 1)

                act.wait_ge(s.zTp, g + 1)
                act.activation(g_zT[:], T[:, 0:P], ACT.Copy).then_inc(s.zT, 1)
                if is_deep:
                    copy_group(0)
                    copy_group(1)
                    copy_group(2)
                act.wait_ge(s.F, g * 2 + 1)
                for c in range(CHUNKS):
                    last = act.activation(g_cl[:, c, :], FB[:, c * P:(c + 1) * P], ACT.Gelu,
                                          bias=feat[:, c, V_BC:V_BC + 1])
                last.then_inc(s.Fa, 1)
                if is_deep:
                    copy_group(3)
                act.wait_ge(s.F, g * 2 + 2)
                for c in range(CHUNKS):
                    last = act.activation(g_gt[:, c, :], FB[:, c * P:(c + 1) * P], ACT.Tanh,
                                          bias=feat[:, c, V_BG:V_BG + 1], scale=0.5)
                last.then_inc(s.Fa, 1)
                act.wait_ge(s.tTp, g + 1)
                act.activation(line[0][:], T[:], ACT.Copy).then_inc(s.tT, 1)
                act.wait_ge(s.tT, g + 1)
                for m in range(2 if is_deep else LINES):
                    if m > 4:
                        act.wait_ge(s.pwl, g * s.pwl_steps + 2 * (m - 5) + 1)
                    to = g_convex[m % 4] if m else g_pw[0]
                    k, o = (V_SS + 2 * m, V_SO + 2 * m) if is_deep else (V_SL + m, V_OF + m)
                    for c in range(CHUNKS):
                        last = act.activation(to[:, c, :], g_tT[:, c, :], ACT.Identity, bias=feat[:, c, o:o + 1],
                                              scale=feat[:, c, k:k + 1])
                    last.then_inc(s.line, 1)
                if is_deep:
                    for e, (c, m, f) in enumerate(EXTRA):
                        k, o = V_SS + 2 * m + f, V_SO + 2 * m + f
                        last = act.activation(g_convex[2 + e // CHUNKS][:, e % CHUNKS, :], g_tT[:, c, :], ACT.Identity,
                                              bias=feat[:, c, o:o + 1], scale=feat[:, c, k:k + 1])
                    last.then_inc(s.line, 1)

            with act.Fori(0, tiles) as g:
                general(g, deep, True)
            act.wait_ge(q_any, 1)
            some = act.value_load(g_any_i[0:1, 0:1], min_val=0, max_val=1)
            with act.If(some > 0):
                with act.Fori(0, tiles) as g:
                    general(g, full, False)

        @block.vector
        def _(dve):
            steps = [0]

            def chain(instruction):
                steps[0] += 1
                instruction.then_inc(s_setup_dve, 1)
                dve.wait_ge(s_setup_dve, steps[0])

            def stats(rows, st, s_st):
                for j in range(TILES):
                    last = dve.bn_stats(st[:, j, :], rows[:, j, :])
                last.then_inc(s_st, 1)

            def meanvar(at, st, s_st, s_mv, mv):
                wait_apart(dve, s_st, at.b + 1, s_wload)
                for j in range(TILES):
                    last = dve.bn_aggr(mv[:, j, :], st[:, j, :])
                last.then_inc(s_mv, 1)

            def ln1_stats(at):
                dve.wait_ge(s_xin[at.parity], 16 * (at.half + 1))
                stats(xs[at.parity], st1, s_ln1_st)

            def ln1_meanvar(at):
                meanvar(at, st1, s_ln1_st, s_ln1_mv, mv1)

            def split_rest(at, layer):
                dve.wait_ge(s_yhi, 2 * at.b + layer + 1)
                dve.tensor_tensor(y_rest[:], P1[:], yp[0][:].rearrange("p j d -> p (j d)"), ALU.subtract)\
                    .then_inc(s_yrest, 1)

            def split_lo(at, layer):
                dve.wait_ge(s_ymid, 2 * at.b + layer + 1)
                dve.tensor_tensor(yp[2][:].rearrange("p j d -> p (j d)"), y_rest[:],
                                  yp[1][:].rearrange("p j d -> p (j d)"), ALU.subtract).then_inc(s_ylo, 1)

            def degree(at):
                dve.wait_ge(s_p2, 4 * at.b + 1)
                dve.tensor_scalar(deg[:], P2[:, 0:TILES], 1.0, None, ALU.max).then_inc(s_deg, 1)
                dve.wait_ge(s_deg, 2 * at.b + 1)
                dve.reciprocal(deg_inv[:], deg[:]).then_inc(s_deg, 1)

            def mix(at, layer):
                dve.wait_ge(s_p1, 6 * at.b + (3, 5)[layer])
                dve.wait_ge(s_rdeg, at.b + 1)
                dve.tensor_tensor(u[:], P1[:], rdeg[:], ALU.mult).then_inc(s_u, 1)

            def add_root(at, layer):
                dve.wait_ge(s_u, 2 * at.b + layer + 1)
                dve.wait_ge(s_p2, 4 * at.b + layer + 3)
                wait(dve, s_eluact, 6 * at.b + 3 * layer)
                dve.tensor_tensor(v[:], u[:], P2[:], ALU.add).then_inc(s_v, 1)

            def elu(at, layer):
                dve.wait_ge(s_eluact, 6 * at.b + 3 * layer + 3)
                dve.tensor_tensor(hT[layer][:], rv[:], em[:], ALU.subtract).then_inc(s_h, 1)

            def residual(at):
                dve.wait_ge(s_p1, 6 * at.b + 6)
                wait(dve, s_x2d, 16 * (at.b - 1))
                wait(dve, s_keep, at.b - 1)
                dve.tensor_tensor(x2[at.parity][:].rearrange("p j d -> p (j d)"), P1[:],
                                  xs[at.parity][:].rearrange("p j d -> p (j d)"), ALU.add).then_inc(s_x2, 1)

            def ln2_stats(at):
                dve.wait_ge(s_x2, at.b + 1)
                stats(x2[at.parity], st2, s_ln2_st)

            def ln2_meanvar(at):
                meanvar(at, st2, s_ln2_st, s_ln2_mv, mv2)

            def find_top(at, j, step):
                tile = at.b * TILES + j
                if step == 0:
                    if j == 0:
                        dve.wait_ge(s_z, at.b + 1)
                    wait_apart(dve, s_hot, 2 * (tile - 3), s_wload)
                    dve.max(top[j][:, 0:8], z[:, j, :]).then_inc(s_top, 1)
                if step == 1:
                    wait_apart(dve, s_top, 5 * tile + 1, s_wload)
                    dve.match_replace(z_left[:], top[j][:, 0:8], z[:, j, :], LOWEST).then_inc(s_top, 1)
                    dve.max_index(top_at[j][:, 0:8], top[j][:, 0:8], z[:, j, :]).then_inc(s_top, 1)
                if step == 2:
                    wait_apart(dve, s_top, 5 * tile + 2, s_wload)
                    dve.max(top[j][:, 8:16], z_left[:]).then_inc(s_top, 1)
                if step == 3:
                    wait_apart(dve, s_top, 5 * tile + 4, s_wload)
                    dve.max_index(top_at[j][:, 8:16], top[j][:, 8:16], z_left[:]).then_inc(s_top, 1)

            def round_(at, i):
                j, k = divmod(i, TOP)
                to = acc[j % 2][k % 2]
                dve.wait_ge(s_gath, at.b * ROUNDS + i + 1)
                if k < 2:
                    if k == 0:
                        wait(dve, s_T, at.b * T_EVENTS + (-1, 0, 1, 2)[j])
                    dve.tensor_scalar(to[:], G[i % 3][:], top[j][:, k:k + 1], None, ALU.add).then_inc(s_round, 1)
                else:
                    dve.wait_ge(s_round, at.b * ROUNDS + i - 1)
                    dve.scalar_tensor_tensor(out=to[:], in0=G[i % 3][:], scalar=top[j][:, k:k + 1],
                                             in1=to[:], op0=ALU.add, op1=ALU.max).then_inc(s_round, 1)

            def merge(at, j):
                even, odd = acc[j % 2]
                dve.wait_ge(s_round, at.b * ROUNDS + (j + 1) * TOP)
                dve.tensor_tensor(even[:], even[:], odd[:], ALU.max).then_inc(s_merged, 1)

            def count_open(at, j):
                dve.wait_ge(s_merged, at.b * TILES + j + 1)
                wait(dve, s_flags, 4 * at.b)
                dve.scalar_tensor_tensor(out=beyond[:], in0=wmax_all[:], scalar=top[j][:, FOUND - 1:FOUND],
                                         in1=acc[j % 2][0][:], op0=ALU.add, op1=ALU.is_gt,
                                         accum_out=open_n[:, j:j + 1]).then_inc(s_open, 1)

            def pwl(at, c, m):
                base = ALL_STEPS * at.b + sum(STEPS[:c])
                to = (cvx, ccv)[m % 2][c % 2]
                lines_due = 2 * m + 2 if m < 2 else m + 3
                first_line = 4 if c == 1 else 0
                dve.wait_ge(s_line, ALL_DRAWN * at.b + sum(DRAWN[:c]) + lines_due)
                if m < 2:
                    wait(dve, s_fused, 4 * at.b + c - 1)
                    dve.tensor_tensor(to[:], line[first_line + 2 * m][:], line[first_line + 2 * m + 1][:], ALU.max)\
                        .then_inc(s_pwl, 1)
                else:
                    dve.wait_ge(s_pwl, base + m - 1)
                    dve.tensor_tensor(to[:], to[:], line[m + 2][:], ALU.max).then_inc(s_pwl, 1)

            def output(at):
                dve.wait_ge(s_F, 9 * at.b + 9)
                dve.wait_ge(s_keep, at.b + 1)
                wait(dve, s_outd, 16 * at.b)
                dve.tensor_tensor(o_s[:].rearrange("p j d -> p (j d)"), FB[:],
                                  x2_before[:].rearrange("p j d -> p (j d)"), ALU.add).then_inc(s_out, 1)

            def tick(at, finish, gnn, ahead):
                before, after, second = at.plus(-1), at.plus(1), at.plus(2)
                for i in range(ROUNDS):
                    round_(at, i)
                    j, k = divmod(i, TOP)
                    if k == 0 and j > 0:
                        merge(at, j - 1)
                    if k == 1 and j > 0:
                        count_open(at, j - 1)
                    if finish and i == 0:
                        merge(before, TILES - 1)
                    if finish and i == 1:
                        count_open(before, TILES - 1)
                    for start in DVE_TOPS:
                        if start <= i < start + 4:
                            find_top(at, DVE_TOPS[start], i - start)
                    if gnn and i == DVE_MIX1:
                        mix(after, 0)
                    if gnn and i == DVE_MIX1 + 1:
                        add_root(after, 0)
                    if gnn and i == DVE_ELU1:
                        elu(after, 0)
                    if gnn and i == DVE_REST2:
                        split_rest(after, 1)
                    if gnn and i == DVE_LO2:
                        split_lo(after, 1)
                    if gnn and i == DVE_MIX2:
                        mix(after, 1)
                    if gnn and i == DVE_MIX2 + 1:
                        add_root(after, 1)
                    if gnn and i == DVE_ELU2:
                        elu(after, 1)
                    if gnn and i == DVE_RESIDUAL:
                        residual(after)
                    if gnn and i == DVE_RESIDUAL + 1:
                        ln2_stats(after)
                    if gnn and i == DVE_RESIDUAL + 2:
                        ln2_meanvar(after)
                    for start in DVE_TOPS_AFTER:
                        if gnn and start <= i < start + 4:
                            find_top(after, DVE_TOPS_AFTER[start], i - start)
                    if ahead and i == DVE_LN1_STATS:
                        ln1_stats(second)
                    if ahead and i == DVE_LN1_STATS + 1:
                        ln1_meanvar(second)
                    if ahead and i == DVE_REST1:
                        split_rest(second, 0)
                    if ahead and i == DVE_DEGREE:
                        degree(second)
                    if ahead and i == DVE_LO1:
                        split_lo(second, 0)
                    if finish and i == DVE_OUTPUT:
                        output(before)
                    if finish:
                        for c in range(CHUNKS):
                            if i in DVE_PWL[c]:
                                pwl(before, c, DVE_PWL[c].index(i))

            dve.wait_ge(s_wload, LOADED)
            first, next_ = fixed(0), fixed(1)
            ln1_stats(first)
            ln1_meanvar(first)
            chain(dve.reduce_max(wmax[:], wt_f[:], AX_X))
            chain(dve.tensor_reduce(wmin[:], wt_f[:], AX_X, ALU.min))
            rest = wt_r[:].rearrange("p (c d) -> p c d", c=CHUNKS)
            chain(dve.tensor_copy(wt_fp[0][:], wt_f[:]))
            chain(dve.tensor_tensor(rest, wt_f[:], wt_fp[0][:], ALU.subtract))
            chain(dve.tensor_copy(wt_fp[1][:], rest))
            dve.tensor_tensor(wt_fp[2][:], rest, wt_fp[1][:], ALU.subtract).then_inc(s_wtf, 1)
            dve.wait_ge(s_share, 1)
            chain(dve.tensor_scalar(share[:, 0:CHUNKS], share[:, 0:CHUNKS], 0.5, 0.5, ALU.mult, ALU.add))
            chain(dve.tensor_scalar(share[:, CHUNKS:FC], share[:, 0:CHUNKS], 1.0, None, ALU.subtract))
            chain(dve.tensor_tensor(slope[:], slope[:], share[:][:, :, None].to_broadcast([P, FC, LINES]), ALU.mult))
            chain(dve.tensor_tensor(offs[:], offs[:], share[:][:, :, None].to_broadcast([P, FC, LINES]), ALU.mult))
            split_rest(first, 0)
            chain(dve.tensor_tensor(lo_hi[:, 0, :], wmin[:], bt_s[:], ALU.add))
            chain(dve.tensor_tensor(lo_hi[:, 1, :], wmax[:], bt_s[:], ALU.add))
            chain(dve.tensor_scalar(lo_hi[:, 0, :], lo_hi[:, 0, :], Z_LO, None, ALU.add))
            chain(dve.tensor_scalar(lo_hi[:, 1, :], lo_hi[:, 1, :], Z_HI, None, ALU.add))
            for e, end in ((0, end_a), (1, end_b)):
                for f in range(2):
                    part = slice(f * CHUNKS, (f + 1) * CHUNKS)
                    at_end = lo_hi[:, e, :][:, :, None].to_broadcast([P, CHUNKS, LINES])
                    chain(dve.tensor_tensor(end[:, part, :], slope[:, part, :], at_end, ALU.mult))
                chain(dve.tensor_tensor(end[:], end[:], offs[:], ALU.add))
            split_lo(first, 0)
            degree(first)
            da, db, cross, low, one = [w[:].rearrange("p (f a b) -> p f a b", a=LINES, b=LINES) for w in work]
            for d, end in ((da, end_a), (db, end_b)):
                chain(dve.tensor_tensor(d, end[:][:, :, :, None].to_broadcast([P, FC, LINES, LINES]),
                                        end[:][:, :, None, :].to_broadcast([P, FC, LINES, LINES]), ALU.subtract))
            chain(dve.tensor_tensor(low, da, db, ALU.subtract))
            chain(dve.tensor_scalar(one, low, 0.0, None, ALU.is_equal))
            chain(dve.tensor_tensor(low, low, one, ALU.add))
            chain(dve.reciprocal(cross, low))
            chain(dve.tensor_tensor(cross, cross, da, ALU.mult))
            chain(dve.tensor_scalar(low, db, 0.0, 2.0, ALU.is_le, ALU.mult))
            chain(dve.tensor_tensor(low, low, cross, ALU.max))
            chain(dve.tensor_scalar(one, da, 0.0, None, ALU.is_lt))
            chain(dve.tensor_tensor(low, low, one, ALU.mult))
            chain(dve.reduce_max(need[:], low, AX_X))
            chain(dve.tensor_scalar(low, cross, -1.0, 1.0, ALU.mult, ALU.add))
            chain(dve.tensor_scalar(one, db, 0.0, None, ALU.is_lt))
            chain(dve.tensor_tensor(low, low, one, ALU.mult))
            chain(dve.tensor_scalar(one, da, 0.0, None, ALU.is_ge))
            chain(dve.tensor_tensor(low, low, one, ALU.mult))
            chain(dve.reduce_max(picked[:], low, AX_X))
            chain(dve.tensor_tensor(need[:], need[:], picked[:], ALU.add))
            chain(dve.tensor_scalar(need[:], need[:], 1.0 + MARGIN, None, ALU.is_le))
            chain(dve.memset(rank[:, :, 0:1], 0.0))
            for k in range(1, LINES):
                chain(dve.tensor_tensor(rank[:, :, k], rank[:, :, k - 1], need[:, :, k - 1], ALU.add))
            chain(dve.tensor_tensor(count[:], rank[:, :, LINES - 1], need[:, :, LINES - 1], ALU.add))
            chain(dve.tensor_tensor(key[:], count[:, 0:CHUNKS], count[:, CHUNKS:FC], ALU.max))
            chain(dve.tensor_tensor(key_sum[:], count[:, 0:CHUNKS], count[:, CHUNKS:FC], ALU.add))
            chain(dve.tensor_scalar(key[:], key[:], float(4 * LINES), None, ALU.mult))
            chain(dve.tensor_tensor(key[:], key[:], key_sum[:], ALU.add))
            chain(dve.tensor_scalar(key[:], key[:], float(FFN), None, ALU.mult))
            chain(dve.tensor_tensor(key[:], key[:], tok[:, 0:CHUNKS], ALU.add))
            dve.tensor_scalar(key_half[:], key[:], 0.5, None, ALU.subtract).then_inc(s_key, 1)
            mix(first, 0)
            add_root(first, 0)
            dve.wait_ge(s_keyr, 1)
            dve.wait_ge(s_key, 1)
            for c in range(CHUNKS):
                if c == 2:
                    elu(first, 0)
                chain(dve.tensor_scalar(wt_r[:], G[0][:], key_half[:, c:c + 1], None, ALU.is_lt))
                chain(dve.reduce_sum(place[:, c:c + 1], wt_r[:], AX_X))
            chain(dve.tensor_copy(wt_r[:], place_i[:]))
            for c in range(CHUNKS):
                chain(dve.tensor_scalar(perm[c][:], wt_r[:], place[:, c:c + 1], None, ALU.is_equal))
                last = dve.tensor_copy(permb[:, c, :], perm[c][:])
            last.then_inc(s_perm, 1)
            for f in range(2):
                part = slice(f * CHUNKS, (f + 1) * CHUNKS)
                chain(dve.tensor_tensor(picked[:, part, :], slope[:, part, :],
                                        bt_s[:][:, :, None].to_broadcast([P, CHUNKS, LINES]), ALU.mult))
            chain(dve.tensor_tensor(offs[:], offs[:], picked[:], ALU.add))
            for m in range(SLOTS):
                if m == 0:
                    split_rest(first, 1)
                if m == 1:
                    split_lo(first, 1)
                if m == 3:
                    mix(first, 1)
                    add_root(first, 1)
                chain(dve.tensor_scalar(pick[:], rank[:], float(m), None, ALU.is_equal))
                chain(dve.tensor_tensor(pick[:], pick[:], need[:], ALU.mult))
                for of, to in ((slope, slot_sl), (offs, slot_of)):
                    chain(dve.tensor_tensor(picked[:], pick[:], of[:], ALU.mult))
                    chain(dve.reduce_sum(to[:, m, :], picked[:], AX_X))
                    if m:
                        chain(dve.tensor_scalar(empty[:], count[:], float(m), None, ALU.is_le))
                        chain(dve.tensor_tensor(empty[:], empty[:], to[:, 0, :], ALU.mult))
                        chain(dve.tensor_tensor(to[:, m, :], to[:, m, :], empty[:], ALU.add))
            for f in range(2):
                part = slice(f * CHUNKS, (f + 1) * CHUNKS)
                chain(dve.tensor_copy(table[:, :, V_SL + f * LINES:V_SL + (f + 1) * LINES], slope[:, part, :]))
                chain(dve.tensor_copy(table[:, :, V_OF + f * LINES:V_OF + (f + 1) * LINES], offs[:, part, :]))
                chain(dve.tensor_copy(table[:, :, V_N + f], count[:, part]))
                for m in range(SLOTS):
                    chain(dve.tensor_copy(table[:, :, V_SS + 2 * m + f], slot_sl[:, m, part]))
                    chain(dve.tensor_copy(table[:, :, V_SO + 2 * m + f], slot_of[:, m, part]))
            chain(dve.tensor_copy(table[:, :, V_BC], bc_s[:]))
            dve.tensor_scalar(table[:, :, V_BG], bg_s[:], 0.5, None, ALU.mult).then_inc(s_table, 1)
            elu(first, 1)
            residual(first)
            ln2_stats(first)
            ln2_meanvar(first)
            ln1_stats(next_)
            ln1_meanvar(next_)
            for j in range(2):
                for step in range(4):
                    find_top(first, j, step)
            for m in range(CHUNKS):
                chain(dve.memset(planned[:, m, :], float(PLAN[m])))
            dve.wait_ge(s_putc, 8)
            chain(dve.tensor_tensor(over[:], feat[:, :, V_N:V_N + 2], planned[:], ALU.is_gt))
            chain(dve.reduce_max(over1[:], over[:].rearrange("p c f -> p (c f)"), AX_X))
            dve.tensor_copy(over1b[:], over1[:]).then_inc(s_setup_done, 1)

            degree(next_)
            split_rest(next_, 0)
            split_lo(next_, 0)
            tick(first, False, True, True)
            tick(fixed(1), True, True, True)
            with dve.Fori(0, 5) as i:
                tick(At(i * 2 + 2, 0, i + 1), True, True, True)
                tick(At(i * 2 + 3, 1, i + 1), True, True, True)
            tick(fixed(12), True, True, True)
            tick(fixed(13), True, True, True)
            tick(fixed(14), True, True, False)
            tick(fixed(15), True, False, False)
            merge(fixed(15), TILES - 1)
            count_open(fixed(15), TILES - 1)
            gsteps = [0]

            def gchain(instruction):
                gsteps[0] += 1
                instruction.then_inc(q_dve, 1)
                dve.wait_ge(q_dve, gsteps[0])

            dve.wait_ge(s_flags, 4 * BATCHES)
            gchain(dve.tensor_scalar(ff[:], flags[:], 0.5, None, ALU.is_gt))
            dve.tensor_copy(fb[:], ff[:]).then_inc(q_fb, 1)
            dve.wait_ge(q_rank, 1)
            gchain(dve.tensor_copy(total[:], P2[:, NCOLS:2 * NCOLS]))
            gchain(dve.tensor_copy(tot[0][:], P2[:, NCOLS:2 * NCOLS]))
            n, q = 1, 0
            while n < NCOLS:
                gchain(dve.tensor_copy(tot[1 - q][:, 0:n], tot[q][:, 0:n]))
                gchain(dve.tensor_tensor(tot[1 - q][:, n:NCOLS], tot[q][:, n:NCOLS], tot[q][:, 0:NCOLS - n], ALU.add))
                n, q = 2 * n, 1 - q
            gchain(dve.tensor_tensor(rk[:], tot[q][:], total[:], ALU.subtract))
            gchain(dve.tensor_tensor(rk[:], rk[:], P2[:, 0:NCOLS], ALU.add))
            gchain(dve.tensor_copy(rk_i[:], rk[:]))
            gchain(dve.tensor_scalar(rk_c_i[:], rk_i[:], 7, None, ALU.logical_shift_right))
            gchain(dve.tensor_scalar(rk_s_i[:], rk_i[:], P - 1, None, ALU.bitwise_and))
            gchain(dve.tensor_copy(rk_c[:], rk_c_i[:]))
            gchain(dve.tensor_copy(rk_s[:], rk_s_i[:]))
            gchain(dve.tensor_tensor(tok[:], tok[:], ff[:], ALU.mult))
            gchain(dve.tensor_scalar(n_tiles_f[:], tot[q][:, NCOLS - 1:NCOLS], float(P - 1), float(P), ALU.add, ALU.max))
            gchain(dve.tensor_copy(n_tiles_i[:], n_tiles_f[:]))
            dve.tensor_scalar(n_tiles_m[:], n_tiles_i[:], 7, None, ALU.logical_shift_right).then_inc(q_n, 1)
            for i in range(NCOLS // RING):
                for p in range(RING):
                    col = i * RING + p
                    dve.wait_ge(q_hotu, col + 1)
                    dve.tensor_scalar(at_slot[:, p, :], iota[:], rk_s[:, col:col + 1], None, ALU.is_equal)
                    dve.tensor_scalar(at_tile[p], iota[:, 0:NCOLS], rk_c[:, col:col + 1], tok[:, col:col + 1],
                                      ALU.is_equal, ALU.mult).then_inc(q_hot, 1)
                for c in ((0,), (1, 2), (3,), ())[i]:
                    for m in range(STEPS[c]):
                        pwl(fixed(15), c, m)
            dve.wait_ge(q_list, 1)
            gchain(dve.tensor_copy(got[:], P1[:, 0:NCOLS]))
            gchain(dve.tensor_scalar(hole[:], got[:], 0.5, float(4 * BATCHES * NODES), ALU.is_lt, ALU.mult))
            gchain(dve.tensor_scalar(src[:], got[:], -1.0, 0.0, ALU.add, ALU.max))
            dve.tensor_tensor(dst[:], src[:], hole[:], ALU.add).then_inc(q_n, 1)
            output(fixed(15))
            dve.wait_ge(q_n, 2)
            tiles = dve.value_load(n_tiles_m[0:1, 0:1], min_val=1, max_val=NCOLS)

            def search_deep(g, s):
                def find(q):
                    rows = (g_z, g_left[0], g_left[1], g_left[0])[q]
                    base = g * (3 * GROUPS - 1) + 3 * q
                    part = slice(8 * q, 8 * q + 8)
                    if q:
                        wait_apart(dve, s.top, base, s_wload)
                    dve.max(g_top[:, part], rows[:]).then_inc(s.top, 1)
                    wait_apart(dve, s.top, base + 1, s_wload)
                    dve.max_index(g_at[:, part], g_top[:, part], rows[:]).then_inc(s.top, 1)
                    if q < GROUPS - 1:
                        dve.match_replace(g_left[q % 2][:], g_top[:, part], rows[:], LOWEST).then_inc(s.top, 1)

                def one_hots(q):
                    dve.wait_ge(s.top, g * (3 * GROUPS - 1) + 3 * q + 2)
                    for k in range(8):
                        last = dve.tensor_scalar(hot[:, 8 * (q % 2) + k, :], iota[:], g_at[:, 8 * q + k:8 * q + k + 1],
                                                 None, ALU.is_equal)
                    last.then_inc(s.hot, 1)

                def rounds(q):
                    for k in range(8):
                        n = 8 * q + k
                        to = g_acc[n % 2]
                        dve.wait_ge(s.gath, g * DEEP + n + 1)
                        if n < 2:
                            dve.tensor_scalar(to[:], G[n % 3][:], g_top[:, n:n + 1], None, ALU.add)\
                                .then_inc(s.round, 1)
                        else:
                            dve.wait_ge(s.round, g * DEEP + n - 1)
                            dve.scalar_tensor_tensor(out=to[:], in0=G[n % 3][:], scalar=g_top[:, n:n + 1],
                                                     in1=to[:], op0=ALU.add, op1=ALU.max).then_inc(s.round, 1)

                for q in range(GROUPS):
                    find(q)
                    if q < 2:
                        one_hots(q)
                for q in range(GROUPS):
                    rounds(q)
                dve.wait_ge(s.round, g * DEEP + DEEP)
                dve.tensor_tensor(g_acc[0][:], g_acc[0][:], g_acc[1][:], ALU.max).then_inc(s.merged, 1)
                dve.wait_ge(s.merged, g + 1)
                dve.scalar_tensor_tensor(out=beyond[:], in0=wmax_all[:], scalar=g_top[:, DEEP - 1:DEEP],
                                         in1=g_acc[0][:], op0=ALU.add, op1=ALU.is_gt,
                                         accum_out=g_open[:]).then_inc(s.open, 1)
                dve.wait_ge(s.open, g * 2 + 1)
                dve.tensor_tensor(g_any[:], g_any[:], g_open[:], ALU.max).then_inc(s.open, 1)

            def search_full(g, s):
                dve.memset(g_acc[0][:], LOWEST).then_inc(s.round, 2)
                with dve.Fori(0, D // 8) as h:
                    for k in range(8):
                        dve.wait_ge(s.gath, g * D + h * 8 + k + 1)
                        dve.wait_ge(s.round, g * (D + 2) + h * 8 + k + 2)
                        dve.scalar_tensor_tensor(out=g_acc[0][:], in0=G[k % 2][:], scalar=g_z[:, bass.ds(h * 8 + k, 1)],
                                                 in1=g_acc[0][:], op0=ALU.add, op1=ALU.max).then_inc(s.round, 1)

            def general(g, s, search):
                dve.wait_ge(s.free, g + 1)
                dve.tensor_copy(src_i[:], src[:, bass.ds(g, 1)]).then_inc(s.idx, 1)
                dve.tensor_copy(dst_i[:], dst[:, bass.ds(g, 1)]).then_inc(s.idx, 1)
                dve.wait_ge(s.rows, g * 16 + 16)
                dve.bn_stats(g_st[:], g_x[:]).then_inc(s.st, 1)
                wait_apart(dve, s.st, g + 1, s_wload)
                dve.bn_aggr(g_mv[:], g_st[:]).then_inc(s.mv, 1)
                dve.wait_ge(s.mv, g + 1)
                wait_apart(dve, s.rs, g * 2 + 2, s_wload)
                dve.tensor_scalar(g_z[:], g_x[:], g_mv[:, 0:1], g_rs[:], ALU.subtract, ALU.mult).then_inc(s.z, 1)
                wait_apart(dve, s.z, g + 1, s_wload)
                search(g, s)
                dve.wait_ge(s.Fa, g * 2 + 2)
                dve.tensor_scalar(g_gt, g_gt, 0.5, 0.5, ALU.mult, ALU.add).then_inc(s.mix, 1)

                def draw(m):
                    to = g_concave[m % 2] if m else g_pw[1]
                    if m > 2:
                        dve.wait_ge(s.pwl, g * s.pwl_steps + 2 * (m - 2))
                    k, o = (V_SS + 2 * m + 1, V_SO + 2 * m + 1) if s is deep else (V_SL + LINES + m, V_OF + LINES + m)
                    for c in range(CHUNKS):
                        last = dve.tensor_scalar(to[:, c, :], g_tT[:, c, :], feat[:, c, k:k + 1], feat[:, c, o:o + 1],
                                                 ALU.mult, ALU.add)
                    last.then_inc(s.drawn, 1)

                dve.wait_ge(s.tT, g + 1)
                draw(0)
                draw(1)
                for m in range(1, s.drawn_lines):
                    if m < s.drawn_lines - 1:
                        draw(m + 1)
                    for f, lines_of, drawn, per in ((0, g_convex[m % 4], s.line, s.lines),
                                                    (1, g_concave[m % 2], s.drawn, s.drawn_lines)):
                        dve.wait_ge(drawn, g * per + m + 1)
                        if m > 1:
                            dve.wait_ge(s.pwl, g * s.pwl_steps + 2 * (m - 2) + f + 1)
                        dve.tensor_tensor(g_pw[f], g_pw[f], lines_of, ALU.max).then_inc(s.pwl, 1)
                if s is deep:
                    dve.wait_ge(s.line, g * s.lines + 3)
                    for e, (c, m, f) in enumerate(EXTRA):
                        dve.wait_ge(s.pwl, g * s.pwl_steps + e + 1)
                        dve.tensor_tensor(g_pw[f][:, c, :], g_pw[f][:, c, :],
                                          g_convex[2 + e // CHUNKS][:, e % CHUNKS, :], ALU.max).then_inc(s.pwl, 1)
                dve.wait_ge(s.pwl, g * s.pwl_steps + s.pwl_steps)
                dve.tensor_tensor(g_pw[0], g_pw[0], g_pw[1], ALU.subtract).then_inc(s.mix, 1)
                dve.wait_ge(s.mix, g * 4 + 2)
                dve.tensor_tensor(g_pw[0], g_pw[0], g_cl, ALU.subtract).then_inc(s.mix, 1)
                dve.wait_ge(s.mix, g * 4 + 3)
                dve.tensor_tensor(g_pw[0], g_pw[0], g_gt, ALU.mult).then_inc(s.mix, 1)
                dve.wait_ge(s.mix, g * 4 + 4)
                dve.tensor_tensor(g_fu, g_pw[0], g_cl, ALU.add).then_inc(s.fused, 1)
                dve.wait_ge(s.o, g + 1)
                dve.tensor_tensor(g_o[:], FB[:, 0:D], g_x[:], ALU.add).then_inc(s.os, 1)

            gchain(dve.reduce_max(g_any[:], outside[:], AX_X))
            with dve.Fori(0, tiles) as g:
                general(g, deep, search_deep)
            gchain(dve.tensor_scalar(g_any_f[:], g_any[:], OPEN_FROM, None, ALU.is_gt))
            dve.tensor_copy(g_anyb[:], g_any_f[:]).then_inc(q_anyb, 1)
            dve.wait_ge(q_anyc, 1)
            gchain(dve.tensor_scalar(g_any_f[:], T[:, 0:1], 0.5, None, ALU.is_gt))
            dve.tensor_copy(g_any_i[:], g_any_f[:]).then_inc(q_any, 1)
            dve.wait_ge(q_any, 1)
            some = dve.value_load(g_any_i[0:1, 0:1], min_val=0, max_val=1)
            with dve.If(some > 0):
                with dve.Fori(0, tiles) as g:
                    general(g, full, search_full)


_INS = ["x", "adj", "L0_gnn_w_rel1", "L0_gnn_w_root1", "L0_gnn_b1", "L0_gnn_w_rel2", "L0_gnn_w_root2", "L0_gnn_b2",
        "L0_ffn_Wt", "L0_ffn_bt", "L0_ffn_sl_cvx", "L0_ffn_of_cvx", "L0_ffn_sl_ccv", "L0_ffn_of_ccv",
        "L0_ffn_alpha", "L0_ffn_Wc", "L0_ffn_bc", "L0_ffn_Wg", "L0_ffn_bg", "L0_ffn_Wd", "L0_ffn_bd"]
_OUTS = [((BATCHES, NODES, D), "float32")]


def kernel(**inputs):
    import numpy as _np
    import concourse.bacc as _bacc
    from concourse import mybir as _mybir
    from concourse.bass_utils import run_bass_kernel_spmd as _run

    nc = _bacc.Bacc("TRN2", target_bir_lowering=False, num_devices=1)
    arrays, args = {}, []
    for name in _INS:
        a = _np.ascontiguousarray(inputs[name])
        arrays[f"in_{name}_dram"] = a
        args.append(nc.dram_tensor(f"in_{name}_dram", a.shape, _mybir.dt.from_np(a.dtype), kind="ExternalInput").ap())
    for i, (shape, dtype) in enumerate(_OUTS):
        dt = _mybir.dt.from_np(_np.dtype(dtype))
        args.append(nc.dram_tensor(f"out_{i}_dram", shape, dt, kind="ExternalOutput").ap())
    build(nc, *args)
    r = _run(nc, [arrays], core_ids=[0])
    got = tuple(r.results[0][f"out_{i}_dram"] for i in range(len(_OUTS)))
    return got[0]
```
